# Optimizing a Trainium2 kernel written in Bass

```python
import numpy as np
import jax
import jax.numpy as jnp

def _softmax(x, axis=-1):
    return jax.nn.softmax(x, axis=axis)

def _gelu(x):
    return jax.nn.gelu(x, approximate=True)

def _silu(x):
    return jax.nn.silu(x)

def _sigmoid(x):
    return jax.nn.sigmoid(x)

def _layernorm(x, axis=-1, eps=1e-05):
    m = jnp.mean(x, axis=axis, keepdims=True)
    v = jnp.var(x, axis=axis, keepdims=True)
    return (x - m) / jnp.sqrt(v + eps)

def _scatter_add(tgt, idx, src, axis=0):
    return tgt.at[idx].add(src)

def _segment_sum(src, seg, n):
    return jax.ops.segment_sum(src, seg, n)
kernel_name = 'mk_gnn_ffn_d2_gnn_r8_885b67'

def setup_inputs(seed: int=0):
    np.random.seed(seed)
    _w = jnp.asarray

    def _rec_inputs():
        import jax
        import jax.numpy as jnp
        _gk = jax.random.key(seed)
        x = -0.0002117 + 1 * jax.random.normal(jax.random.fold_in(_gk, 1), (6250, 256), jnp.float32)
        src = jax.random.randint(jax.random.fold_in(_gk, 2), (200000,), 0, 6250, jnp.int32)
        dst = jnp.minimum((6250 * jax.random.uniform(jax.random.fold_in(_gk, 3), (200000,)) ** 2.0).astype(jnp.int32), 49999)
        _o = jnp.argsort(dst, stable=True)
        src = src[_o]
        dst = dst[_o]
        return (x, src, dst)
    x, src, dst = _rec_inputs()

    def _L0_gnn_setup():
        import jax, jax.numpy as jnp
        import numpy as np
        N_NODES = 12500
        N_EDGES = 200000
        D_IN = 256
        D_OUT = 256
        key = jax.random.key(seed)
        k1, k2, k3, k4 = jax.random.split(key, 4)
        node_embed = jax.random.normal(k1, (N_NODES, D_IN), dtype=jnp.float32)
        edges = jax.random.randint(k2, (N_EDGES, 2), 0, N_NODES, dtype=jnp.int64)
        W = jax.random.normal(k3, (D_OUT, D_IN), dtype=jnp.float32) * (1.0 / np.sqrt(D_IN))
        b = jax.random.normal(k4, (D_OUT,), dtype=jnp.float32) * 0.01
        return {'node_embed': node_embed, 'edges': edges, 'W': W, 'b': b}
    _L0_gnn_all = _L0_gnn_setup()
    _L0_gnn_in = {k: v for k, v in _L0_gnn_all.items() if k in ('W', 'b')}
    del _L0_gnn_all

    def _L0_ffn_setup():
        import jax, jax.numpy as jnp
        import numpy as np
        DIM = 256
        H = 8
        D = 64
        G = 64
        INNER = H * D
        SCALE = D ** (-0.5)
        key = jax.random.key(seed)
        ks = jax.random.split(key, 12)
        B, N = (4, 2048)
        x = jax.random.normal(ks[0], (B, N, DIM), dtype=jnp.float32)
        s = lambda fan_in: 1.0 / np.sqrt(fan_in)
        W_fx = jax.random.normal(ks[1], (DIM, INNER), dtype=jnp.float32) * s(DIM)
        b_fx = jnp.zeros((INNER,), dtype=jnp.float32)
        W_x = jax.random.normal(ks[2], (DIM, INNER), dtype=jnp.float32) * s(DIM)
        b_x = jnp.zeros((INNER,), dtype=jnp.float32)
        A = jax.random.normal(ks[3], (G, D), dtype=jnp.float32)
        Q, _ = jnp.linalg.qr(A.T)
        W_slice = Q[:, :G].astype(jnp.float32)
        b_slice = jnp.zeros((G,), dtype=jnp.float32)
        W_q = jax.random.normal(ks[4], (D, D), dtype=jnp.float32) * s(D)
        W_k = jax.random.normal(ks[5], (D, D), dtype=jnp.float32) * s(D)
        W_v = jax.random.normal(ks[6], (D, D), dtype=jnp.float32) * s(D)
        W_out = jax.random.normal(ks[7], (INNER, DIM), dtype=jnp.float32) * s(INNER)
        b_out = jnp.zeros((DIM,), dtype=jnp.float32)
        temperature = jnp.ones((1, H, 1, 1), dtype=jnp.float32) * 0.5
        return {'x': x, 'W_fx': W_fx, 'b_fx': b_fx, 'W_x': W_x, 'b_x': b_x, 'W_slice': W_slice, 'b_slice': b_slice, 'W_q': W_q, 'W_k': W_k, 'W_v': W_v, 'W_out': W_out, 'b_out': b_out, 'temperature': temperature}
    _L0_ffn_all = _L0_ffn_setup()
    _L0_ffn_in = {k: v for k, v in _L0_ffn_all.items() if k in ('W_fx', 'b_fx', 'W_x', 'b_x', 'W_slice', 'b_slice', 'W_q', 'W_k', 'W_v', 'W_out', 'b_out', 'temperature')}
    del _L0_ffn_all

    def _L1_gnn_setup():
        import jax, jax.numpy as jnp
        import numpy as np
        N = 12500
        E = 200000
        D_IN = 256
        HID = 256
        OUT = 256

        def _mean_agg(x, src, dst, n):
            s = jax.ops.segment_sum(x[src], dst, num_segments=n)
            deg = jax.ops.segment_sum(jnp.ones((src.shape[0],), x.dtype), dst, num_segments=n)
            return s / jnp.maximum(deg, 1.0)[:, None]
        key = jax.random.key(seed)
        ks = jax.random.split(key, 12)
        x = jax.random.normal(ks[0], (N, D_IN), dtype=jnp.float32)
        edge_index = jax.random.randint(ks[1], (2, E), 0, N, dtype=jnp.int64)
        s = 0.05
        return {'x': x, 'edge_index': edge_index, 'Wl1': jax.random.normal(ks[2], (D_IN, HID), jnp.float32) * s, 'Wr1': jax.random.normal(ks[3], (D_IN, HID), jnp.float32) * s, 'b1': jnp.zeros((HID,), jnp.float32), 'Wlin1': jax.random.normal(ks[4], (D_IN, HID), jnp.float32) * s, 'blin1': jnp.zeros((HID,), jnp.float32), 'Wl2': jax.random.normal(ks[5], (HID, OUT), jnp.float32) * s, 'Wr2': jax.random.normal(ks[6], (HID, OUT), jnp.float32) * s, 'b2': jnp.zeros((OUT,), jnp.float32), 'Wlin2': jax.random.normal(ks[7], (HID, OUT), jnp.float32) * s, 'blin2': jnp.zeros((OUT,), jnp.float32)}
    _L1_gnn_all = _L1_gnn_setup()
    _L1_gnn_in = {k: v for k, v in _L1_gnn_all.items() if k in ('Wl1', 'Wr1', 'b1', 'Wlin1', 'blin1', 'Wl2', 'Wr2', 'b2', 'Wlin2', 'blin2')}
    del _L1_gnn_all

    def _L1_ffn_setup():
        import math
        import jax, jax.numpy as jnp
        import numpy as np
        CAPACITY_FACTOR = 1.25
        key = jax.random.key(seed)
        ks = jax.random.split(key, 5)
        B, L, D, F, E = (8, 1024, 256, 1024, 8)
        h = jax.random.normal(ks[0], (B, L, D), dtype=jnp.float32)
        gate_w = jax.random.normal(ks[1], (D, E), dtype=jnp.float32) * 0.02
        gate_b = jnp.zeros((E,), dtype=jnp.float32)
        w1 = jax.random.normal(ks[2], (E, D, F), dtype=jnp.float32) * (1.0 / math.sqrt(D))
        b1 = jnp.zeros((E, F), dtype=jnp.float32)
        w2 = jax.random.normal(ks[3], (E, F, D), dtype=jnp.float32) * (1.0 / math.sqrt(F))
        b2 = jnp.zeros((E, D), dtype=jnp.float32)
        return {'h': h, 'gate_w': gate_w, 'gate_b': gate_b, 'w1': w1, 'b1': b1, 'w2': w2, 'b2': b2}
    _L1_ffn_all = _L1_ffn_setup()
    _L1_ffn_in = {k: v for k, v in _L1_ffn_all.items() if k in ('gate_w', 'gate_b', 'w1', 'b1', 'w2', 'b2')}
    del _L1_ffn_all
    return {'x': x, 'src': src, 'dst': dst, 'L0_gnn_W': _L0_gnn_in['W'], 'L0_gnn_b': _L0_gnn_in['b'], 'L0_ffn_W_fx': _L0_ffn_in['W_fx'], 'L0_ffn_b_fx': _L0_ffn_in['b_fx'], 'L0_ffn_W_x': _L0_ffn_in['W_x'], 'L0_ffn_b_x': _L0_ffn_in['b_x'], 'L0_ffn_W_slice': _L0_ffn_in['W_slice'], 'L0_ffn_b_slice': _L0_ffn_in['b_slice'], 'L0_ffn_W_q': _L0_ffn_in['W_q'], 'L0_ffn_W_k': _L0_ffn_in['W_k'], 'L0_ffn_W_v': _L0_ffn_in['W_v'], 'L0_ffn_W_out': _L0_ffn_in['W_out'], 'L0_ffn_b_out': _L0_ffn_in['b_out'], 'L0_ffn_temperature': _L0_ffn_in['temperature'], 'L1_gnn_Wl1': _L1_gnn_in['Wl1'], 'L1_gnn_Wr1': _L1_gnn_in['Wr1'], 'L1_gnn_b1': _L1_gnn_in['b1'], 'L1_gnn_Wlin1': _L1_gnn_in['Wlin1'], 'L1_gnn_blin1': _L1_gnn_in['blin1'], 'L1_gnn_Wl2': _L1_gnn_in['Wl2'], 'L1_gnn_Wr2': _L1_gnn_in['Wr2'], 'L1_gnn_b2': _L1_gnn_in['b2'], 'L1_gnn_Wlin2': _L1_gnn_in['Wlin2'], 'L1_gnn_blin2': _L1_gnn_in['blin2'], 'L1_ffn_gate_w': _L1_ffn_in['gate_w'], 'L1_ffn_gate_b': _L1_ffn_in['gate_b'], 'L1_ffn_w1': _L1_ffn_in['w1'], 'L1_ffn_b1': _L1_ffn_in['b1'], 'L1_ffn_w2': _L1_ffn_in['w2'], 'L1_ffn_b2': _L1_ffn_in['b2']}

def reference(x, src, dst, L0_gnn_W, L0_gnn_b, L0_ffn_W_fx, L0_ffn_b_fx, L0_ffn_W_x, L0_ffn_b_x, L0_ffn_W_slice, L0_ffn_b_slice, L0_ffn_W_q, L0_ffn_W_k, L0_ffn_W_v, L0_ffn_W_out, L0_ffn_b_out, L0_ffn_temperature, L1_gnn_Wl1, L1_gnn_Wr1, L1_gnn_b1, L1_gnn_Wlin1, L1_gnn_blin1, L1_gnn_Wl2, L1_gnn_Wr2, L1_gnn_b2, L1_gnn_Wlin2, L1_gnn_blin2, L1_ffn_gate_w, L1_ffn_gate_b, L1_ffn_w1, L1_ffn_b1, L1_ffn_w2, L1_ffn_b2):
    import jax
    import jax.numpy as jnp

    def _L0_gnn_ref(node_embed, edges, W, b):
        import jax, jax.numpy as jnp
        import numpy as np
        N_NODES = 12500
        N_EDGES = 200000
        D_IN = 256
        D_OUT = 256
        h = node_embed @ W.T + b
        N = node_embed.shape[0]
        src = edges[:, 0]
        dst = edges[:, 1]
        deg = jax.ops.segment_sum(jnp.ones_like(src, dtype=h.dtype), src, num_segments=N) + 1.0
        dinv = deg ** (-0.5)
        m = h * dinv[:, None]
        agg = jax.ops.segment_sum(m[dst], src, num_segments=N) + m
        return agg * dinv[:, None]

    def _L0_ffn_ref(x, W_fx, b_fx, W_x, b_x, W_slice, b_slice, W_q, W_k, W_v, W_out, b_out, temperature):
        import jax, jax.numpy as jnp
        import numpy as np
        DIM = 256
        H = 8
        D = 64
        G = 64
        INNER = H * D
        SCALE = D ** (-0.5)
        B, N, _ = x.shape
        fx_mid = (x @ W_fx + b_fx).reshape(B, N, H, D).transpose(0, 2, 1, 3)
        x_mid = (x @ W_x + b_x).reshape(B, N, H, D).transpose(0, 2, 1, 3)
        temp = jnp.clip(temperature, 0.1, 5.0)
        slice_weights = jax.nn.softmax((x_mid @ W_slice + b_slice) / temp, axis=-1)
        slice_norm = slice_weights.sum(axis=2)
        slice_token = jnp.einsum('bhnc,bhng->bhgc', fx_mid, slice_weights)
        slice_token = slice_token / (slice_norm[..., None] + 1e-05)
        q = slice_token @ W_q
        k = slice_token @ W_k
        v = slice_token @ W_v
        attn = jax.nn.softmax(jnp.einsum('bhgc,bhkc->bhgk', q, k) * SCALE, axis=-1)
        out_slice = jnp.einsum('bhgk,bhkc->bhgc', attn, v)
        out_x = jnp.einsum('bhgc,bhng->bhnc', out_slice, slice_weights)
        out_x = out_x.transpose(0, 2, 1, 3).reshape(B, N, INNER)
        return out_x @ W_out + b_out

    def _L1_gnn_ref(x, edge_index, Wl1, Wr1, b1, Wlin1, blin1, Wl2, Wr2, b2, Wlin2, blin2):
        import jax, jax.numpy as jnp
        import numpy as np
        N = 12500
        E = 200000
        D_IN = 256
        HID = 256
        OUT = 256

        def _mean_agg(x, src, dst, n):
            s = jax.ops.segment_sum(x[src], dst, num_segments=n)
            deg = jax.ops.segment_sum(jnp.ones((src.shape[0],), x.dtype), dst, num_segments=n)
            return s / jnp.maximum(deg, 1.0)[:, None]
        src, dst = (edge_index[0], edge_index[1])
        agg1 = _mean_agg(x, src, dst, x.shape[0])
        h = agg1 @ Wl1 + x @ Wr1 + b1 + x @ Wlin1 + blin1
        h = jax.nn.relu(h)
        agg2 = _mean_agg(h, src, dst, h.shape[0])
        out = agg2 @ Wl2 + h @ Wr2 + b2 + h @ Wlin2 + blin2
        return out

    def _L1_ffn_ref(h, gate_w, gate_b, w1, b1, w2, b2):
        import math
        import jax, jax.numpy as jnp
        import numpy as np
        CAPACITY_FACTOR = 1.25
        B, L, D = h.shape
        E = gate_w.shape[1]
        T = B * L
        C = max(1, math.ceil(CAPACITY_FACTOR * T / E))
        x = h.reshape(T, D)
        logits = x @ gate_w + gate_b
        probs = jax.nn.softmax(logits, axis=-1)
        idx = jnp.argmax(probs, axis=-1)
        prb = jnp.take_along_axis(probs, idx[:, None], axis=1)[:, 0]
        one_hot = jax.nn.one_hot(idx, E, dtype=jnp.float32)
        pos = (jnp.cumsum(one_hot, axis=0) * one_hot).sum(-1).astype(jnp.int32) - 1
        kept = pos < C
        pos_safe = jnp.where(kept, pos, C)
        buf = jnp.zeros((E, C, D), dtype=h.dtype).at[idx, pos_safe].set(x, mode='drop')
        hmid = jax.nn.relu(jnp.einsum('ecd,edf->ecf', buf, w1) + b1[:, None, :])
        ybuf = jnp.einsum('ecf,efd->ecd', hmid, w2) + b2[:, None, :]
        pos_g = jnp.minimum(pos, C - 1)
        y_tok = ybuf[idx, pos_g] * (prb * kept)[:, None]
        y = y_tok.reshape(B, L, D)
        y = jnp.nan_to_num(y, nan=0.0, posinf=10000.0, neginf=-10000.0)
        return y
    edge_index = jnp.stack([src, dst])
    edge_index_t = jnp.stack([src, dst], axis=1)
    x = x + _L0_gnn_ref(_layernorm(x, axis=-1), edge_index_t, L0_gnn_W, L0_gnn_b)
    x = x + _L0_ffn_ref(_layernorm(x, axis=-1)[None], L0_ffn_W_fx, L0_ffn_b_fx, L0_ffn_W_x, L0_ffn_b_x, L0_ffn_W_slice, L0_ffn_b_slice, L0_ffn_W_q, L0_ffn_W_k, L0_ffn_W_v, L0_ffn_W_out, L0_ffn_b_out, L0_ffn_temperature)[0]
    x = x + _L1_gnn_ref(_layernorm(x, axis=-1), edge_index, L1_gnn_Wl1, L1_gnn_Wr1, L1_gnn_b1, L1_gnn_Wlin1, L1_gnn_blin1, L1_gnn_Wl2, L1_gnn_Wr2, L1_gnn_b2, L1_gnn_Wlin2, L1_gnn_blin2)
    x = x + _L1_ffn_ref(_layernorm(x, axis=-1)[None], L1_ffn_gate_w, L1_ffn_gate_b, L1_ffn_w1, L1_ffn_b1, L1_ffn_w2, L1_ffn_b2)[0]
    return x

_drawn_inputs = setup_inputs


def setup_inputs(seed=0):
    import zlib

    import numpy as np

    out = dict(_drawn_inputs(seed))
    spreads = {'L0_ffn_b_fx': (0.0, 0.1),
     'L0_ffn_b_x': (0.0, 0.8),
     'L0_ffn_b_slice': (0.0, 2.0),
     'L0_ffn_b_out': (0.0, 0.1),
     'L0_ffn_temperature': (0.5, 0.6),
     'L1_gnn_b1': (0.0, 0.1),
     'L1_gnn_blin1': (0.0, 0.1),
     'L1_gnn_b2': (0.0, 0.1),
     'L1_gnn_blin2': (0.0, 0.1),
     'L1_ffn_gate_b': (0.0, 0.1),
     'L1_ffn_b1': (0.0, 0.8),
     'L1_ffn_b2': (0.0, 0.654)}
    factors = {'L0_gnn_b': 3.018,
     'L0_ffn_W_x': 8.0,
     'L0_ffn_W_slice': 8.0,
     'L0_ffn_W_q': 8.0,
     'L0_ffn_W_k': 8.0}
    for name, (base, spread) in spreads.items():
        noise = np.random.default_rng([zlib.crc32(name.encode()), seed]).standard_normal(out[name].shape)
        drawn = base * np.exp(spread * noise) if base else spread * noise
        out[name] = jnp.asarray(drawn.astype(out[name].dtype))
    for name, factor in factors.items():
        out[name] = (out[name] * factor).astype(out[name].dtype)
    return out
```

```python
from contextlib import ExitStack

import numpy as np

import concourse.bass as bass
from concourse import mybir

fp32 = mybir.dt.float32
bf16 = mybir.dt.bfloat16
i32 = mybir.dt.int32
ALU = mybir.AluOpType
ACT = mybir.ActivationFunctionType
AX = mybir.AxisListType

P = 128
N = 6250
D = 256
E = 200000
NB = -(-N // P)
LAST = N - (NB - 1) * P
KD = D // P
EPS = 1e-5

CE = 125
GC = 4
GE = CE * GC
BG = 4
BC = BG * GC
BE = CE * BC
BATCHES = E // BE
BITS = 13
assert BATCHES * BE == E and BATCHES % 2 == 0 and N < 1 << BITS

SW = 256
NSLAB = -(-N // SW)
SH = 64
COUNTS = NSLAB * P * SH * SW
SPARE = COUNTS

H, G, C = 8, 64, 64
HG = H * G

EX = 8
FF = 1024
ROWS = 1024
CAP = max(1, -(-5 * N // (4 * EX)))


class Own:

    def __init__(self, eng, sem):
        self.eng, self.sem, self.at, self.k = eng, sem, 0, 0

    def loop(self, at):
        self.at, self.k = at, 0

    def __call__(self, ins):
        self.k += 1
        ins.then_inc(self.sem, 1)
        self.eng.wait_ge(self.sem, self.at + self.k)


def pairs(eng, n, body):
    with eng.Fori(0, n // 2) as t:
        body(2 * t, 0, t)
        body(2 * t + 1, 1, t)
    if n % 2:
        body(n - 1, 0, n // 2)


def moments(nc, step, stats, mv, var):
    n2 = float(D)
    step(nc.vector.tensor_tensor(mv[:, 1, :], stats[:, :, 1], stats[:, :, 4], ALU.subtract))
    step(nc.vector.tensor_tensor(mv[:, 0, :], stats[:, :, 1], stats[:, :, 4], ALU.add))
    step(nc.vector.tensor_scalar(mv[:, 0, :], mv[:, 0, :], 0.5, None, ALU.mult))
    step(nc.vector.tensor_tensor(mv[:, 1, :], mv[:, 1, :], mv[:, 1, :], ALU.mult))
    step(nc.vector.tensor_tensor(var[:, :], stats[:, :, 2], stats[:, :, 5], ALU.add))
    step(nc.vector.tensor_scalar(mv[:, 1, :], mv[:, 1, :], n2 / 4, None, ALU.mult))
    step(nc.vector.tensor_tensor(var[:, :], var[:, :], mv[:, 1, :], ALU.add))
    step(nc.vector.tensor_scalar(var[:, :], var[:, :], 1 / n2, None, ALU.mult))


class Core:

    def __init__(self, nc, ctx, ins, out):
        self.nc, self.ctx, self.ins, self.out = nc, ctx, ins, out
        self.x = self.sb(ctx, "nodes", [P, NB, D], fp32)
        self.ident = self.sb(ctx, "ident", [P, P], fp32)
        self.valid = self.sb(ctx, "valid", [P, NB], fp32)
        self.eps = self.sb(ctx, "eps", [P, 1], fp32)
        self.deg = self.sb(ctx, "deg", [P, 2, NB], fp32)
        self.kept = nc.dram_tensor("kept_nodes", [NB * P, D], fp32).ap()
        self.inbox = nc.dram_tensor("inbox", [EX * ROWS + NB * P, D], fp32).ap()
        self.outbox = nc.dram_tensor("outbox", [EX * ROWS, D], fp32).ap()
        self.counts = nc.dram_tensor("counts", [COUNTS + GE, 1], fp32).ap()

    def sb(self, ctx, name, shape, dt):
        return ctx.enter_context(self.nc.sbuf_tensor(name, shape, dt))

    def ps(self, ctx, name, shape, dt=fp32):
        return ctx.enter_context(self.nc.psum_tensor(name, shape, dt))

    def sem(self, name):
        return self.ctx.enter_context(self.nc.semaphore(name))


def counts_slab(k, slab, b0, b1):
    v = k.counts[0:COUNTS, :].rearrange("(g p h w) o -> g p h (w o)", g=NSLAB, p=P, h=SH)
    return v[slab, :, b0:b1, :]


def row(vec, n=P):
    return vec.rearrange("(o n) -> o n", o=1).to_broadcast([n, vec.shape[0]])


def stage_linear(k, feat):
    nc = k.nc
    x = k.x
    with ExitStack() as c:
        zero = k.sb(c, "zero", [P, NB * SW], fp32)
        wt = k.sb(c, "wt", [P, KD, D], fp32)
        bias = k.sb(c, "bias", [P, D], fp32)
        stats = k.sb(c, "stats", [P, NB, 6], fp32)
        mv = k.sb(c, "mv", [P, 2, NB], fp32)
        sd = k.sb(c, "sd", [P, NB], fp32)
        rstd = k.sb(c, "rstd", [P, NB], fp32)
        xn = k.sb(c, "xn", [P, 2, D], fp32)
        xnT = k.sb(c, "xnT", [P, 2, KD, P], fp32)
        pT = [k.ps(c, f"pT{i}", [P, KD, P]) for i in range(2)]
        pH = [k.ps(c, f"pH{i}", [P, D]) for i in range(2)]
        x_zeroed, stats_made, x_in, w_in, zeros, mask_made, counts_zeroed = map(
            k.sem, ("a_x_zeroed", "a_stats_made", "a_x_in", "a_w_in", "a_zeros", "a_mask_made", "counts_zeroed"))
        var_ready, sd_ready, xn_ready, t_done, xnT_ready, h_done, h_used, own, pown = map(
            k.sem, ("a_var", "a_sd", "a_xn", "a_t", "a_xnT", "a_h", "a_h_used", "a_own", "a_pown"))
        with nc.Block() as block:

            @block.sync
            def _(sp):
                sp.wait_ge(x_zeroed, 1)
                sp.dma_start(x[:, 0:NB - 1, :], k.ins["x"][0:(NB - 1) * P, :].rearrange(
                    "(b p) d -> p b d", p=P)).then_inc(x_in, 16)
                sp.dma_start(x[0:LAST, NB - 1, :], k.ins["x"][(NB - 1) * P:N, :]).then_inc(x_in, 16)
                sp.dma_start(wt[:, :, :], k.ins["L0_gnn_Wt"].rearrange("(t p) n -> p t n", p=P)).then_inc(w_in, 16)
                sp.dma_start(bias[:, :], row(k.ins["L0_gnn_b"])).then_inc(w_in, 16)
                sp.wait_ge(zeros, 1)
                for g in range(NSLAB):
                    sp.dma_start(counts_slab(k, g, 0, NB), zero[:, :].rearrange("p (h w) -> p h w", w=SW)
                                 ).then_inc(counts_zeroed, 16)
                sp.dma_start(k.counts[COUNTS:COUNTS + GE, :].rearrange("(p w) o -> p (w o)", p=CE),
                             zero[0:CE, 0:GC]).then_inc(counts_zeroed, 16)
                sp.dma_start(k.inbox[0:EX * ROWS, :].rearrange("(p r) d -> p (r d)", p=P)[:, 0:NB * SW], zero[:, :]
                             ).then_inc(counts_zeroed, 16)
                sp.dma_start(k.inbox[0:EX * ROWS, :].rearrange("(p r) d -> p (r d)", p=P)[:, NB * SW:EX * ROWS * D // P],
                             zero[:, 0:EX * ROWS * D // P - NB * SW]).then_inc(counts_zeroed, 16)
                sp.wait_ge(counts_zeroed, 16 * (NSLAB + 3))

            @block.gpsimd
            def _(pool):
                step = Own(pool, pown)
                pool.memset(x[:, NB - 1, :], 0.0).then_inc(x_zeroed, 1)
                pool.memset(k.eps[:, :], EPS)
                step(pool.memset(k.ident[:, :], 0.0))
                step(pool.affine_select(out=k.ident[:, :], in_=k.ident[:, :], compare_op=ALU.not_equal, fill=1.0,
                                        base=0, pattern=[[-1, P]], channel_multiplier=1))
                step(pool.memset(k.valid[:, :], 1.0))
                pool.affine_select(out=k.valid[:, NB - 1:NB], in_=k.valid[:, NB - 1:NB], compare_op=ALU.is_ge,
                                   fill=0.0, base=LAST - 1, pattern=[[0, 1]], channel_multiplier=-1
                                   ).then_inc(mask_made, 1)

            @block.vector
            def _(dve):
                step = Own(dve, own)
                nc.vector.memset(zero[:, :], 0.0).then_inc(zeros, 1)
                dve.wait_ge(x_in, 32)
                with dve.Fori(0, NB) as i:
                    nc.vector.bn_stats(stats[:, i, :], x[:, i, :]).then_inc(stats_made, 1)
                dve.wait_ge(stats_made, NB)
                moments(nc, step, stats, mv, sd)
                dve.sem_inc(var_ready, 1)
                dve.wait_ge(sd_ready, 1)
                step(nc.vector.reciprocal(rstd[:, :], sd[:, :]))

                def norm(i, par):
                    dve.wait_ge(t_done, i)
                    nc.vector.tensor_scalar(xn[:, par, :], x[:, i, :], mv[:, 0, bass.ts(i, 1)], rstd[:, bass.ts(i, 1)],
                                            ALU.subtract, ALU.mult).then_inc(xn_ready, 1)

                def add_bias(i, par):
                    dve.wait_ge(h_done, i + 1)
                    nc.vector.tensor_tensor(feat[:, i, :], pH[par][:, :], bias[:, :], ALU.add).then_inc(h_used, 1)

                dve.wait_ge(w_in, 32)

                def body(i, par, _):
                    norm(i, par)
                    add_bias(i, par)

                pairs(dve, NB, body)

            @block.scalar
            def _(act):
                act.wait_ge(var_ready, 1)
                act.wait_ge(x_zeroed, 1)
                act.wait_ge(mask_made, 1)
                nc.scalar.activation(sd[:, :], sd[:, :], ACT.Sqrt, bias=k.eps[:, 0:1]).then_inc(sd_ready, 1)

                def body(i, par, _):
                    act.wait_ge(t_done, i + 1)
                    act.wait_ge(h_done, i)
                    nc.scalar.copy(xnT[:, par, :, :], pT[par][:, :, :]).then_inc(xnT_ready, 1)

                pairs(act, NB, body)

            @block.tensor
            def _(pe):
                pe.wait_ge(w_in, 32)
                pe.wait_ge(mask_made, 1)

                def body(i, par, _):
                    pe.wait_ge(xn_ready, i + 1)
                    for t in range(KD):
                        last = nc.tensor.transpose(pT[par][:, t, :], xn[:, par, t * P:(t + 1) * P], k.ident[:, :])
                    last.then_inc(t_done, 1)
                    pe.wait_ge(xnT_ready, i + 1)
                    pe.wait_ge(h_used, i)
                    for t in range(KD):
                        last = nc.tensor.matmul(pH[par][:, :], xnT[:, par, t, :], wt[:, t, :],
                                                start=(t == 0), stop=(t == KD - 1))
                    last.then_inc(h_done, 1)

                pairs(pe, NB, body)


def stage_count(k):
    nc = k.nc
    delta = 2.0 ** -10
    assert GE * delta < 0.5
    with ExitStack() as c:
        node = k.sb(c, "node", [CE, 2, 2, BC], i32)
        raw = k.sb(c, "raw", [2 * BITS, 2, BE], i32)
        bit = k.sb(c, "bit", [2 * BITS, BE], i32)
        code = k.sb(c, "code", [2 * BITS, 2, BE], bf16)
        shift = k.sb(c, "shift", [2 * BITS, 1], i32)
        identb = k.sb(c, "identb", [CE, CE], bf16)
        earlier = k.sb(c, "earlier", [CE, GC, GE], bf16)
        lane = k.sb(c, "lane", [CE, P], bf16)
        spare = k.sb(c, "spare", [CE, GC], i32)
        part = k.sb(c, "part", [CE, 7, BC], i32)
        cell = k.sb(c, "cell", [CE, 2, BC], i32)
        lowi = k.sb(c, "lowi", [CE, 4, BC], i32)
        low = k.sb(c, "low", [CE, 2, 4, BC], bf16)
        hot = k.sb(c, "hot", [CE, 2, 2, GC, P], bf16)
        hoth = k.sb(c, "hoth", [CE, 2, 2, GC, NB], bf16)
        junk = k.sb(c, "junk", [CE, GC, GE], bf16)
        score = k.sb(c, "score", [CE, 2, GC], fp32)
        whole = k.sb(c, "whole", [CE, GC], i32)
        first = k.sb(c, "first", [CE, GC], i32)
        value = k.sb(c, "value", [CE, 2, GC], fp32)
        index = k.sb(c, "index", [CE, 2, GC], i32)
        neg = k.sb(c, "neg", [CE, 1], fp32)
        zb = k.sb(c, "zb", [CE, P], bf16)
        agree = [k.ps(c, f"agree{i}", [P, 512]) for i in range(GC)]
        degp = [k.ps(c, f"degp{i}", [P, 512]) for i in range(2)]
        edges_in = [k.sem(f"edges_in{i}") for i in range(2)]
        edges_used = [k.sem(f"edges_used{i}") for i in range(2)]
        (consts, codes_ready, hot_ready, hot_used, agree_ready, score_ready, score_used,
         slots_ready, slots_free, scattered, deg_done, own, pown) = map(k.sem, (
             "b_consts", "b_codes_ready", "b_hot_ready", "b_hot_used", "b_agree_ready",
             "b_score_ready", "b_score_used", "b_slots_ready", "b_slots_free", "b_scattered",
             "b_deg_done", "b_own", "b_pown"))
        with nc.Block() as block:

            @block.sync
            def _(sp):
                def batch(t, par):
                    sp.wait_ge(edges_used[par], t + 1)
                    for j, name in enumerate(("src", "dst")):
                        v = k.ins[name].rearrange("(b n) -> b n", n=BE)[2 * t + par, :]
                        sp.dma_start(node[:, par, j, :], v.rearrange("(p k) -> p k", k=BC)).then_inc(edges_in[par], 16)
                        sp.dma_start(raw[j * BITS:(j + 1) * BITS, par, :], row(v, BITS)).then_inc(edges_in[par], 16)

                with sp.Fori(0, BATCHES // 2) as t:
                    batch(t, 0)
                    batch(t, 1)

            @block.gpsimd
            def _(pool):
                step = Own(pool, pown)
                pool.iota(shift[:, :], [[0, 1]], base=0, channel_multiplier=1)
                pool.iota(lane[:, :], [[1, P]], base=0, channel_multiplier=0, allow_small_or_imprecise_dtypes=True)
                pool.iota(spare[:, :], [[1, GC]], base=SPARE, channel_multiplier=GC)
                pool.memset(neg[:, :], 1.0 - 2 * BITS)
                pool.memset(zb[:, :], 0.0)
                step(pool.memset(identb[:, :], 0.0))
                step(pool.affine_select(out=identb[:, :], in_=identb[:, :], compare_op=ALU.not_equal, fill=1.0,
                                        base=0, pattern=[[-1, CE]], channel_multiplier=1))
                step(pool.memset(earlier[:, :, :], delta))
                step(pool.affine_select(out=earlier[:, :, :], in_=earlier[:, :, :], compare_op=ALU.is_gt, fill=0.0,
                                        base=0, pattern=[[1, GC], [-1, GE]], channel_multiplier=GC))
                pool.drain().then_inc(consts, 1)

                def group(n, par, _):
                    pool.wait_ge(slots_ready, n + 1)
                    pool.wait_ge(scattered, 16 * GC * n)
                    pool.sem_inc(slots_free, 1)
                    for j in range(GC):
                        pool.indirect_dma_start(
                            out=k.counts[:, :], out_offset=bass.IndirectOffsetOnAxis(ap=index[:, par, j:j + 1], axis=0),
                            in_=value[:, par, j:j + 1], in_offset=None, compute_op=ALU.add).then_inc(scattered, 16)

                pairs(pool, BATCHES * BG, group)
                pool.wait_ge(scattered, 16 * GC * BATCHES * BG)

            @block.vector
            def _(dve):
                step = Own(dve, own)
                PER = 4 + 4 * BG
                dve.wait_ge(consts, 1)
                step(nc.vector.tensor_scalar(bit[:, 0:1], shift[:, :], float(BITS), float(BITS), ALU.is_ge, ALU.mult))
                step(nc.vector.tensor_tensor(shift[:, :], shift[:, :], bit[:, 0:1], ALU.subtract))
                for par in range(2):
                    dve.sem_inc(edges_used[par], 1)
                tt = nc.vector.tensor_tensor
                ts = nc.vector.tensor_scalar

                def prepare(t, par, before):
                    dve.wait_ge(edges_in[par], 64 * t + 64)
                    step(ts(bit[:, :], raw[:, par, :], shift[:, 0:1], 1, ALU.logical_shift_right, ALU.bitwise_and))
                    dve.wait_ge(hot_used, BG * before)
                    ts(code[:, par, :], bit[:, :], 2.0, -1.0, ALU.mult, ALU.add).then_inc(codes_ready, 1)
                    src, dst = node[:, par, 0, :], node[:, par, 1, :]
                    ts(part[:, 0, :], dst, 8, 21, ALU.logical_shift_right, ALU.logical_shift_left)
                    ts(part[:, 1, :], dst, SW - 1, None, ALU.bitwise_and)
                    ts(part[:, 2, :], src, P - 1, 14, ALU.bitwise_and, ALU.logical_shift_left)
                    ts(part[:, 3, :], src, 7, 8, ALU.logical_shift_right, ALU.logical_shift_left)
                    ts(lowi[:, 0, :], src, P - 1, None, ALU.bitwise_and)
                    ts(lowi[:, 1, :], dst, P - 1, None, ALU.bitwise_and)
                    ts(lowi[:, 2, :], src, 7, None, ALU.logical_shift_right)
                    step(ts(lowi[:, 3, :], dst, 7, None, ALU.logical_shift_right))
                    dve.sem_inc(edges_used[par], 1)
                    tt(part[:, 4, :], part[:, 0, :], part[:, 1, :], ALU.bitwise_or)
                    nc.vector.tensor_copy(low[:, par, :, :], lowi[:, :, :])
                    step(tt(part[:, 5, :], part[:, 2, :], part[:, 3, :], ALU.bitwise_or))
                    step(tt(cell[:, par, :], part[:, 4, :], part[:, 5, :], ALU.bitwise_or))

                def groups(b, par):
                    for g in range(BG):
                        n = BG * b + g
                        gp = g % 2
                        js = slice(g * GC, (g + 1) * GC)
                        dve.wait_ge(hot_used, n)
                        tt(hot[:, gp, :, :, :],
                           lane[:, :].rearrange("p (a b l) -> p a b l", a=1, b=1).to_broadcast([CE, 2, GC, P]),
                           low[:, par, 0:2, js].unsqueeze(3).to_broadcast([CE, 2, GC, P]), ALU.is_equal)
                        tt(hoth[:, gp, :, :, :],
                           lane[:, 0:NB].rearrange("p (a b l) -> p a b l", a=1, b=1).to_broadcast([CE, 2, GC, NB]),
                           low[:, par, 2:4, js].unsqueeze(3).to_broadcast([CE, 2, GC, NB]), ALU.is_equal
                           ).then_inc(hot_ready, 1)
                        dve.wait_ge(score_ready, GC * n + 2 * GC)
                        dve.wait_ge(slots_free, n)
                        step(nc.vector.tensor_copy(whole[:, :], score[:, gp, :]))
                        step(tt(first[:, :], score[:, gp, :], whole[:, :], ALU.is_equal))
                        nc.vector.tensor_copy(index[:, gp, :], spare[:, :])
                        step(tt(value[:, gp, :], score[:, gp, :], first[:, :], ALU.mult))
                        dve.sem_inc(score_used, 1)
                        step(nc.vector.copy_predicated(index[:, gp, :], first[:, :], cell[:, par, js]))
                        dve.sem_inc(slots_ready, 1)

                prepare(0, 0, 0)
                first_step = step.k

                def both(t, more):
                    step.loop(first_step + 2 * PER * t)
                    prepare(t, 1, 2 * t)
                    groups(2 * t, 0)
                    if more:
                        prepare(t + 1, 0, 2 * t + 1)
                    groups(2 * t + 1, 1)

                with dve.Fori(0, BATCHES // 2 - 1) as t:
                    both(t, True)
                both(BATCHES // 2 - 1, False)
                dve.wait_ge(deg_done, 1)
                for j in range(2):
                    nc.vector.tensor_copy(k.deg[:, j, :], degp[j][:, 0:NB])

            @block.scalar
            def _(act):
                act.wait_ge(consts, 1)
                act.preload_act_table(ACT.Relu)
                act.sem_inc(score_ready, GC)

                def batch(b):
                    for g in range(BG):
                        n = BG * b + g
                        act.wait_ge(score_used, n)
                        for j in range(GC):
                            act.wait_ge(agree_ready, GC * n + j + 1)
                            nc.scalar.activation(junk[:, j, :], agree[j][0:CE, 0:GE], ACT.Relu, bias=neg[:, 0:1],
                                                 accum_out=score[:, g % 2, j:j + 1]).then_inc(score_ready, 1)

                with act.Fori(0, BATCHES) as b:
                    batch(b)

            @block.tensor
            def _(pe):
                pe.wait_ge(consts, 1)
                for j in range(2):
                    nc.tensor.matmul(degp[j][:, 0:NB], zb[:, :], zb[:, 0:NB], start=True, stop=False,
                                     skip_group_check=True)

                def batch(t, par):
                    b = 2 * t + par
                    pe.wait_ge(codes_ready, b + 1)
                    kk = code[:, par, :].rearrange("b (p k) -> b p k", k=BC)
                    for g in range(BG):
                        n = BG * b + g
                        for j in range(GC):
                            pe.wait_ge(score_ready, GC * n + j + 1)
                            nc.tensor.matmul(agree[j][0:CE, 0:GE], kk[:, :, g * GC + j],
                                             kk[:, :, g * GC:(g + 1) * GC], start=True, stop=False)
                            last = nc.tensor.matmul(agree[j][0:CE, 0:GE], identb[:, :], earlier[:, j, :],
                                                    start=False, stop=True)
                            last.then_inc(agree_ready, 1)
                        pe.wait_ge(hot_ready, n + 1)
                        for s in range(2):
                            for j in range(GC):
                                last = nc.tensor.matmul(degp[s][:, 0:NB], hot[:, g % 2, s, j, :], hoth[:, g % 2, s, j, :],
                                                        start=False, stop=False, skip_group_check=True)
                        last.then_inc(hot_used, 1)

                with pe.Fori(0, BATCHES // 2) as t:
                    batch(t, 0)
                    batch(t, 1)
                for j in range(2):
                    last = nc.tensor.matmul(degp[j][:, 0:NB], zb[:, :], zb[:, 0:NB], start=False, stop=True,
                                            skip_group_check=True)
                last.then_inc(deg_done, 1)


def stage_sum_out(k, feat):
    nc = k.nc
    x = k.x
    Q = 4
    groups = [list(range(q, min(q + Q, NB))) for q in range(0, NB, Q)]
    NQ = len(groups)
    EVEN, ODD = (NQ + 1) // 2, NQ // 2
    with ExitStack() as c:
        rows = [k.sb(c, f"rows{i}", [P, NSLAB, SW], fp32) for i in range(2)]
        turned = [k.sb(c, f"turned{i}", [P, Q, P], fp32) for i in range(Q)]
        dinv = k.sb(c, "dinv", [P, NB], fp32)
        t0 = k.sb(c, "c_t0", [P, NB], fp32)
        both = k.sb(c, "c_both", [P, 2, D], fp32)
        pT = [k.ps(c, f"cT{i}", [P, Q, P]) for i in range(Q)]
        pS = [k.ps(c, f"cS{i}", [P, D]) for i in range(2)]
        rows_in = [k.sem(f"c_rows_in{i}") for i in range(2)]
        rows_used, sd_in, sd_out, m_ready, t_done, act_out, dve_out, mm_done, sum_done, sum_used, x_done, own = map(k.sem, (
            "c_rows_used", "c_sd_in", "c_sd_out", "c_m_ready", "c_t_done", "c_act_out", "c_dve_out", "c_mm_done",
            "c_sum_done", "c_sum_used", "c_x_done", "c_own"))
        by_block = k.counts[0:COUNTS, :].rearrange("(g p h w) o -> p h g (w o)", g=NSLAB, p=P, h=SH)
        with nc.Block() as block:

            @block.sync
            def _(sp):
                sp.sem_inc(rows_used, 2)

                def body(i, par, _):
                    sp.wait_ge(rows_used, i + 1)
                    sp.dma_start(rows[par][:, :, :], by_block[:, i, :, :]).then_inc(rows_in[par], 16)

                pairs(sp, NB, body)

            @block.vector
            def _(dve):
                step = Own(dve, own)
                step(nc.vector.tensor_scalar(t0[:, :], k.deg[:, 0, :], 1.0, None, ALU.add))
                dve.sem_inc(sd_in, 1)
                dve.wait_ge(sd_out, 1)
                step(nc.vector.reciprocal(dinv[:, :], t0[:, :]))
                nc.vector.tensor_tensor(feat[:, :, :], feat[:, :, :], dinv[:, :].unsqueeze(2).to_broadcast([P, NB, D]),
                                        ALU.mult).then_inc(m_ready, 1)
                dve.wait_ge(m_ready, 1)
                dve.sem_inc(sum_used, 1)
                before = step.k

                def finish(i, par):
                    dve.wait_ge(sum_done, i + 1)
                    step(nc.vector.tensor_tensor(both[:, par, :], pS[par][:, :], feat[:, i, :], ALU.add))
                    dve.sem_inc(sum_used, 1)
                    nc.vector.scalar_tensor_tensor(x[:, i, :], both[:, par, :], dinv[:, bass.ts(i, 1)], x[:, i, :],
                                                   ALU.mult, ALU.add).then_inc(x_done, 1)

                def body(i, par, _):
                    step.loop(before + i)
                    for q in range(1, NQ, 2):
                        dve.wait_ge(t_done, NQ * i + q + 1)
                        dve.wait_ge(mm_done, NQ * i + max(q - Q + 1, 0))
                        nc.vector.tensor_copy(turned[q % Q][:, 0:len(groups[q]), :],
                                              pT[q % Q][:, 0:len(groups[q]), :]).then_inc(dve_out, 1)
                    finish(i, par)

                pairs(dve, NB, body)
                dve.wait_ge(x_done, NB)
                nc.vector.tensor_scalar(x[:, NB - 1, :], x[:, NB - 1, :], k.valid[:, NB - 1:NB], None, ALU.mult)

            @block.scalar
            def _(act):
                act.wait_ge(sd_in, 1)
                nc.scalar.activation(t0[:, :], t0[:, :], ACT.Sqrt).then_inc(sd_out, 1)

                def body(i, par, _):
                    for q in range(0, NQ, 2):
                        act.wait_ge(t_done, NQ * i + q + 1)
                        act.wait_ge(mm_done, NQ * i + max(q - Q + 1, 0))
                        nc.scalar.copy(turned[q % Q][:, 0:len(groups[q]), :],
                                       pT[q % Q][:, 0:len(groups[q]), :]).then_inc(act_out, 1)

                pairs(act, NB, body)

            @block.tensor
            def _(pe):
                pe.wait_ge(m_ready, 1)

                def copied(i, q):
                    if q % 2:
                        pe.wait_ge(dve_out, ODD * i + max((q + 1) // 2, 0))
                    else:
                        pe.wait_ge(act_out, EVEN * i + max(q // 2 + 1, 0))

                def turn(i, par, q):
                    copied(i, q - Q)
                    for n, b in enumerate(groups[q]):
                        last = nc.tensor.transpose(pT[q % Q][:, n, :], rows[par][:, b // 2, (b % 2) * P:(b % 2 + 1) * P],
                                                   k.ident[:, :])
                    last.then_inc(t_done, 1)
                    if q == NQ - 1:
                        pe.wait_ge(t_done, NQ * i + NQ)
                        pe.sem_inc(rows_used, 1)

                def body(i, par, t):
                    pe.wait_ge(rows_in[par], 16 * t + 16)
                    turn(i, par, 0)
                    turn(i, par, 1)
                    pe.wait_ge(sum_used, i)
                    for q in range(NQ):
                        if q + 2 < NQ:
                            turn(i, par, q + 2)
                        copied(i, q)
                        for n, b in enumerate(groups[q]):
                            last = nc.tensor.matmul(pS[par][:, :], turned[q % Q][:, n, :], feat[:, b, :],
                                                    start=(b == 0), stop=(b == NB - 1))
                        last.then_inc(mm_done, 1)
                    last = nc.tensor.nop()
                    pe.wait_ge(mm_done, NQ * i + NQ)
                    pe.sem_inc(sum_done, 1)

                pairs(pe, NB, body)


def stage_slice(k):
    nc = k.nc
    x = k.x
    PT = HG // P
    with ExitStack() as c:
        wT = k.sb(c, "d_wT", [P, NB, PT, P], fp32)
        stats = k.sb(c, "d_stats", [P, NB, 6], fp32)
        mv = k.sb(c, "d_mv", [P, 2, NB], fp32)
        sd = k.sb(c, "d_sd", [P, NB], fp32)
        rstd = k.sb(c, "d_rstd", [P, NB], fp32)
        ow = k.sb(c, "d_ow", [P, PT, D], fp32)
        bout = k.sb(c, "d_bout", [P, D], fp32)
        wfx = k.sb(c, "d_wfx", [P, KD, HG], fp32)
        bfx = k.sb(c, "d_bfx", [1, HG], fp32)
        wq, wk, wv = (k.sb(c, f"d_w{n}", [C, C], fp32) for n in "qkv")
        wout = k.sb(c, "d_wout", [C, H, D], fp32)
        sums = k.sb(c, "d_sums", [P, PT, D + 1], fp32)
        stats_made, var_ready, sd_ready, own, w_in, sums_ready, ow_ready = map(
            k.sem, ("d_stats_made", "d_var", "d_sd", "d_own", "d_w_in", "d_sums_ready", "d_ow_ready"))
        NW = 8

        with ExitStack() as c1:
            wxT = k.sb(c1, "d_wxT", [C, H, D], fp32)
            wsl = k.sb(c1, "d_wsl", [C, G], fp32)
            bx = k.sb(c1, "d_bx", [C, H], fp32)
            bxw = k.sb(c1, "d_bxw", [C, H, P], fp32)
            bsl = k.sb(c1, "d_bsl", [P, G], fp32)
            temp = k.sb(c1, "d_temp", [P, H], fp32)
            wc = k.sb(c1, "d_wc", [P, KD, HG], fp32)
            bc = k.sb(c1, "d_bc", [P, H, G], fp32)
            xa = k.sb(c1, "d_xa", [P, 2, D + 1], fp32)
            xnT = k.sb(c1, "d_xnT", [P, 2, KD, P], fp32)
            lg = k.sb(c1, "d_lg", [P, 2, H, G], fp32)
            sw = k.sb(c1, "d_sw", [P, 2, HG], fp32)
            mx = k.sb(c1, "d_mx", [P, 2, H], fp32)
            pS = [k.ps(c1, f"dS{i}", [P, D + 1]) for i in range(PT)]
            pT = k.ps(c1, "dT", [P, KD, P])
            pL = [k.ps(c1, f"dL{i}", [P, HG]) for i in range(2)]
            pW = k.ps(c1, "dW", [P, PT, P])
            (wc_ready, w_scaled, bxw_ready, xn_ready, t_done, xnT_ready, l_ready, l_shifted, e_ready, sw_ready, st_done,
             w_done, w_stored, c_in) = map(k.sem, (
                 "d_wc_ready", "d_w_scaled", "d_bxw_ready", "d_xn_ready", "d_t_done", "d_xnT_ready", "d_l_ready",
                 "d_l_shifted", "d_e_ready", "d_sw_ready", "d_st_done", "d_w_done", "d_w_stored", "d_c_in"))
            with nc.Block() as block:

                @block.sync
                def _(sp):
                    ld = lambda o, i: sp.dma_start(o, i).then_inc(c_in, 16)
                    ld(wxT[:, :, :], k.ins["L0_ffn_W_xt"].rearrange("(h c) f -> c h f", c=C))
                    ld(wsl[:, :], k.ins["L0_ffn_W_slice"])
                    ld(bx[:, :], k.ins["L0_ffn_b_xt"])
                    ld(bsl[:, :], row(k.ins["L0_ffn_b_slice"]))
                    ld(temp[:, :], k.ins["L0_ffn_temperature"].rearrange("a h b c -> a (h b c)").to_broadcast([P, H]))
                    sp.wait_ge(c_in, 16 * 5)
                    ld = lambda o, i: sp.dma_start(o, i).then_inc(w_in, 16)
                    ld(wfx[:, :, :], k.ins["L0_ffn_W_fx"].rearrange("(t p) n -> p t n", p=P))
                    ld(bfx[:, :], row(k.ins["L0_ffn_b_fx"], 1))
                    ld(wq[:, :], k.ins["L0_ffn_W_q"])
                    ld(wk[:, :], k.ins["L0_ffn_W_k"])
                    ld(wv[:, :], k.ins["L0_ffn_W_v"])
                    ld(wout[:, :, :], k.ins["L0_ffn_W_out"].rearrange("(h c) n -> c h n", c=C))
                    ld(bout[:, :], row(k.ins["L0_ffn_b_out"]))
                    sp.wait_ge(w_in, 16 * 7)

                @block.vector
                def _(dve):
                    step = Own(dve, own)
                    tt, ts = nc.vector.tensor_tensor, nc.vector.tensor_scalar
                    dve.wait_ge(c_in, 16 * 5)
                    nc.vector.tensor_copy(bxw[:, :, :], bx[:, :].unsqueeze(2).to_broadcast([C, H, P])
                                          ).then_inc(bxw_ready, 1)
                    step(ts(temp[:, :], temp[:, :], 0.1, 5.0, ALU.max, ALU.min))
                    step(nc.vector.reciprocal(temp[:, :], temp[:, :]))
                    dve.wait_ge(wc_ready, 1)
                    rt = temp[:, :].unsqueeze(2).to_broadcast([P, H, G])
                    for t in range(KD):
                        tt(wc[:, t, :].rearrange("p (h g) -> p h g", h=H), pL[t][:, :].rearrange("p (h g) -> p h g", h=H),
                           rt, ALU.mult)
                    step(tt(bc[:, :, :], pS[0][:, :].rearrange("p (h g) -> p h g", h=H) if False else
                            pW[:, :, :].rearrange("p a b -> p (a b)").rearrange("p (h g) -> p h g", h=H),
                            bsl[:, :].unsqueeze(1).to_broadcast([P, H, G]), ALU.add))
                    step(tt(bc[:, :, :], bc[:, :, :], rt, ALU.mult))
                    dve.sem_inc(w_scaled, 1)
                    with dve.Fori(0, NB) as i:
                        nc.vector.bn_stats(stats[:, i, :], x[:, i, :]).then_inc(stats_made, 1)
                    dve.wait_ge(stats_made, NB)
                    moments(nc, step, stats, mv, sd)
                    dve.sem_inc(var_ready, 1)
                    dve.wait_ge(sd_ready, 1)
                    step(nc.vector.reciprocal(rstd[:, :], sd[:, :]))

                    def norm(i, par):
                        dve.wait_ge(st_done, i)
                        ts(xa[:, par, 0:D], x[:, i, :], mv[:, 0, bass.ts(i, 1)], rstd[:, bass.ts(i, 1)],
                           ALU.subtract, ALU.mult)
                        nc.vector.tensor_copy(xa[:, par, D:D + 1], k.valid[:, bass.ts(i, 1)]).then_inc(xn_ready, 1)

                    norm(0, 0)
                    before = step.k

                    def body(i, par, _):
                        step.loop(before + 4 * i)
                        if not (isinstance(i, int) and i == NB - 1):
                            norm(i + 1, 1 - par)
                        dve.wait_ge(l_ready, i + 1)
                        l = lg[:, par, :, :]
                        step(tt(l, pL[par][:, :].rearrange("p (h g) -> p h g", h=H), bc[:, :, :], ALU.add))
                        step(nc.vector.tensor_reduce(mx[:, par, :], l, axis=AX.X, op=ALU.max))
                        tt(l, l, mx[:, par, :].unsqueeze(2).to_broadcast([P, H, G]), ALU.subtract).then_inc(l_shifted, 1)
                        dve.wait_ge(e_ready, i + 1)
                        step(nc.vector.tensor_reduce(mx[:, par, :], l, axis=AX.X, op=ALU.add))
                        step(nc.vector.reciprocal(mx[:, par, :], mx[:, par, :]))
                        dve.wait_ge(w_done, i)
                        tt(sw[:, par, :].rearrange("p (h g) -> p h g", h=H), l,
                           mx[:, par, :].unsqueeze(2).to_broadcast([P, H, G]), ALU.mult).then_inc(sw_ready, 1)

                    pairs(dve, NB, body)
                    step.loop(before + 4 * NB)
                    dve.wait_ge(st_done, NB + 1)
                    for j in range(PT):
                        nc.vector.tensor_copy(sums[:, j, :], pS[j][:, :])

                @block.scalar
                def _(act):
                    act.wait_ge(var_ready, 1)
                    nc.scalar.activation(sd[:, :], sd[:, :], ACT.Sqrt, bias=k.eps[:, 0:1]).then_inc(sd_ready, 1)
                    act.preload_act_table(ACT.Exp)

                    def turn(i, par):
                        act.wait_ge(t_done, i + 1)
                        act.wait_ge(l_ready, i)
                        nc.scalar.copy(xnT[:, par, :, :], pT[:, :, :]).then_inc(xnT_ready, 1)

                    turn(0, 0)

                    def body(i, par, _):
                        if not (isinstance(i, int) and i == NB - 1):
                            turn(i + 1, 1 - par)
                        act.wait_ge(l_shifted, i + 1)
                        nc.scalar.activation(lg[:, par, :, :], lg[:, par, :, :], ACT.Exp).then_inc(e_ready, 1)
                        act.wait_ge(w_done, i + 1)
                        nc.scalar.copy(wT[:, i, :, :], pW[:, :, :]).then_inc(w_stored, 1)

                    pairs(act, NB, body)

                @block.tensor
                def _(pe):
                    pe.wait_ge(bxw_ready, 1)
                    for h in range(H):
                        hs = slice(h * G, (h + 1) * G)
                        for t in range(KD):
                            nc.tensor.matmul(pL[t][:, hs], wxT[:, h, t * P:(t + 1) * P], wsl[:, :], start=True, stop=True)
                        last = nc.tensor.matmul(pW[:, :, :].rearrange("p a b -> p (a b)")[:, hs], bxw[:, h, :], wsl[:, :],
                                                start=True, stop=True)
                    last.then_inc(wc_ready, 1)
                    pe.wait_ge(w_scaled, 1)
                    pe.sem_inc(st_done, 1)

                    def front(i, par):
                        pe.wait_ge(xn_ready, i + 1)
                        pe.wait_ge(xnT_ready, i)
                        for t in range(KD):
                            last = nc.tensor.transpose(pT[:, t, :], xa[:, par, t * P:(t + 1) * P], k.ident[:, :])
                        last.then_inc(t_done, 1)
                        pe.wait_ge(xnT_ready, i + 1)
                        pe.wait_ge(l_shifted, i)
                        for t in range(KD):
                            last = nc.tensor.matmul(pL[par][:, :], xnT[:, par, t, :], wc[:, t, :],
                                                    start=(t == 0), stop=(t == KD - 1))
                        last.then_inc(l_ready, 1)

                    def back(i, par, first, last_):
                        pe.wait_ge(sw_ready, i + 1)
                        pe.wait_ge(w_stored, i)
                        for j in range(PT):
                            last = nc.tensor.matmul(pS[j][:, :], sw[:, par, j * P:(j + 1) * P], xa[:, par, :],
                                                    start=first, stop=last_, skip_group_check=True)
                        last.then_inc(st_done, 1)
                        for j in range(PT):
                            last = nc.tensor.transpose(pW[:, j, :], sw[:, par, j * P:(j + 1) * P], k.ident[:, :])
                        last.then_inc(w_done, 1)

                    front(0, 0)
                    front(1, 1)
                    back(0, 0, True, False)
                    with pe.Fori(0, (NB - 3) // 2) as t:
                        front(2 * t + 2, 0)
                        back(2 * t + 1, 1, False, False)
                        front(2 * t + 3, 1)
                        back(2 * t + 2, 0, False, False)
                    front(NB - 1, 0)
                    back(NB - 2, 1, False, False)
                    back(NB - 1, 0, False, True)

        with ExitStack() as c2:
            tokT = k.sb(c2, "d_tokT", [C, HG], fp32)
            qT = k.sb(c2, "d_qT", [C, HG], fp32)
            kT = k.sb(c2, "d_kT", [C, HG], fp32)
            vv = k.sb(c2, "d_vv", [G, HG], fp32)
            att = k.sb(c2, "d_att", [G, H, G], fp32)
            attT = k.sb(c2, "d_attT", [G, HG], fp32)
            oT = k.sb(c2, "d_oT", [C, HG], fp32)
            sT = k.sb(c2, "d_sT", [P, KD, HG], fp32)
            nT = k.sb(c2, "d_nT", [1, HG], fp32)
            mx = k.sb(c2, "d_amx", [G, H], fp32)
            rn = k.sb(c2, "d_rn", [P, PT], fp32)
            pp = [k.ps(c2, f"dP{i}", [P, 512]) for i in range(8)]
            pe_done, other_done, vown = map(k.sem, ("d_pe_done", "d_other_done", "d_vown"))
            with nc.Block() as block:

                @block.vector
                def _(dve):
                    step = Own(dve, vown)
                    tt, ts = nc.vector.tensor_tensor, nc.vector.tensor_scalar

                    def after_pe(n):
                        dve.wait_ge(pe_done, n)

                    step(ts(rn[:, :], sums[:, :, D], 1e-5, None, ALU.add))
                    step(nc.vector.reciprocal(rn[:, :], rn[:, :]))
                    step(tt(sums[:, :, :], sums[:, :, :], rn[:, :].unsqueeze(2).to_broadcast([P, PT, D + 1]), ALU.mult))
                    dve.sem_inc(other_done, 1)
                    after_pe(1)
                    for t in range(KD):
                        nc.vector.tensor_copy(sT[:, t, :], pp[t][:, :])
                    step(nc.vector.tensor_copy(nT[:, :], pp[2][0:1, :]))
                    dve.sem_inc(other_done, 1)
                    after_pe(2)
                    step(nc.vector.tensor_copy(tokT[:, :], pp[3][0:C, :]))
                    dve.sem_inc(other_done, 1)
                    after_pe(3)
                    nc.vector.tensor_copy(qT[:, :], pp[4][0:C, :])
                    nc.vector.tensor_copy(kT[:, :], pp[5][0:C, :])
                    step(nc.vector.tensor_copy(vv[:, :], pp[6][0:G, :]))
                    dve.sem_inc(other_done, 1)
                    after_pe(4)
                    s3 = pp[7][0:G, :].rearrange("p (h g) -> p h g", h=H)
                    step(nc.vector.tensor_reduce(mx[:, :], s3, axis=AX.X, op=ALU.max))
                    step(tt(att[:, :, :], s3, mx[:, :].unsqueeze(2).to_broadcast([G, H, G]), ALU.subtract))
                    dve.sem_inc(other_done, 1)
                    dve.wait_ge(other_done, 6)
                    step(nc.vector.tensor_reduce(mx[:, :], att[:, :, :], axis=AX.X, op=ALU.add))
                    step(nc.vector.reciprocal(mx[:, :], mx[:, :]))
                    step(tt(att[:, :, :], att[:, :, :], mx[:, :].unsqueeze(2).to_broadcast([G, H, G]), ALU.mult))
                    dve.sem_inc(other_done, 1)
                    after_pe(5)
                    step(nc.vector.tensor_copy(attT[:, :], pp[0][0:G, :]))
                    dve.sem_inc(other_done, 1)
                    after_pe(6)
                    step(nc.vector.tensor_copy(oT[:, :], pp[1][0:C, :]))
                    dve.sem_inc(other_done, 1)
                    after_pe(7)
                    for j in range(PT):
                        nc.vector.tensor_copy(ow[:, j, :], pp[2 + j][:, 0:D])

                @block.scalar
                def _(act):
                    act.wait_ge(other_done, 5)
                    nc.scalar.activation(att[:, :, :], att[:, :, :], ACT.Exp, scale=float(C) ** -0.5).then_inc(other_done, 1)

                @block.tensor
                def _(pe):
                    mm = nc.tensor.matmul
                    hs = [slice(h * C, (h + 1) * C) for h in range(H)]
                    pe.wait_ge(other_done, 1)
                    for j in range(PT):
                        js = slice(j * P, (j + 1) * P)
                        for t in range(KD):
                            nc.tensor.transpose(pp[t][:, js], sums[:, j, t * P:(t + 1) * P], k.ident[:, :])
                        last = nc.tensor.transpose(pp[2][0:1, js], sums[:, j, D:D + 1], k.ident[:, :])
                    last.then_inc(pe_done, 1)
                    pe.wait_ge(other_done, 2)
                    for h in range(H):
                        for t in range(KD):
                            mm(pp[3][0:C, hs[h]], wfx[:, t, hs[h]], sT[:, t, hs[h]], start=(t == 0), stop=False)
                        last = mm(pp[3][0:C, hs[h]], bfx[:, hs[h]], nT[:, hs[h]], start=False, stop=True)
                    last.then_inc(pe_done, 1)
                    pe.wait_ge(other_done, 3)
                    mm(pp[4][0:C, :], wq[:, :], tokT[:, :], start=True, stop=True)
                    mm(pp[5][0:C, :], wk[:, :], tokT[:, :], start=True, stop=True)
                    for h in range(H):
                        last = mm(pp[6][0:G, hs[h]], tokT[:, hs[h]], wv[:, :], start=True, stop=True)
                    last.then_inc(pe_done, 1)
                    pe.wait_ge(other_done, 4)
                    for h in range(H):
                        last = mm(pp[7][0:G, hs[h]], qT[:, hs[h]], kT[:, hs[h]], start=True, stop=True)
                    last.then_inc(pe_done, 1)
                    pe.wait_ge(other_done, 7)
                    for h in range(H):
                        last = nc.tensor.transpose(pp[0][0:G, hs[h]], att[:, h, :], k.ident[0:G, 0:G])
                    last.then_inc(pe_done, 1)
                    pe.wait_ge(other_done, 8)
                    for h in range(H):
                        last = mm(pp[1][0:C, hs[h]], vv[:, hs[h]], attT[:, hs[h]], start=True, stop=True)
                    last.then_inc(pe_done, 1)
                    pe.wait_ge(other_done, 9)
                    for h in range(H):
                        o = (h % 2) * G
                        last = mm(pp[2 + h // 2][o:o + G, 0:D], oT[:, hs[h]], wout[:, h, :], start=True, stop=True)
                    last.then_inc(pe_done, 1)

        with ExitStack() as c3:
            st = k.sb(c3, "d_st", [P, 2, PT, P], fp32)
            tmp = k.sb(c3, "d_tmp", [P, 2, D], fp32)
            pO = [k.ps(c3, f"dO{i}", [P, D]) for i in range(2)]
            st_ready, o_ready, o_used, own3, x_out = map(k.sem, ("d_st_ready", "d_o_ready", "d_o_used", "d_own3", "d_x_out"))
            with nc.Block() as block:

                @block.gpsimd
                def _(pool):
                    def body(i, par, _):
                        pool.wait_ge(o_ready, i)
                        pool.tensor_copy(st[:, par, :, :], wT[:, i, :, :]).then_inc(st_ready, 1)

                    pairs(pool, NB, body)

                @block.tensor
                def _(pe):
                    def body(i, par, _):
                        pe.wait_ge(st_ready, i + 1)
                        pe.wait_ge(o_used, i)
                        for j in range(PT):
                            last = nc.tensor.matmul(pO[par][:, :], st[:, par, j, :], ow[:, j, :],
                                                    start=(j == 0), stop=(j == PT - 1))
                        last.then_inc(o_ready, 1)

                    pairs(pe, NB, body)

                @block.vector
                def _(dve):
                    step = Own(dve, own3)

                    def body(i, par, _):
                        step.loop(i)
                        dve.wait_ge(o_ready, i + 1)
                        step(nc.vector.tensor_tensor(tmp[:, par, :], pO[par][:, :], bout[:, :], ALU.add))
                        dve.sem_inc(o_used, 1)
                        nc.vector.tensor_tensor(x[:, i, :], x[:, i, :], tmp[:, par, :], ALU.add)

                    pairs(dve, NB, body)


def stage_norm(k, src, dst, keep):
    nc = k.nc
    with ExitStack() as c:
        stats = k.sb(c, "e_stats", [P, NB, 6], fp32)
        mv = k.sb(c, "e_mv", [P, 2, NB], fp32)
        sd = k.sb(c, "e_sd", [P, NB], fp32)
        rstd = k.sb(c, "e_rstd", [P, NB], fp32)
        stats_made, var_ready, sd_ready, own, kept = map(k.sem, ("e_stats_made", "e_var", "e_sd", "e_own", "e_kept"))
        with nc.Block() as block:

            @block.sync
            def _(sp):
                sp.dma_start(keep.rearrange("(b p) d -> p b d", p=P), src[:, :, :]).then_inc(kept, 16)
                sp.wait_ge(kept, 16)

            @block.vector
            def _(dve):
                step = Own(dve, own)
                with dve.Fori(0, NB) as i:
                    nc.vector.bn_stats(stats[:, i, :], src[:, i, :]).then_inc(stats_made, 1)
                dve.wait_ge(stats_made, NB)
                moments(nc, step, stats, mv, sd)
                dve.sem_inc(var_ready, 1)
                dve.wait_ge(sd_ready, 1)
                step(nc.vector.reciprocal(rstd[:, :], sd[:, :]))
                with dve.Fori(0, NB) as i:
                    nc.vector.tensor_scalar(dst[:, i, :], src[:, i, :], mv[:, 0, bass.ts(i, 1)],
                                            rstd[:, bass.ts(i, 1)], ALU.subtract, ALU.mult)

            @block.scalar
            def _(act):
                act.wait_ge(var_ready, 1)
                nc.scalar.activation(sd[:, :], sd[:, :], ACT.Sqrt, bias=k.eps[:, 0:1]).then_inc(sd_ready, 1)


def stage_sage(k, n, src, dst, residual):
    nc = k.nc
    HALF = [(0, (NB + 1) // 2), ((NB + 1) // 2, NB)]
    with ExitStack() as c:
        piece = [k.sb(c, f"f{n}_piece{i}", [P, HALF[0][1], SW], fp32) for i in range(2)]
        wl = k.sb(c, f"f{n}_wl", [P, KD, D], fp32)
        wr = k.sb(c, f"f{n}_wr", [P, KD, D], fp32)
        wlin = k.sb(c, f"f{n}_wlin", [P, KD, D], fp32)
        b0 = k.sb(c, f"f{n}_b0", [P, D], fp32)
        b1 = k.sb(c, f"f{n}_b1", [P, D], fp32)
        rdeg = k.sb(c, f"f{n}_rdeg", [P, NB], fp32)
        agg = k.sb(c, f"f{n}_agg", [P, KD, SW], fp32)
        own_rows = k.sb(c, f"f{n}_rows", [P, 2, D], fp32)
        own_T = k.sb(c, f"f{n}_rowsT", [P, 2, KD, P], fp32)
        old = k.sb(c, f"f{n}_old", [P, 2, D], fp32)
        mix = k.sb(c, f"f{n}_mix", [P, 2, D], fp32)
        pA = [k.ps(c, f"f{n}A{i}", [P, SW]) for i in range(KD)]
        pT = k.ps(c, f"f{n}T", [P, 2, KD, P])
        pM = [k.ps(c, f"f{n}M{i}", [P, D]) for i in range(2)]
        pR = [k.ps(c, f"f{n}R{i}", [P, D]) for i in range(2)]
        piece_in = [k.sem(f"f{n}_piece_in{i}") for i in range(2)]
        piece_used = [k.sem(f"f{n}_piece_used{i}") for i in range(2)]
        (w_in, w_ready, old_in, old_used, agg_done, agg_ready, rows_ready, t_done, rT_ready, m_done, m_used, own,
         mixed) = (k.sem(f"f{n}_{m}") for m in (
             "w_in", "w_ready", "old_in", "old_used", "agg_done", "agg_ready", "rows_ready", "t_done", "rT_ready",
             "m_done", "m_used", "own", "mixed"))

        def slabs(eng, body):
            with eng.Fori(0, NSLAB - 1) as g:
                body(g, 2)
            body(NSLAB - 1, NB - 2 * (NSLAB - 1))

        with nc.Block() as block:

            @block.sync
            def _(sp):
                for w, name in ((wl, f"L1_gnn_Wl{n}"), (wr, f"L1_gnn_Wr{n}"), (wlin, f"L1_gnn_Wlin{n}")):
                    sp.dma_start(w[:, :, :], k.ins[name].rearrange("(t p) n -> p t n", p=P)).then_inc(w_in, 16)
                sp.dma_start(b0[:, :], row(k.ins[f"L1_gnn_b{n}"])).then_inc(w_in, 16)
                sp.dma_start(b1[:, :], row(k.ins[f"L1_gnn_blin{n}"])).then_inc(w_in, 16)

                def body(g, blocks):
                    for j, (lo, hi) in enumerate(HALF):
                        sp.wait_ge(piece_used[j], g)
                        sp.dma_start(piece[j][:, 0:hi - lo, :], counts_slab(k, g, lo, hi)).then_inc(piece_in[j], 16)
                    if residual is not None:
                        sp.wait_ge(old_used, g)
                        sp.dma_start(old[:, 0:blocks, :], residual.rearrange("(b p) d -> p b d", p=P)[
                            :, bass.ds(2 * g, blocks), :]).then_inc(old_in, 16)

                slabs(sp, body)

            @block.gpsimd
            def _(pool):
                def body(g, blocks):
                    pool.wait_ge(t_done, g)
                    pool.tensor_copy(own_rows[:, 0:blocks, :], src[:, bass.ds(2 * g, blocks), :]).then_inc(rows_ready, 1)

                slabs(pool, body)

            @block.vector
            def _(dve):
                step = Own(dve, own)
                tt, ts = nc.vector.tensor_tensor, nc.vector.tensor_scalar
                dve.wait_ge(w_in, 16 * 5)
                tt(b0[:, :], b0[:, :], b1[:, :], ALU.add)
                step(ts(rdeg[:, :], k.deg[:, 1, :], 1.0, None, ALU.max))
                step(nc.vector.reciprocal(rdeg[:, :], rdeg[:, :]))
                step(tt(wr[:, :, :], wr[:, :, :], wlin[:, :, :], ALU.add))
                dve.sem_inc(w_ready, 1)
                before = step.k

                def body(g, blocks):
                    per = 3 if residual is not None else 2
                    step.loop(before + 2 * per * g)
                    dve.wait_ge(m_done, g + 1)
                    dve.wait_ge(mixed, g)
                    for j in range(blocks):
                        step(nc.vector.scalar_tensor_tensor(mix[:, j, :], pM[j][:, :], rdeg[:, bass.ds(2 * g + j, 1)],
                                                            b0[:, :], ALU.mult, ALU.add))
                        step(tt(mix[:, j, :], mix[:, j, :], pR[j][:, :], ALU.add))
                    if residual is not None:
                        dve.wait_ge(old_in, 16 * g + 16)
                        for j in range(blocks):
                            step(tt(dst[:, 2 * g + j, :], mix[:, j, :], old[:, j, :], ALU.add))
                        dve.sem_inc(mixed, 1)
                        dve.sem_inc(old_used, 1)
                    dve.sem_inc(m_used, 1)

                slabs(dve, body)

            @block.scalar
            def _(act):
                act.preload_act_table(ACT.Relu)

                def body(g, blocks):
                    act.wait_ge(t_done, g + 1)
                    act.wait_ge(m_done, g)
                    nc.scalar.copy(own_T[:, 0:blocks, :, :], pT[:, 0:blocks, :, :]).then_inc(rT_ready, 1)
                    act.wait_ge(agg_done, g + 1)
                    for t in range(KD):
                        last = nc.scalar.copy(agg[:, t, :], pA[t][:, :])
                    last.then_inc(agg_ready, 1)
                    if residual is None:
                        act.wait_ge(m_used, g + 1)
                        nc.scalar.activation(dst[:, bass.ds(2 * g, blocks), :], mix[:, 0:blocks, :], ACT.Relu
                                             ).then_inc(mixed, 1)

                slabs(act, body)

            @block.tensor
            def _(pe):
                pe.wait_ge(w_ready, 1)

                def body(g, blocks):
                    pe.wait_ge(rows_ready, g + 1)
                    pe.wait_ge(rT_ready, g)
                    for j in range(blocks):
                        for t in range(KD):
                            last = nc.tensor.transpose(pT[:, j, t, :], own_rows[:, j, t * P:(t + 1) * P], k.ident[:, :])
                    last.then_inc(t_done, 1)
                    pe.wait_ge(agg_ready, g)
                    for j, (lo, hi) in enumerate(HALF):
                        pe.wait_ge(piece_in[j], 16 * g + 16)
                        for b in range(lo, hi):
                            for t in range(KD):
                                last = nc.tensor.matmul(pA[t][:, :], src[:, b, t * P:(t + 1) * P], piece[j][:, b - lo, :],
                                                        start=(b == 0), stop=(b == NB - 1))
                        last.then_inc(piece_used[j], 1)
                    last = nc.tensor.nop()
                    pe.wait_ge(piece_used[1], g + 1)
                    pe.sem_inc(agg_done, 1)
                    pe.wait_ge(rT_ready, g + 1)
                    pe.wait_ge(m_used, g)
                    for j in range(blocks):
                        for t in range(KD):
                            nc.tensor.matmul(pR[j][:, :], own_T[:, j, t, :], wr[:, t, :], start=(t == 0), stop=(t == KD - 1))
                    pe.wait_ge(agg_ready, g + 1)
                    for j in range(blocks):
                        for t in range(KD):
                            last = nc.tensor.matmul(pM[j][:, :], agg[:, t, j * P:(j + 1) * P], wl[:, t, :],
                                                    start=(t == 0), stop=(t == KD - 1))
                    last.then_inc(m_done, 1)

                slabs(pe, body)


def stage_route(k, x3, tok, where, weight):
    nc = k.nc
    with ExitStack() as c:
        stats = k.sb(c, "g_stats", [P, NB, 6], fp32)
        mv = k.sb(c, "g_mv", [P, 2, NB], fp32)
        sd = k.sb(c, "g_sd", [P, NB], fp32)
        rstd = k.sb(c, "g_rstd", [P, NB], fp32)
        tn = k.sb(c, "g_tn", [P, 2, D], fp32)
        tT = k.sb(c, "g_tT", [P, 2, KD, P], fp32)
        gw = k.sb(c, "g_gw", [P, KD, EX], fp32)
        gb = k.sb(c, "g_gb", [P, EX], fp32)
        lg = k.sb(c, "g_lg", [P, NB, EX], fp32)
        hot = k.sb(c, "g_hot", [P, NB, EX], fp32)
        cum = k.sb(c, "g_cum", [P, NB, EX], fp32)
        total = k.sb(c, "g_total", [P, NB, EX], fp32)
        a, b, e, pos, kept = (k.sb(c, f"g_{n}", [P, NB], fp32) for n in ("a", "b", "e", "pos", "kept"))
        rank = k.sb(c, "g_rank", [P, EX], fp32)
        token = k.sb(c, "g_token", [P, NB], fp32)
        upto = k.sb(c, "g_upto", [P, P], fp32)
        ones = k.sb(c, "g_ones", [P, P], fp32)
        pT = [k.ps(c, f"gT{i}", [P, KD, P]) for i in range(2)]
        pG = [k.ps(c, f"gG{i}", [P, EX]) for i in range(2)]
        pC = [k.ps(c, f"gC{i}", [P, NB * EX]) for i in range(2)]
        (w_in, stats_made, var_ready, sd_ready, own, consts, tn_ready, stored, t_done, tT_ready, g_done, g_used,
         shifted, e_ready, hot_ready, cum_done, pown) = map(k.sem, (
             "g_w_in", "g_stats_made", "g_var", "g_sd_ready", "g_own", "g_consts", "g_tn_ready", "g_stored", "g_t_done",
             "g_tT_ready", "g_g_done", "g_g_used", "g_shifted", "g_e_ready", "g_hot_ready", "g_cum_done", "g_pown"))
        with nc.Block() as block:

            @block.sync
            def _(sp):
                sp.dma_start(gw[:, :, :], k.ins["L1_ffn_gate_w"].rearrange("(t p) n -> p t n", p=P)).then_inc(w_in, 16)
                sp.dma_start(gb[:, :], row(k.ins["L1_ffn_gate_b"])).then_inc(w_in, 16)

            @block.gpsimd
            def _(pool):
                step = Own(pool, pown)
                pool.iota(rank[:, :], [[-1, EX]], base=EX, channel_multiplier=0, allow_small_or_imprecise_dtypes=True)
                pool.iota(token[:, :], [[P, NB]], base=0, channel_multiplier=1, allow_small_or_imprecise_dtypes=True)
                pool.memset(ones[:, :], 1.0)
                step(pool.memset(upto[:, :], 1.0))
                step(pool.affine_select(out=upto[:, :], in_=upto[:, :], compare_op=ALU.is_ge, fill=0.0, base=0,
                                        pattern=[[1, P]], channel_multiplier=-1))
                pool.sem_inc(consts, 1)

                def body(i, par, _):
                    pool.wait_ge(tn_ready, i + 1)
                    pool.tensor_copy(tok[:, i, :], tn[:, par, :]).then_inc(stored, 1)

                pairs(pool, NB, body)

            @block.vector
            def _(dve):
                step = Own(dve, own)
                tt, ts = nc.vector.tensor_tensor, nc.vector.tensor_scalar
                with dve.Fori(0, NB) as i:
                    nc.vector.bn_stats(stats[:, i, :], x3[:, i, :]).then_inc(stats_made, 1)
                dve.wait_ge(stats_made, NB)
                moments(nc, step, stats, mv, sd)
                dve.sem_inc(var_ready, 1)
                dve.wait_ge(sd_ready, 1)
                step(nc.vector.reciprocal(rstd[:, :], sd[:, :]))
                dve.wait_ge(w_in, 32)

                def norm(i, par):
                    dve.wait_ge(t_done, i)
                    dve.wait_ge(stored, i)
                    ts(tn[:, par, :], x3[:, i, :], mv[:, 0, bass.ts(i, 1)], rstd[:, bass.ts(i, 1)],
                       ALU.subtract, ALU.mult).then_inc(tn_ready, 1)

                def body(i, par, _):
                    norm(i, par)
                    dve.wait_ge(g_done, i + 1)
                    tt(lg[:, i, :], pG[par][:, :], gb[:, :], ALU.add).then_inc(g_used, 1)

                pairs(dve, NB, body)
                dve.wait_ge(g_used, NB)
                dve.wait_ge(consts, 1)
                wide = lambda v: v.unsqueeze(2).to_broadcast([P, NB, EX])
                step(nc.vector.tensor_reduce(a[:, :], lg[:, :, :], axis=AX.X, op=ALU.max))
                step(tt(lg[:, :, :], lg[:, :, :], wide(a[:, :]), ALU.subtract))
                dve.sem_inc(shifted, 1)
                dve.wait_ge(e_ready, 1)
                step(nc.vector.tensor_reduce(a[:, :], lg[:, :, :], axis=AX.X, op=ALU.add))
                step(nc.vector.reciprocal(weight[:, :], a[:, :]))
                step(ts(hot[:, :, :], lg[:, :, :], 1.0, None, ALU.is_ge))
                rk = rank[:, :].unsqueeze(1).to_broadcast([P, NB, EX])
                step(tt(hot[:, :, :], hot[:, :, :], rk, ALU.mult))
                step(nc.vector.tensor_reduce(e[:, :], hot[:, :, :], axis=AX.X, op=ALU.max))
                step(tt(hot[:, :, :], rk, wide(e[:, :]), ALU.is_equal))
                step(ts(e[:, :], e[:, :], -1.0, float(EX), ALU.mult, ALU.add))
                step(tt(hot[:, :, :], hot[:, :, :], wide(k.valid[:, :]), ALU.mult))
                dve.sem_inc(hot_ready, 1)
                dve.wait_ge(cum_done, 1)
                flat = lambda v: v[:, :, :].rearrange("p b e -> p (b e)")
                nc.vector.tensor_copy(flat(cum), pC[0][:, :])
                step(nc.vector.tensor_copy(flat(total), pC[1][:, :]))
                step(tt(flat(cum), flat(cum), flat(total), ALU.subtract))
                src, other = total, lg
                reach = 1
                while reach < NB:
                    nc.vector.tensor_copy(other[:, 0:reach, :], src[:, 0:reach, :])
                    step(tt(other[:, reach:NB, :], src[:, reach:NB, :], src[:, 0:NB - reach, :], ALU.add))
                    src, other = other, src
                    reach *= 2
                step(tt(flat(cum), flat(cum), flat(src), ALU.add))
                step(tt(cum[:, :, :], cum[:, :, :], hot[:, :, :], ALU.mult))
                step(nc.vector.tensor_reduce(pos[:, :], cum[:, :, :], axis=AX.X, op=ALU.add))
                step(ts(pos[:, :], pos[:, :], -1.0, None, ALU.add))
                step(ts(kept[:, :], pos[:, :], float(CAP), None, ALU.is_lt))
                tt(weight[:, :], weight[:, :], kept[:, :], ALU.mult)
                step(ts(pos[:, :], pos[:, :], float(CAP - 1), 0.0, ALU.min, ALU.max))
                step(ts(e[:, :], e[:, :], float(ROWS), None, ALU.mult))
                step(tt(pos[:, :], pos[:, :], e[:, :], ALU.add))
                nc.vector.tensor_copy(where[:, 1, :], pos[:, :])
                step(ts(a[:, :], token[:, :], float(EX * ROWS), None, ALU.add))
                step(tt(pos[:, :], pos[:, :], a[:, :], ALU.subtract))
                step(tt(pos[:, :], pos[:, :], kept[:, :], ALU.mult))
                step(tt(pos[:, :], pos[:, :], a[:, :], ALU.add))
                nc.vector.tensor_copy(where[:, 0, :], pos[:, :])

            @block.scalar
            def _(act):
                act.wait_ge(var_ready, 1)
                nc.scalar.activation(sd[:, :], sd[:, :], ACT.Sqrt, bias=k.eps[:, 0:1]).then_inc(sd_ready, 1)

                def body(i, par, _):
                    act.wait_ge(t_done, i + 1)
                    act.wait_ge(g_done, i)
                    nc.scalar.copy(tT[:, par, :, :], pT[par][:, :, :]).then_inc(tT_ready, 1)

                pairs(act, NB, body)
                act.wait_ge(shifted, 1)
                nc.scalar.activation(lg[:, :, :], lg[:, :, :], ACT.Exp).then_inc(e_ready, 1)

            @block.tensor
            def _(pe):
                pe.wait_ge(w_in, 32)

                def body(i, par, _):
                    pe.wait_ge(tn_ready, i + 1)
                    pe.wait_ge(tT_ready, i)
                    for t in range(KD):
                        last = nc.tensor.transpose(pT[par][:, t, :], tn[:, par, t * P:(t + 1) * P], k.ident[:, :])
                    last.then_inc(t_done, 1)
                    pe.wait_ge(tT_ready, i + 1)
                    pe.wait_ge(g_used, i)
                    for t in range(KD):
                        last = nc.tensor.matmul(pG[par][:, :], tT[:, par, t, :], gw[:, t, :], start=(t == 0),
                                                stop=(t == KD - 1))
                    last.then_inc(g_done, 1)

                pairs(pe, NB, body)
                pe.wait_ge(hot_ready, 1)
                h = hot[:, :, :].rearrange("p b e -> p (b e)")
                nc.tensor.matmul(pC[0][:, :], upto[:, :], h, start=True, stop=True)
                nc.tensor.matmul(pC[1][:, :], ones[:, :], h, start=True, stop=True).then_inc(cum_done, 1)


def stage_experts(k, x3, tok, where, weight):
    nc = k.nc
    FT = FF // P
    TT = ROWS // P
    LT = CAP - (TT - 1) * P
    SPLIT = [(0, (CAP + 1) // 2), ((CAP + 1) // 2, CAP)]
    inbox, outbox = k.inbox, k.outbox
    sent, = (k.sem("h_sent"),)
    with nc.Block() as block:

        @block.gpsimd
        def _(pool):
            for b in range(NB):
                n = P if b < NB - 1 else LAST
                pool.indirect_dma_start(out=inbox[:, :], out_offset=bass.IndirectOffsetOnAxis(ap=where[0:n, 0, b:b + 1], axis=0),
                                        in_=tok[0:n, b, :], in_offset=None).then_inc(sent, 16)
            pool.wait_ge(sent, 16 * NB)

    with ExitStack() as c:
        w1 = [k.sb(c, f"h_w1{i}", [P, KD, FF], fp32) for i in range(2)]
        w2 = [k.sb(c, f"h_w2{i}", [P, FT, D], fp32) for i in range(2)]
        b1 = [k.sb(c, f"h_b1{i}", [P, FT], fp32) for i in range(2)]
        b2 = k.sb(c, "h_b2", [P, EX, D], fp32)
        rows = k.sb(c, "h_rows", [P, TT, D], fp32)
        rT = k.sb(c, "h_rT", [P, KD, TT, P], fp32)
        hT = k.sb(c, "h_hT", [P, FT, CAP], fp32)
        y = k.sb(c, "h_y", [P, TT, D], fp32)
        pT = [k.ps(c, f"hT{i}", [P, KD, P]) for i in range(2)]
        pH = [k.ps(c, f"hH{i}", [P, 512]) for i in range(4)]
        pY = [k.ps(c, f"hY{i}", [P, D]) for i in range(2)]
        w_in = [k.sem(f"h_w_in{i}") for i in range(2)]
        (b_in, rows_in, t_done, rT_ready, h_done, h_ready, y_done, y_ready, y_out) = map(k.sem, (
            "h_b_in", "h_rows_in", "h_t_done", "h_rT_ready", "h_h_done", "h_h_ready", "h_y_done", "h_y_ready", "h_y_out"))
        NH = FT * 2
        with nc.Block() as block:

            @block.sync
            def _(sp):
                sp.dma_start(b2[:, :, :].rearrange("p e d -> p (e d)"), row(k.ins["L1_ffn_b2"].rearrange("e d -> (e d)"))
                             ).then_inc(b_in, 16)

                def body(e, par, _):
                    sp.wait_ge(t_done, TT * e)
                    sp.dma_start(rows[:, :, :], inbox[0:EX * ROWS, :].rearrange("(e t p) d -> p e t d", e=EX, p=P)[
                        :, e, :, :]).then_inc(rows_in, 16)
                    sp.wait_ge(y_ready, TT * e)
                    sp.dma_start(w1[par][:, :, :], k.ins["L1_ffn_w1"].rearrange("e (t p) f -> p e t f", p=P)[
                        :, e, :, :]).then_inc(w_in[par], 16)
                    sp.dma_start(w2[par][:, :, :], k.ins["L1_ffn_w2"].rearrange("e (t p) d -> p e t d", p=P)[
                        :, e, :, :]).then_inc(w_in[par], 16)
                    sp.dma_start(b1[par][:, :], k.ins["L1_ffn_b1t"][:, e, :]).then_inc(w_in[par], 16)

                pairs(sp, EX, body)

            @block.gpsimd
            def _(pool):
                def body(e, par, _):
                    pool.wait_ge(y_ready, TT * e + TT)
                    pool.dma_start(outbox.rearrange("(e t p) d -> p e t d", e=EX, p=P)[:, e, :, :], y[:, :, :]
                                   ).then_inc(y_out, 16)

                pairs(pool, EX, body)
                pool.wait_ge(y_out, 16 * EX)

            @block.vector
            def _(dve):
                dve.wait_ge(b_in, 16)
                nc.vector.memset(y[:, TT - 1, :], 0.0)

                def body(e, par, _):
                    for q in range(TT):
                        dve.wait_ge(t_done, TT * e + q + 1)
                        dve.wait_ge(h_done, NH * e)
                        nc.vector.tensor_copy(rT[:, :, q, :], pT[q % 2][:, :, :]).then_inc(rT_ready, 1)
                    dve.wait_ge(y_out, 16 * e)
                    for q in range(TT):
                        dve.wait_ge(y_done, TT * e + q + 1)
                        m = P if q < TT - 1 else LT
                        nc.vector.tensor_tensor(y[0:m, q, :], pY[q % 2][0:m, :], b2[0:m, e, :], ALU.add
                                                ).then_inc(y_ready, 1)

                pairs(dve, EX, body)

            @block.scalar
            def _(act):
                act.preload_act_table(ACT.Relu)

                def body(e, par, t):
                    act.wait_ge(w_in[par], 48 * t + 48)
                    act.wait_ge(y_done, TT * e)
                    for f in range(FT):
                        for j, (lo, hi) in enumerate(SPLIT):
                            n = 2 * f + j
                            act.wait_ge(h_done, NH * e + n + 1)
                            nc.scalar.activation(hT[:, f, lo:hi], pH[n % 4][:, 0:hi - lo], ACT.Relu,
                                                 bias=b1[par][:, f:f + 1]).then_inc(h_ready, 1)

                pairs(act, EX, body)

            @block.tensor
            def _(pe):
                def body(e, par, t_):
                    pe.wait_ge(rows_in, 16 * e + 16)
                    for q in range(TT):
                        pe.wait_ge(rT_ready, TT * e + max(q - 1, 0))
                        for t in range(KD):
                            last = nc.tensor.transpose(pT[q % 2][:, t, :], rows[:, q, t * P:(t + 1) * P], k.ident[:, :])
                        last.then_inc(t_done, 1)
                    pe.wait_ge(w_in[par], 48 * t_ + 48)
                    pe.wait_ge(rT_ready, TT * e + TT)
                    rv = rT[:, :, :, :].rearrange("p t q n -> p t (q n)")
                    for f in range(FT):
                        for j, (lo, hi) in enumerate(SPLIT):
                            n = 2 * f + j
                            pe.wait_ge(h_ready, NH * e + max(n - 3, 0))
                            for t in range(KD):
                                last = nc.tensor.matmul(pH[n % 4][:, 0:hi - lo], w1[par][:, t, f * P:(f + 1) * P],
                                                        rv[:, t, lo:hi], start=(t == 0), stop=(t == KD - 1))
                            last.then_inc(h_done, 1)
                    pe.wait_ge(h_ready, NH * e + NH)
                    for q in range(TT):
                        m = P if q < TT - 1 else LT
                        pe.wait_ge(y_ready, TT * e + max(q - 1, 0))
                        for f in range(FT):
                            last = nc.tensor.matmul(pY[q % 2][0:m, :], hT[:, f, q * P:q * P + m], w2[par][:, f, :],
                                                    start=(f == 0), stop=(f == FT - 1))
                        last.then_inc(y_done, 1)

                pairs(pe, EX, body)

    with ExitStack() as c:
        PB = 7
        rest = k.sb(c, "i_rest", [P, 2, PB, D], fp32)
        odd = k.sb(c, "i_odd", [P, 2, PB, D], i32)
        zero = k.sb(c, "i_zero", [P, PB, D], fp32)
        fetched = [k.sem(f"i_fetched{i}") for i in range(NB // PB)]
        own, ready, stored = map(k.sem, ("i_own", "i_ready", "i_stored"))
        assert NB % PB == 0
        with nc.Block() as block:

            @block.gpsimd
            def _(pool):
                for b in range(NB):
                    n = P if b < NB - 1 else LAST
                    pool.indirect_dma_start(out=tok[0:n, b, :], out_offset=None, in_=outbox[:, :],
                                            in_offset=bass.IndirectOffsetOnAxis(ap=where[0:n, 1, b:b + 1], axis=0)
                                            ).then_inc(fetched[b // PB], 16)

            @block.vector
            def _(dve):
                step = Own(dve, own)
                tt, ts = nc.vector.tensor_tensor, nc.vector.tensor_scalar
                step(nc.vector.memset(zero[:, :, :], 0.0))
                for q in range(NB // PB):
                    dve.wait_ge(fetched[q], 16 * PB)
                    bs = slice(q * PB, (q + 1) * PB)
                    y = tok[:, bs, :]
                    r, o = rest[:, q % 2, :, :], odd[:, q % 2, :, :]
                    step(tt(y, y, weight[:, bs].unsqueeze(2).to_broadcast([P, PB, D]), ALU.mult))
                    step(tt(r, y, y, ALU.subtract))
                    step(ts(o, r, 0.0, None, ALU.not_equal))
                    step(ts(r, y, 10000.0, -10000.0, ALU.min, ALU.max))
                    step(nc.vector.copy_predicated(y, o, r))
                    step(tt(o, y, y, ALU.not_equal))
                    step(nc.vector.copy_predicated(y, o, zero[:, :, :]))
                    tt(x3[:, bs, :], x3[:, bs, :], y, ALU.add).then_inc(ready, 1)

            @block.sync
            def _(sp):
                whole = k.out[0:(NB - 1) * P, :].rearrange("(b p) d -> p b d", p=P)
                for q in range(NB // PB):
                    sp.wait_ge(ready, q + 1)
                    hi = min((q + 1) * PB, NB - 1)
                    sp.dma_start(whole[:, q * PB:hi, :], x3[:, q * PB:hi, :]).then_inc(stored, 16)
                sp.dma_start(k.out[(NB - 1) * P:N, :], x3[0:LAST, NB - 1, :]).then_inc(stored, 16)
                sp.wait_ge(stored, 16 * (NB // PB + 1))


def program(nc, ins, out, stages=99):
    with ExitStack() as ctx:
        k = Core(nc, ctx, ins, out)
        with ExitStack() as c:
            feat = k.sb(c, "feat", [P, NB, D], fp32)
            stage_linear(k, feat)
            stage_count(k)
            stage_sum_out(k, feat)
        if stages == 3:
            return dump(k, k.x)
        stage_slice(k)
        if stages == 4:
            return dump(k, k.x)
        with ExitStack() as c:
            feat = k.sb(c, "feat2", [P, NB, D], fp32)
            stage_norm(k, k.x, feat, k.kept)
            stage_sage(k, 1, feat, k.x, None)
            stage_sage(k, 2, k.x, feat, k.kept)
            if stages == 5:
                return dump(k, feat)
            where = k.sb(c, "where", [P, 2, NB], i32)
            weight = k.sb(c, "weight", [P, NB], fp32)
            stage_route(k, feat, k.x, where, weight)
            stage_experts(k, feat, k.x, where, weight)


def dump(k, t):
    s = k.sem("dump")
    with k.nc.Block() as block:
        @block.sync
        def _(sp):
            sp.dma_start(k.out[0:(NB - 1) * P, :].rearrange("(b p) d -> p b d", p=P), t[:, 0:NB - 1, :]).then_inc(s, 16)
            sp.dma_start(k.out[(NB - 1) * P:N, :], t[0:LAST, NB - 1, :]).then_inc(s, 16)
            sp.wait_ge(s, 32)


def kernel(**inputs):
    import numpy as _np
    import concourse.bacc as _bacc
    from concourse import mybir as _mybir
    from concourse.bass_utils import run_bass_kernel_spmd as _run

    arrays = {n: _np.asarray(v) for n, v in inputs.items()}
    arrays["L0_gnn_Wt"] = arrays.pop("L0_gnn_W").T
    arrays["L0_ffn_W_xt"] = arrays.pop("L0_ffn_W_x").T
    arrays["L0_ffn_b_xt"] = arrays.pop("L0_ffn_b_x").reshape(H, C).T
    arrays["L1_ffn_b1t"] = arrays.pop("L1_ffn_b1").reshape(EX, FF // P, P).transpose(2, 0, 1)
    arrays = {n: _np.ascontiguousarray(v) for n, v in arrays.items()}
    nc = _bacc.Bacc("TRN2", target_bir_lowering=False, num_devices=1)
    ins = {n: nc.dram_tensor("in_" + n, a.shape, _mybir.dt.from_np(a.dtype), kind="ExternalInput").ap()
           for n, a in arrays.items()}
    out = nc.dram_tensor("out_x", (N, D), fp32, kind="ExternalOutput").ap()
    program(nc, ins, out)
    r = _run(nc, [{"in_" + n: a for n, a in arrays.items()}], core_ids=[0])
    return r.results[0]["out_x"]
```

```python
from contextlib import ExitStack

import numpy as np

import concourse.bass as bass
from concourse import mybir

fp32 = mybir.dt.float32
fp32r = mybir.dt.float32r
bf16 = mybir.dt.bfloat16
i32 = mybir.dt.int32
ALU = mybir.AluOpType
ACT = mybir.ActivationFunctionType
AX = mybir.AxisListType

P = 128
N = 6250
D = 256
E = 200000
NB = -(-N // P)
LAST = N - (NB - 1) * P
KD = D // P
EPS = 1e-5

CE = 125
GC = 8
GE = CE * GC
BG = 2
BC = BG * GC
BE = CE * BC
BATCHES = E // BE
BITS = 13
assert BATCHES * BE == E and BATCHES % 2 == 0 and N < 1 << BITS
EXACT = 1 << 12

SW = 256
NSLAB = -(-N // SW)
SH = 64
COUNTS = NSLAB * P * SH * SW
SPARE = COUNTS

H, G, C = 8, 64, 64
HG = H * G

EX = 8
FF = 1024
ROWS = 1024
CAP = max(1, -(-5 * N // (4 * EX)))


class Own:

    def __init__(self, eng, sem):
        self.eng, self.sem, self.at, self.k = eng, sem, 0, 0

    def loop(self, at):
        self.at, self.k = at, 0

    def __call__(self, ins):
        self.k += 1
        ins.then_inc(self.sem, 1)
        self.eng.wait_ge(self.sem, self.at + self.k)


def ring(eng, n, body, ways=2, peel=1):
    rounds = n // ways
    for i in range(ways * peel):
        body(i, i % ways, i // ways)
    if rounds > peel + 1:
        with eng.Fori(peel, rounds - 1) as t:
            for j in range(ways):
                body(ways * t + j, j, t)
    for i in range(ways * (rounds - 1), n):
        body(i, i % ways, i // ways)


def pairs(eng, n, body):
    ring(eng, n, body)


def moments(nc, step, stats, mv, var):
    n2 = float(D)
    step(nc.vector.tensor_tensor(mv[:, 1, :], stats[:, :, 1], stats[:, :, 4], ALU.subtract))
    step(nc.vector.tensor_tensor(mv[:, 0, :], stats[:, :, 1], stats[:, :, 4], ALU.add))
    step(nc.vector.tensor_scalar(mv[:, 0, :], mv[:, 0, :], 0.5, None, ALU.mult))
    step(nc.vector.tensor_tensor(mv[:, 1, :], mv[:, 1, :], mv[:, 1, :], ALU.mult))
    step(nc.vector.tensor_tensor(var[:, :], stats[:, :, 2], stats[:, :, 5], ALU.add))
    step(nc.vector.tensor_scalar(mv[:, 1, :], mv[:, 1, :], n2 / 4, None, ALU.mult))
    step(nc.vector.tensor_tensor(var[:, :], var[:, :], mv[:, 1, :], ALU.add))
    step(nc.vector.tensor_scalar(var[:, :], var[:, :], 1 / n2, None, ALU.mult))


class Core:

    def __init__(self, nc, ctx, ins, out):
        self.nc, self.ctx, self.ins, self.out = nc, ctx, ins, out
        self.sems = []
        self.ident = self.sb(ctx, "ident", [P, P], fp32)
        self.valid = self.sb(ctx, "valid", [P, NB], fp32)
        self.eps = self.sb(ctx, "eps", [P, 1], fp32)
        self.deg = self.sb(ctx, "deg", [P, 2, NB], fp32)
        self.dinv = self.sb(ctx, "dinv", [P, NB], fp32)
        self.nought = self.sb(ctx, "nought", [P, 2], fp32)
        self.many = self.sb(ctx, "many", [1, 1], i32)
        scratch = lambda name: nc.dram_tensor(name, [NB * P, D], fp32).ap()
        self.h0, self.x1, self.x2, self.h1, self.x3 = map(scratch, ("h0", "x1", "x2", "h1", "x3"))
        self.inbox = nc.dram_tensor("inbox", [EX * ROWS + NB * P, D], fp32).ap()
        self.outbox = nc.dram_tensor("outbox", [EX * ROWS, D], fp32).ap()
        self.counts = nc.dram_tensor("counts", [COUNTS + GE, 1], fp32).ap()

    def sb(self, ctx, name, shape, dt):
        return ctx.enter_context(self.nc.sbuf_tensor(name, shape, dt))

    def ps(self, ctx, name, shape, dt=fp32):
        return ctx.enter_context(self.nc.psum_tensor(name, shape, dt))

    def sem(self, name):
        s = self.nc.alloc_semaphore(name)
        self.sems.append(s)
        return s

    def done(self):
        self.nc.clear_and_free_semaphores(self.sems)
        self.nc.all_engine_barrier()
        self.sems = []


def counts_slab(k, slab, b0, b1):
    v = k.counts[0:COUNTS, :].rearrange("(g p h w) o -> g p h (w o)", g=NSLAB, p=P, h=SH)
    return v[slab, :, b0:b1, :]


def row(vec, n=P):
    return vec.rearrange("(o n) -> o n", o=1).to_broadcast([n, vec.shape[0]])


def stage_linear(k):
    nc = k.nc
    with ExitStack() as c:
        x = k.sb(c, "a_x", [P, NB, D], fp32)
        zero = k.sb(c, "zero", [P, NB * SW], fp32)
        wt = k.sb(c, "wt", [P, KD, D], fp32)
        bias = k.sb(c, "bias", [P, D], fp32)
        stats = k.sb(c, "stats", [P, NB, 6], fp32)
        mv = k.sb(c, "mv", [P, 2, NB], fp32)
        sd = k.sb(c, "sd", [P, NB], fp32)
        rstd = k.sb(c, "rstd", [P, NB], fp32)
        xn = k.sb(c, "xn", [P, 2, D], fp32)
        xnT = k.sb(c, "xnT", [P, 2, KD, P], fp32)
        pT = [k.ps(c, f"pT{i}", [P, KD, P]) for i in range(2)]
        pH = [k.ps(c, f"pH{i}", [P, D]) for i in range(2)]
        x_zeroed, stats_made, x_in, w_in, zeros, mask_made, counts_zeroed = map(
            k.sem, ("a_x_zeroed", "a_stats_made", "a_x_in", "a_w_in", "a_zeros", "a_mask_made", "counts_zeroed"))
        var_ready, sd_ready, xn_ready, t_done, xnT_ready, h_done, h_used, h_stored, own, pown = map(
            k.sem, ("a_var", "a_sd", "a_xn", "a_t", "a_xnT", "a_h", "a_h_used", "a_h_stored", "a_own", "a_pown"))
        with nc.Block() as block:

            @block.sync
            def _(sp):
                sp.wait_ge(x_zeroed, 1)
                sp.dma_start(x[:, 0:NB - 1, :], k.ins["x"][0:(NB - 1) * P, :].rearrange(
                    "(b p) d -> p b d", p=P)).then_inc(x_in, 16)
                sp.dma_start(x[0:LAST, NB - 1, :], k.ins["x"][(NB - 1) * P:N, :]).then_inc(x_in, 16)
                sp.dma_start(wt[:, :, :], k.ins["L0_gnn_Wt"].rearrange("(t p) n -> p t n", p=P)).then_inc(w_in, 16)
                sp.dma_start(bias[:, :], row(k.ins["L0_gnn_b"])).then_inc(w_in, 16)
                sp.wait_ge(zeros, 1)
                for g in range(NSLAB):
                    sp.dma_start(counts_slab(k, g, 0, NB), zero[:, :].rearrange("p (h w) -> p h w", w=SW)
                                 ).then_inc(counts_zeroed, 16)
                sp.dma_start(k.counts[COUNTS:COUNTS + GE, :].rearrange("(p w) o -> p (w o)", p=CE),
                             zero[0:CE, 0:GC]).then_inc(counts_zeroed, 16)
                sp.dma_start(k.inbox[0:EX * ROWS, :].rearrange("(p r) d -> p (r d)", p=P)[:, 0:NB * SW], zero[:, :]
                             ).then_inc(counts_zeroed, 16)
                sp.dma_start(k.inbox[0:EX * ROWS, :].rearrange("(p r) d -> p (r d)", p=P)[:, NB * SW:EX * ROWS * D // P],
                             zero[:, 0:EX * ROWS * D // P - NB * SW]).then_inc(counts_zeroed, 16)
                sp.wait_ge(h_used, NB)
                sp.dma_start(k.h0.rearrange("(b p) d -> p b d", p=P), x[:, :, :]).then_inc(h_stored, 16)
                sp.wait_ge(counts_zeroed, 16 * (NSLAB + 3))
                sp.wait_ge(h_stored, 16)

            @block.gpsimd
            def _(pool):
                step = Own(pool, pown)
                pool.memset(x[:, NB - 1, :], 0.0).then_inc(x_zeroed, 1)
                pool.memset(k.eps[:, :], EPS)
                pool.memset(k.nought[:, :], 0.0)
                step(pool.memset(k.ident[:, :], 0.0))
                step(pool.affine_select(out=k.ident[:, :], in_=k.ident[:, :], compare_op=ALU.not_equal, fill=1.0,
                                        base=0, pattern=[[-1, P]], channel_multiplier=1))
                step(pool.memset(k.valid[:, :], 1.0))
                pool.affine_select(out=k.valid[:, NB - 1:NB], in_=k.valid[:, NB - 1:NB], compare_op=ALU.is_ge,
                                   fill=0.0, base=LAST - 1, pattern=[[0, 1]], channel_multiplier=-1
                                   ).then_inc(mask_made, 1)

            @block.vector
            def _(dve):
                step = Own(dve, own)
                nc.vector.memset(zero[:, :], 0.0).then_inc(zeros, 1)
                dve.wait_ge(x_in, 32)
                with dve.Fori(0, NB) as i:
                    nc.vector.bn_stats(stats[:, i, :], x[:, i, :]).then_inc(stats_made, 1)
                dve.wait_ge(stats_made, NB)
                moments(nc, step, stats, mv, sd)
                dve.sem_inc(var_ready, 1)
                dve.wait_ge(sd_ready, 1)
                step(nc.vector.reciprocal(rstd[:, :], sd[:, :]))

                def norm(i, par):
                    dve.wait_ge(t_done, i)
                    nc.vector.tensor_scalar(xn[:, par, :], x[:, i, :], mv[:, 0, bass.ts(i, 1)], rstd[:, bass.ts(i, 1)],
                                            ALU.subtract, ALU.mult).then_inc(xn_ready, 1)

                def add_bias(i, par):
                    dve.wait_ge(h_done, i + 1)
                    nc.vector.tensor_tensor(x[:, i, :], pH[par][:, :], bias[:, :], ALU.add).then_inc(h_used, 1)

                dve.wait_ge(w_in, 32)

                norm(0, 0)

                def body(i, par, _):
                    if not (isinstance(i, int) and i == NB - 1):
                        norm(i + 1, 1 - par)
                    add_bias(i, par)

                pairs(dve, NB, body)

            @block.scalar
            def _(act):
                act.wait_ge(var_ready, 1)
                act.wait_ge(x_zeroed, 1)
                act.wait_ge(mask_made, 1)
                nc.scalar.activation(sd[:, :], sd[:, :], ACT.Sqrt, bias=k.eps[:, 0:1]).then_inc(sd_ready, 1)

                def body(i, par, _):
                    act.wait_ge(t_done, i + 1)
                    act.wait_ge(h_used, i)
                    nc.scalar.copy(xnT[:, par, :, :], pT[par][:, :, :]).then_inc(xnT_ready, 1)

                pairs(act, NB, body)

            @block.tensor
            def _(pe):
                pe.wait_ge(w_in, 32)
                pe.wait_ge(mask_made, 1)

                def turn(i, par):
                    pe.wait_ge(xn_ready, i + 1)
                    for t in range(KD):
                        last = nc.tensor.transpose(pT[par][:, t, :], xn[:, par, t * P:(t + 1) * P], k.ident[:, :])
                    last.then_inc(t_done, 1)

                turn(0, 0)

                def body(i, par, _):
                    if not (isinstance(i, int) and i == NB - 1):
                        turn(i + 1, 1 - par)
                    pe.wait_ge(xnT_ready, i + 1)
                    pe.wait_ge(h_used, i)
                    for t in range(KD):
                        last = nc.tensor.matmul(pH[par][:, :], xnT[:, par, t, :], wt[:, t, :],
                                                start=(t == 0), stop=(t == KD - 1))
                    last.then_inc(h_done, 1)

                pairs(pe, NB, body)


def stage_count(k, limit):
    nc = k.nc
    delta = 2.0 ** -11
    assert GE * delta < 0.5
    MARK = 32
    KC = MARK + GC
    with ExitStack() as c:
        node = k.sb(c, "node", [CE, 2, 2, BC], i32)
        raw = k.sb(c, "raw", [2 * BITS, 2, BE], i32)
        bit = k.sb(c, "bit", [2 * BITS, BE], i32)
        theirs = k.sb(c, "theirs", [KC, 2, BE], bf16)
        mine = k.sb(c, "mine", [KC, 2, BE], bf16)
        shift = k.sb(c, "shift", [2 * BITS, 1], i32)
        identb = k.sb(c, "identb", [CE, CE], bf16)
        earlier = k.sb(c, "earlier", [CE, CE], bf16)
        lane = k.sb(c, "lane", [CE, P], bf16)
        spare = k.sb(c, "spare", [CE, GC], i32)
        part = k.sb(c, "part", [CE, 7, BC], i32)
        cell = k.sb(c, "cell", [CE, 2, BC], i32)
        lowi = k.sb(c, "lowi", [CE, 4, BC], i32)
        low = k.sb(c, "low", [CE, 2, 4, BC], bf16)
        hot = k.sb(c, "hot", [CE, 2, 2, GC, P], bf16)
        hoth = k.sb(c, "hoth", [CE, 2, 2, GC, NB], bf16)
        junk = k.sb(c, "junk", [CE, 3, 2, GE // 2], bf16)
        score = k.sb(c, "score", [CE, 2, GC], fp32)
        whole = k.sb(c, "whole", [CE, GC], i32)
        first = k.sb(c, "first", [CE, GC], i32)
        value = k.sb(c, "value", [CE, 2, GC], fp32)
        index = k.sb(c, "index", [CE, 2, GC], i32)
        neg = k.sb(c, "neg", [CE, 1], fp32)
        top = k.sb(c, "top", [P, 2], fp32)
        alltop = k.sb(c, "alltop", [P, 2], fp32)
        zb = k.sb(c, "zb", [CE, P], bf16)
        agree = [k.ps(c, f"agree{i}", [P, 2, 512]) for i in range(3)]
        degp = k.ps(c, "degp", [P, 512])
        edges_in = [k.sem(f"edges_in{i}") for i in range(2)]
        edges_used = [k.sem(f"edges_used{i}") for i in range(2)]
        (consts, codes_ready, hot_ready, hot_used, agree_ready, score_ready, score_used,
         slots_ready, slots_free, scattered, deg_done, deg_ready, top_ready, own, pown) = map(k.sem, (
             "b_consts", "b_codes_ready", "b_hot_ready", "b_hot_used", "b_agree_ready",
             "b_score_ready", "b_score_used", "b_slots_ready", "b_slots_free", "b_scattered",
             "b_deg_done", "b_deg_ready", "b_top_ready", "b_own", "b_pown"))
        with nc.Block() as block:

            @block.sync
            def _(sp):
                def batch(b, par, t):
                    if not isinstance(t, int) or t:
                        sp.wait_ge(edges_used[par], t)
                    for j, name in enumerate(("src", "dst")):
                        v = k.ins[name].rearrange("(b n) -> b n", n=BE)[2 * t + par, :]
                        sp.dma_start(node[:, par, j, :], v.rearrange("(p k) -> p k", k=BC)).then_inc(edges_in[par], 16)
                        sp.dma_start(raw[j * BITS:(j + 1) * BITS, par, :], row(v, BITS)).then_inc(edges_in[par], 16)

                pairs(sp, BATCHES, batch)

            @block.gpsimd
            def _(pool):
                step = Own(pool, pown)
                pool.iota(shift[:, :], [[0, 1]], base=0, channel_multiplier=1)
                pool.iota(lane[:, :], [[1, P]], base=0, channel_multiplier=0, allow_small_or_imprecise_dtypes=True)
                pool.iota(spare[:, :], [[1, GC]], base=SPARE, channel_multiplier=GC)
                pool.memset(neg[:, :], 1.0 - 2 * BITS)
                pool.memset(zb[:, :], 0.0)
                step(pool.memset(identb[:, :], 0.0))
                step(pool.affine_select(out=identb[:, :], in_=identb[:, :], compare_op=ALU.not_equal, fill=1.0,
                                        base=0, pattern=[[-1, CE]], channel_multiplier=1))
                step(pool.memset(earlier[:, :], delta))
                pool.memset(mine[:, :, :], 0.0)
                step(pool.memset(theirs[:, :, :], 0.0))
                step(pool.memset(mine[MARK:KC, :, :], delta))
                step(pool.memset(theirs[MARK:KC, :, :], 1.0))
                step(pool.affine_select(out=earlier[:, :], in_=earlier[:, :], compare_op=ALU.is_gt, fill=0.0, base=0,
                                        pattern=[[-1, CE]], channel_multiplier=1))
                for i in range(2):
                    for v, keep in ((mine, ALU.is_gt), (theirs, ALU.is_equal)):
                        of = v[MARK:KC, i, :].rearrange("r (n j) -> r n j", j=GC)
                        step(pool.affine_select(out=of, in_=of, compare_op=keep, fill=0.0, base=0,
                                                pattern=[[0, BE // GC], [1, GC]], channel_multiplier=-1))
                pool.drain().then_inc(consts, 1)

                def group(n, par, _):
                    pool.wait_ge(slots_ready, n + 1)
                    pool.wait_ge(scattered, 16 * GC * n)
                    pool.sem_inc(slots_free, 1)
                    for j in range(GC):
                        pool.indirect_dma_start(
                            out=k.counts[:, :], out_offset=bass.IndirectOffsetOnAxis(ap=index[:, par, j:j + 1], axis=0),
                            in_=value[:, par, j:j + 1], in_offset=None, compute_op=ALU.add).then_inc(scattered, 16)

                pairs(pool, BATCHES * BG, group)
                pool.wait_ge(scattered, 16 * GC * BATCHES * BG)
                pool.wait_ge(deg_ready, 1)
                pool.partition_all_reduce(alltop[:, :], top[:, :], P, bass.bass_isa.ReduceOp.max).then_inc(top_ready, 1)

            @block.vector
            def _(dve):
                step = Own(dve, own)
                PER = 4 + 4 * BG
                dve.wait_ge(consts, 1)
                step(nc.vector.tensor_scalar(bit[:, 0:1], shift[:, :], float(BITS), float(BITS), ALU.is_ge, ALU.mult))
                step(nc.vector.tensor_tensor(shift[:, :], shift[:, :], bit[:, 0:1], ALU.subtract))
                tt = nc.vector.tensor_tensor
                ts = nc.vector.tensor_scalar

                def prepare(t, par, before):
                    dve.wait_ge(edges_in[par], 64 * t + 64)
                    step(ts(bit[:, :], raw[:, par, :], shift[:, 0:1], 1, ALU.logical_shift_right, ALU.bitwise_and))
                    dve.wait_ge(hot_used, BG * before)
                    ts(mine[0:2 * BITS, par, :], bit[:, :], 2.0, -1.0, ALU.mult, ALU.add).then_inc(codes_ready, 1)
                    ts(theirs[0:2 * BITS, par, :], bit[:, :], 2.0, -1.0, ALU.mult, ALU.add).then_inc(codes_ready, 1)
                    src, dst = node[:, par, 0, :], node[:, par, 1, :]
                    ts(part[:, 0, :], dst, 8, 21, ALU.logical_shift_right, ALU.logical_shift_left)
                    ts(part[:, 1, :], dst, SW - 1, None, ALU.bitwise_and)
                    ts(part[:, 2, :], src, P - 1, 14, ALU.bitwise_and, ALU.logical_shift_left)
                    ts(part[:, 3, :], src, 7, 8, ALU.logical_shift_right, ALU.logical_shift_left)
                    ts(lowi[:, 0, :], src, P - 1, None, ALU.bitwise_and)
                    ts(lowi[:, 1, :], dst, P - 1, None, ALU.bitwise_and)
                    ts(lowi[:, 2, :], src, 7, None, ALU.logical_shift_right)
                    step(ts(lowi[:, 3, :], dst, 7, None, ALU.logical_shift_right))
                    dve.sem_inc(edges_used[par], 1)
                    tt(part[:, 4, :], part[:, 0, :], part[:, 1, :], ALU.bitwise_or)
                    nc.vector.tensor_copy(low[:, par, :, :], lowi[:, :, :])
                    step(tt(part[:, 5, :], part[:, 2, :], part[:, 3, :], ALU.bitwise_or))
                    step(tt(cell[:, par, :], part[:, 4, :], part[:, 5, :], ALU.bitwise_or))

                def groups(b, par):
                    for g in range(BG):
                        n = BG * b + g
                        gp = g % 2
                        js = slice(g * GC, (g + 1) * GC)
                        dve.wait_ge(hot_used, n)
                        tt(hot[:, gp, :, :, :],
                           lane[:, :].rearrange("p (a b l) -> p a b l", a=1, b=1).to_broadcast([CE, 2, GC, P]),
                           low[:, par, 0:2, js].unsqueeze(3).to_broadcast([CE, 2, GC, P]), ALU.is_equal)
                        tt(hoth[:, gp, :, :, :],
                           lane[:, 0:NB].rearrange("p (a b l) -> p a b l", a=1, b=1).to_broadcast([CE, 2, GC, NB]),
                           low[:, par, 2:4, js].unsqueeze(3).to_broadcast([CE, 2, GC, NB]), ALU.is_equal
                           ).then_inc(hot_ready, 1)
                        dve.wait_ge(score_ready, GC * n + GC + 2)
                        dve.wait_ge(slots_free, n)
                        step(nc.vector.tensor_copy(whole[:, :], score[:, gp, :]))
                        step(tt(first[:, :], score[:, gp, :], whole[:, :], ALU.is_equal))
                        nc.vector.tensor_copy(index[:, gp, :], spare[:, :])
                        step(tt(value[:, gp, :], score[:, gp, :], first[:, :], ALU.mult))
                        dve.sem_inc(score_used, 1)
                        step(nc.vector.copy_predicated(index[:, gp, :], first[:, :], cell[:, par, js]))
                        dve.sem_inc(slots_ready, 1)

                prepare(0, 0, 0)
                first_step = step.k

                def both(t, more):
                    step.loop(first_step + 2 * PER * t)
                    prepare(t, 1, 2 * t)
                    groups(2 * t, 0)
                    if more:
                        prepare(t + 1, 0, 2 * t + 1)
                    groups(2 * t + 1, 1)

                both(0, True)
                with dve.Fori(1, BATCHES // 2 - 1) as t:
                    both(t, True)
                both(BATCHES // 2 - 1, False)
                dve.wait_ge(deg_done, 1)
                step(nc.vector.tensor_copy(k.deg[:, :, :], degp[:, 0:2 * NB].rearrange("p (s b) -> p s b", s=2)))
                step(nc.vector.tensor_reduce(top[:, :], k.deg[:, :, :], axis=AX.X, op=ALU.max))
                dve.sem_inc(deg_ready, 1)
                dve.wait_ge(top_ready, 1)
                step(tt(top[0:1, 0:1], alltop[0:1, 0:1], alltop[0:1, 1:2], ALU.min))
                ts(k.many[:, :], top[0:1, 0:1], float(limit), None, ALU.is_gt)

            @block.scalar
            def _(act):
                act.wait_ge(consts, 1)
                act.preload_act_table(ACT.Relu)
                act.sem_inc(score_ready, 2)

                def group(n, par, _):
                    act.wait_ge(score_used, n)
                    for j in range(GC):
                        act.wait_ge(agree_ready, GC * n + j + 1)
                        nc.scalar.activation(junk[:, j % 3, :, :], agree[j % 3][0:CE, :, 0:GE // 2], ACT.Relu,
                                             bias=neg[:, 0:1], accum_out=score[:, par, j:j + 1]
                                             ).then_inc(score_ready, 1)

                pairs(act, BATCHES * BG, group)

            @block.tensor
            def _(pe):
                pe.wait_ge(consts, 1)
                nc.tensor.matmul(degp[:, 0:2 * NB], zb[:, :], zb[:, 0:2 * NB], start=True, stop=False,
                                 skip_group_check=True)

                def batch(b, par, t):
                    pe.wait_ge(codes_ready, 2 * b + 2)
                    by_chunk = [v[:, par, :].rearrange("b (p k) -> b k p", k=BC) for v in (mine, theirs)]
                    for g in range(BG):
                        n = BG * b + g
                        for j in range(GC):
                            pe.wait_ge(score_ready, GC * n + j + (1 if j < 2 else 0))
                            me = by_chunk[0][:, g * GC + j, :]
                            for h in range(2):
                                half = g * GC + h * GC // 2
                                holds = j // (GC // 2) == h
                                o = agree[j % 3][0:CE, h, 0:GE // 2]
                                last = nc.tensor.matmul(o, me, by_chunk[1][:, half:half + GC // 2, :],
                                                        start=True, stop=not holds)
                                if holds:
                                    at = j % (GC // 2) * CE
                                    last = nc.tensor.matmul(o[:, at:at + CE], identb[:, :], earlier[:, :],
                                                            start=False, stop=True)
                            last.then_inc(agree_ready, 1)
                        pe.wait_ge(hot_ready, n + 1)
                        for s in range(2):
                            for j in range(GC):
                                last = nc.tensor.matmul(degp[:, s * NB:(s + 1) * NB], hot[:, g % 2, s, j, :],
                                                        hoth[:, g % 2, s, j, :], start=False, stop=False,
                                                        skip_group_check=True)
                        last.then_inc(hot_used, 1)

                pairs(pe, BATCHES, batch)
                nc.tensor.matmul(degp[:, 0:2 * NB], zb[:, :], zb[:, 0:2 * NB], start=False, stop=True,
                                 skip_group_check=True).then_inc(deg_done, 1)


def stage_split(k, tag, source, hi, lo, scale):
    nc = k.nc
    PB = 7
    assert NB % PB == 0
    parts = NB // PB
    with ExitStack() as c:
        buf = k.sb(c, f"{tag}_buf", [P, 2, PB, D], fp32)
        stats = k.sb(c, f"{tag}_stats", [P, PB, 6], fp32)
        mv = k.sb(c, f"{tag}_mv", [P, 2, PB], fp32)
        sd = k.sb(c, f"{tag}_sd", [P, PB], fp32)
        rstd = k.sb(c, f"{tag}_rstd", [P, PB], fp32)
        loaded = [k.sem(f"{tag}_loaded{i}") for i in range(2)]
        deg1, used, var_ready, sd_ready, scaled, hi_ready, own = (k.sem(f"{tag}_{m}") for m in (
            "deg1", "used", "var_ready", "sd_ready", "scaled", "hi_ready", "own"))
        with nc.Block() as block:

            @block.sync
            def _(sp):
                def body(q, par, t):
                    if not isinstance(q, int) or q >= 2:
                        sp.wait_ge(used, q - 1)
                    sp.dma_start(buf[:, par, :, :], source.rearrange("(b p) d -> p b d", p=P)[
                        :, bass.ts(q, PB), :]).then_inc(loaded[par], 16)

                pairs(sp, parts, body)

            @block.vector
            def _(dve):
                step = Own(dve, own)
                tt, ts = nc.vector.tensor_tensor, nc.vector.tensor_scalar
                if scale == "degree":
                    step(ts(k.dinv[:, :], k.deg[:, 0, :], 1.0, None, ALU.add))
                    dve.sem_inc(deg1, 1)
                    dve.wait_ge(sd_ready, 1)
                    step(nc.vector.reciprocal(k.dinv[:, :], k.dinv[:, :]))
                before = step.k
                per = 9 if scale == "norm" else 0

                def prepare(q, par, t):
                    dve.wait_ge(loaded[par], 16 * t + 16)
                    b = buf[:, par, :, :]
                    if scale == "norm":
                        step.loop(before + (per + PB) * q)
                        for j in range(PB):
                            step(nc.vector.bn_stats(stats[:, j, :], b[:, j, :]))
                        moments(nc, step, stats, mv, sd)
                        dve.sem_inc(var_ready, 1)
                        dve.wait_ge(sd_ready, q + 1)
                        step(nc.vector.reciprocal(rstd[:, :], sd[:, :]))
                        for j in range(PB):
                            last = ts(b[:, j, :], b[:, j, :], mv[:, 0, j:j + 1], rstd[:, j:j + 1], ALU.subtract, ALU.mult)
                        last.then_inc(scaled, 1)
                    elif scale == "degree":
                        tt(b, b, k.dinv[:, bass.ts(q, PB)].unsqueeze(2).to_broadcast([P, PB, D]), ALU.mult
                           ).then_inc(scaled, 1)
                    else:
                        dve.sem_inc(scaled, 1)

                prepare(0, 0, 0)

                def body(q, par, t):
                    if not (isinstance(q, int) and q == parts - 1):
                        prepare(q + 1, 1 - par, t if par == 0 else t + 1)
                    dve.wait_ge(hi_ready, q + 1)
                    tt(lo[:, bass.ts(q, PB), :], buf[:, par, :, :], hi[:, bass.ts(q, PB), :].bitcast(fp32),
                       ALU.subtract).then_inc(used, 1)

                pairs(dve, parts, body)

            @block.scalar
            def _(act):
                if scale == "degree":
                    act.wait_ge(deg1, 1)
                    nc.scalar.activation(k.dinv[:, :], k.dinv[:, :], ACT.Sqrt).then_inc(sd_ready, 1)
                if scale == "norm":
                    act.preload_act_table(ACT.Sqrt)

                def body(q, par, t):
                    if scale == "norm":
                        act.wait_ge(var_ready, q + 1)
                        nc.scalar.activation(sd[:, :], sd[:, :], ACT.Sqrt, bias=k.eps[:, 0:1]).then_inc(sd_ready, 1)
                    act.wait_ge(scaled, q + 1)
                    if scale is None:
                        act.wait_ge(loaded[par], 16 * t + 16)
                    nc.scalar.copy(hi[:, bass.ts(q, PB), :], buf[:, par, :, :]).then_inc(hi_ready, 1)

                pairs(act, parts, body)


def stage_sum_out(k, hi, lo):
    nc = k.nc
    Q = 4
    groups = [list(range(q, min(q + Q, NB))) for q in range(0, NB, Q)]
    NQ = len(groups)
    EVEN, ODD = (NQ + 1) // 2, NQ // 2
    with ExitStack() as c:
        rows = [k.sb(c, f"rows{i}", [P, NSLAB, SW], fp32) for i in range(2)]
        turned = [k.sb(c, f"turned{i}", [P, Q, P], fp32r) for i in range(Q)]
        turned_lo = [k.sb(c, f"turned_lo{i}", [P, Q, P], fp32r) for i in range(Q)]
        old = k.sb(c, "c_old", [P, 2, D], fp32)
        new = k.sb(c, "c_new", [P, 2, D], fp32)
        pT = [k.ps(c, f"cT{i}", [P, Q, P]) for i in range(Q)]
        pS = [k.ps(c, f"cS{i}", [P, D]) for i in range(2)]
        rows_in = [k.sem(f"c_rows_in{i}") for i in range(2)]
        old_in = [k.sem(f"c_old_in{i}") for i in range(2)]
        new_out = [k.sem(f"c_new_out{i}") for i in range(2)]
        t_done, act_out, dve_out, lo_out, mm_done, sum_used, new_ready, own = map(k.sem, (
            "c_t_done", "c_act_out", "c_dve_out", "c_lo_out", "c_mm_done", "c_sum_used", "c_new_ready", "c_own"))
        by_block = k.counts[0:COUNTS, :].rearrange("(g p h w) o -> p h g (w o)", g=NSLAB, p=P, h=SH)
        x_rows = k.ins["x"]
        with nc.Block() as block:

            @block.sync
            def _(sp):
                def body(i, par, _):
                    if not isinstance(i, int) or i >= 2:
                        sp.wait_ge(t_done, NQ * (i - 1))
                    sp.dma_start(rows[par][:, :, :], by_block[:, i, :, :]).then_inc(rows_in[par], 16)

                pairs(sp, NB, body)

            @block.gpsimd
            def _(pool):
                def load(i, par):
                    if isinstance(i, int) and i == NB - 1:
                        pool.dma_start(old[0:LAST, par, :], x_rows[i * P:N, :]).then_inc(old_in[par], 16)
                    else:
                        pool.dma_start(old[:, par, :], x_rows[bass.ts(i, P), :]).then_inc(old_in[par], 16)

                load(0, 0)
                load(1, 1)

                def body(i, par, _):
                    pool.wait_ge(new_ready, i + 1)
                    pool.dma_start(k.x1[bass.ts(i, P), :], new[:, par, :]).then_inc(new_out[par], 16)
                    if not (isinstance(i, int) and i >= NB - 2):
                        load(i + 2, par)

                pairs(pool, NB, body)
                pool.wait_ge(new_out[0], 16 * ((NB + 1) // 2))
                pool.wait_ge(new_out[1], 16 * (NB // 2))

            @block.vector
            def _(dve):
                step = Own(dve, own)
                tt = nc.vector.tensor_tensor
                many = dve.value_load(k.many[0:1, 0:1], min_val=0, max_val=1)

                def finish(i, par, t):
                    dve.wait_ge(mm_done, NQ * i + NQ)
                    dve.wait_ge(new_out[par], 16 * t)
                    n = new[:, par, :]
                    step(tt(n, pS[par][:, :], hi[:, i, :].bitcast(fp32), ALU.add))
                    dve.sem_inc(sum_used, 1)
                    step(tt(n, n, lo[:, i, :].bitcast(fp32), ALU.add))
                    dve.wait_ge(old_in[par], 16 * t + 16)
                    last = nc.vector.scalar_tensor_tensor(n, n, k.dinv[:, bass.ts(i, 1)], old[:, par, :], ALU.mult, ALU.add)
                    if isinstance(i, int) and i == NB - 1:
                        step(last)
                        last = nc.vector.tensor_scalar(n, n, k.valid[:, i:i + 1], None, ALU.mult)
                    last.then_inc(new_ready, 1)

                def body(i, par, t):
                    step.loop(2 * i)
                    for q in range(NQ):
                        m = len(groups[q])
                        hi_part, bank = turned[q % Q][:, 0:m, :], pT[q % Q][:, 0:m, :]
                        if q % 2:
                            dve.wait_ge(t_done, NQ * i + q + 1)
                            if q >= Q:
                                dve.wait_ge(mm_done, NQ * i + q - Q + 1)
                            else:
                                dve.wait_ge(mm_done, NQ * i)
                            nc.vector.tensor_copy(hi_part, bank).then_inc(dve_out, 1)
                        with dve.If(many > 0):
                            dve.wait_ge(act_out, EVEN * i + (q + 2) // 2)
                            dve.wait_ge(dve_out, ODD * i + (q + 1) // 2)
                            dve.wait_ge(mm_done, NQ * i + max(q - Q + 1, 0))
                            tt(turned_lo[q % Q][:, 0:m, :], bank, hi_part.bitcast(fp32), ALU.subtract).then_inc(lo_out, 1)
                    finish(i, par, t)

                pairs(dve, NB, body)

            @block.scalar
            def _(act):
                def body(i, par, _):
                    for q in range(0, NQ, 2):
                        act.wait_ge(t_done, NQ * i + q + 1)
                        act.wait_ge(mm_done, NQ * i + max(q - Q + 1, 0))
                        nc.scalar.copy(turned[q % Q][:, 0:len(groups[q]), :],
                                       pT[q % Q][:, 0:len(groups[q]), :]).then_inc(act_out, 1)

                pairs(act, NB, body)

            @block.tensor
            def _(pe):
                many = pe.value_load(k.many[0:1, 0:1], min_val=0, max_val=1)
                pe.sem_inc(sum_used, 1)

                def copied(i, q):
                    if q < 0 and isinstance(i, int) and i == 0:
                        return
                    if q % 2:
                        pe.wait_ge(dve_out, ODD * i + max((q + 1) // 2, 0))
                    else:
                        pe.wait_ge(act_out, EVEN * i + max(q // 2 + 1, 0))
                    with pe.If(many > 0):
                        pe.wait_ge(lo_out, NQ * i + max(q + 1, 0))

                def turn(i, par, q):
                    copied(i, q - Q)
                    for n, b in enumerate(groups[q]):
                        last = nc.tensor.transpose(pT[q % Q][:, n, :], rows[par][:, b // 2, (b % 2) * P:(b % 2 + 1) * P],
                                                   k.ident[:, :])
                    last.then_inc(t_done, 1)

                def add(par, tile, q, stop):
                    for n, b in enumerate(groups[q]):
                        for part in (hi, lo):
                            last = nc.tensor.matmul(pS[par][:, :], tile[:, n, :], part[:, b, :],
                                                    start=(b == 0 and part is hi and tile is turned[q % Q]),
                                                    stop=(stop and b == NB - 1 and part is lo), skip_group_check=True)
                    return last

                def body(i, par, t):
                    pe.wait_ge(rows_in[par], 16 * t + 16)
                    turn(i, par, 0)
                    turn(i, par, 1)
                    pe.wait_ge(sum_used, i)
                    for q in range(NQ):
                        if q + 2 < NQ:
                            turn(i, par, q + 2)
                        copied(i, q)
                        add(par, turned[q % Q], q, False)
                        with pe.If(many > 0):
                            add(par, turned_lo[q % Q], q, False)
                        nc.tensor.matmul(pS[par][0:2, 0:2], k.nought[:, 0:2], k.nought[:, 0:2], start=False,
                                         stop=(q == NQ - 1), skip_group_check=True).then_inc(mm_done, 1)

                pairs(pe, NB, body)


def stage_slice(k):
    nc = k.nc
    PT = HG // P
    with ExitStack() as c:
        x = k.sb(c, "d_x", [P, NB, D], fp32)
        wT = k.sb(c, "d_wT", [P, NB, PT, P], fp32)
        stats = k.sb(c, "d_stats", [P, NB, 6], fp32)
        mv = k.sb(c, "d_mv", [P, 2, NB], fp32)
        sd = k.sb(c, "d_sd", [P, NB], fp32)
        rstd = k.sb(c, "d_rstd", [P, NB], fp32)
        ow = k.sb(c, "d_ow", [P, PT, D], fp32)
        bout = k.sb(c, "d_bout", [P, D], fp32)
        wfx = k.sb(c, "d_wfx", [P, KD, HG], fp32)
        bfx = k.sb(c, "d_bfx", [1, HG], fp32)
        wq, wk, wv = (k.sb(c, f"d_w{n}", [C, C], fp32) for n in "qkv")
        wout = k.sb(c, "d_wout", [C, H, D], fp32)
        sums = k.sb(c, "d_sums", [P, PT, D + 1], fp32)
        stats_made, var_ready, sd_ready, own, w_in, sums_ready, ow_ready = map(
            k.sem, ("d_stats_made", "d_var", "d_sd", "d_own", "d_w_in", "d_sums_ready", "d_ow_ready"))
        NW = 8

        with ExitStack() as c1:
            wxT = k.sb(c1, "d_wxT", [C, H, D], fp32)
            wsl = k.sb(c1, "d_wsl", [C, G], fp32)
            bx = k.sb(c1, "d_bx", [C, H], fp32)
            bsl = k.sb(c1, "d_bsl", [P, G], fp32)
            temp = k.sb(c1, "d_temp", [P, H], fp32)
            wc = k.sb(c1, "d_wc", [P, KD, HG], fp32)
            bc = k.sb(c1, "d_bc", [P, H, G], fp32)
            xa = k.sb(c1, "d_xa", [P, 4, D + 1], fp32)
            xnT = k.sb(c1, "d_xnT", [P, 2, KD, P], fp32)
            lg = k.sb(c1, "d_lg", [P, 2, H, G], fp32)
            bxw = lg[0:C, :, :, :].rearrange("p a h g -> p (a h g)").rearrange("p (h n) -> p h n", n=P)
            ex = k.sb(c1, "d_ex", [P, 2, H, G], fp32)
            sw = k.sb(c1, "d_sw", [P, 2, HG], fp32)
            mx = k.sb(c1, "d_mx", [P, 2, H], fp32)
            es = k.sb(c1, "d_es", [P, 2, H], fp32)
            rs = k.sb(c1, "d_rs", [P, 2, H], fp32)
            pS = [k.ps(c1, f"dS{i}", [P, D + 1]) for i in range(PT)]
            pT = k.ps(c1, "dT", [P, KD, P])
            pL = [k.ps(c1, f"dL{i}", [P, HG]) for i in range(2)]
            pW = k.ps(c1, "dW", [P, PT, P])
            (wc_ready, w_scaled, bxw_ready, xn_ready, t_done, xnT_ready, l_ready, l_shifted, e_ready, sums_done, sw_ready, st_done,
             w_done, w_stored, c_in, x_in) = map(k.sem, (
                 "d_wc_ready", "d_w_scaled", "d_bxw_ready", "d_xn_ready", "d_t_done", "d_xnT_ready", "d_l_ready",
                 "d_l_shifted", "d_e_ready", "d_sums_done", "d_sw_ready", "d_st_done", "d_w_done", "d_w_stored", "d_c_in", "d_x_in"))
            with nc.Block() as block:

                @block.sync
                def _(sp):
                    sp.dma_start(x[:, :, :], k.x1.rearrange("(b p) d -> p b d", p=P)).then_inc(x_in, 16)
                    ld = lambda o, i: sp.dma_start(o, i).then_inc(c_in, 16)
                    ld(wxT[:, :, :], k.ins["L0_ffn_W_xt"].rearrange("(h c) f -> c h f", c=C))
                    ld(wsl[:, :], k.ins["L0_ffn_W_slice"])
                    ld(bx[:, :], k.ins["L0_ffn_b_xt"])
                    ld(bsl[:, :], row(k.ins["L0_ffn_b_slice"]))
                    ld(temp[:, :], k.ins["L0_ffn_temperature"].rearrange("a h b c -> a (h b c)").to_broadcast([P, H]))
                    sp.wait_ge(c_in, 16 * 5)
                    ld = lambda o, i: sp.dma_start(o, i).then_inc(w_in, 16)
                    ld(wfx[:, :, :], k.ins["L0_ffn_W_fx"].rearrange("(t p) n -> p t n", p=P))
                    ld(bfx[:, :], row(k.ins["L0_ffn_b_fx"], 1))
                    ld(wq[:, :], k.ins["L0_ffn_W_q"])
                    ld(wk[:, :], k.ins["L0_ffn_W_k"])
                    ld(wv[:, :], k.ins["L0_ffn_W_v"])
                    ld(wout[:, :, :], k.ins["L0_ffn_W_out"].rearrange("(h c) n -> c h n", c=C))
                    ld(bout[:, :], row(k.ins["L0_ffn_b_out"]))
                    sp.wait_ge(w_in, 16 * 7)

                @block.vector
                def _(dve):
                    step = Own(dve, own)
                    tt, ts = nc.vector.tensor_tensor, nc.vector.tensor_scalar
                    dve.wait_ge(c_in, 16 * 5)
                    nc.vector.tensor_copy(bxw[:, :, :], bx[:, :].unsqueeze(2).to_broadcast([C, H, P])
                                          ).then_inc(bxw_ready, 1)
                    step(ts(temp[:, :], temp[:, :], 0.1, 5.0, ALU.max, ALU.min))
                    step(nc.vector.reciprocal(temp[:, :], temp[:, :]))
                    dve.wait_ge(wc_ready, 1)
                    rt = temp[:, :].unsqueeze(2).to_broadcast([P, H, G])
                    for t in range(KD):
                        tt(wc[:, t, :].rearrange("p (h g) -> p h g", h=H), pL[t][:, :].rearrange("p (h g) -> p h g", h=H),
                           rt, ALU.mult)
                    step(tt(bc[:, :, :], pW[:, :, :].rearrange("p a b -> p (a b)").rearrange("p (h g) -> p h g", h=H),
                            bsl[:, :].unsqueeze(1).to_broadcast([P, H, G]), ALU.add))
                    step(tt(bc[:, :, :], bc[:, :, :], rt, ALU.mult))
                    dve.sem_inc(w_scaled, 1)
                    dve.wait_ge(x_in, 16)
                    with dve.Fori(0, NB) as i:
                        nc.vector.bn_stats(stats[:, i, :], x[:, i, :]).then_inc(stats_made, 1)
                    dve.wait_ge(stats_made, NB)
                    moments(nc, step, stats, mv, sd)
                    dve.sem_inc(var_ready, 1)
                    dve.wait_ge(sd_ready, 1)
                    step(nc.vector.reciprocal(rstd[:, :], sd[:, :]))

                    def norm(i, w):
                        if not isinstance(i, int) or i >= 4:
                            dve.wait_ge(st_done, i - 3)
                        ts(xa[:, w, 0:D], x[:, i, :], mv[:, 0, bass.ts(i, 1)], rstd[:, bass.ts(i, 1)],
                           ALU.subtract, ALU.mult)
                        nc.vector.tensor_copy(xa[:, w, D:D + 1], k.valid[:, bass.ts(i, 1)]).then_inc(xn_ready, 1)

                    def shift(i, par):
                        dve.wait_ge(l_ready, i + 1)
                        if not isinstance(i, int) or i >= 2:
                            dve.wait_ge(e_ready, i - 1)
                        l = lg[:, par, :, :]
                        step(tt(l, pL[par][:, :].rearrange("p (h g) -> p h g", h=H), bc[:, :, :], ALU.add))
                        step(nc.vector.tensor_reduce(mx[:, par, :], l, axis=AX.X, op=ALU.max))
                        tt(l, l, mx[:, par, :].unsqueeze(2).to_broadcast([P, H, G]), ALU.subtract).then_inc(l_shifted, 1)

                    def total(i, par):
                        dve.wait_ge(e_ready, i + 1)
                        step(nc.vector.tensor_reduce(es[:, par, :], ex[:, par, :, :], axis=AX.X, op=ALU.add))
                        if not isinstance(i, int) or i >= 2:
                            dve.wait_ge(sw_ready, i - 1)
                        nc.vector.reciprocal(rs[:, par, :], es[:, par, :]).then_inc(sums_done, 1)

                    norm(0, 0)
                    norm(1, 1)
                    norm(2, 2)
                    shift(0, 0)
                    before = step.k

                    def body(i, w, _):
                        step.loop(before + 3 * i)
                        if not (isinstance(i, int) and i >= NB - 3):
                            norm(i + 3, (w + 3) % 4)
                        if not (isinstance(i, int) and i >= NB - 1):
                            shift(i + 1, (w + 1) % 2)
                        total(i, w % 2)

                    ring(dve, NB, body, 4)
                    dve.wait_ge(st_done, NB)
                    for j in range(PT):
                        nc.vector.tensor_copy(sums[:, j, :], pS[j][:, :])

                @block.scalar
                def _(act):
                    act.wait_ge(var_ready, 1)
                    nc.scalar.activation(sd[:, :], sd[:, :], ACT.Sqrt, bias=k.eps[:, 0:1]).then_inc(sd_ready, 1)
                    act.preload_act_table(ACT.Exp)

                    def turn(i, par):
                        act.wait_ge(t_done, i + 1)
                        if not isinstance(i, int) or i >= 2:
                            act.wait_ge(l_ready, i - 1)
                        nc.scalar.copy(xnT[:, par, :, :], pT[:, :, :]).then_inc(xnT_ready, 1)

                    def exps(i, par):
                        act.wait_ge(l_shifted, i + 1)
                        if not isinstance(i, int) or i >= 2:
                            act.wait_ge(sw_ready, i - 1)
                        nc.scalar.activation(ex[:, par, :, :], lg[:, par, :, :], ACT.Exp).then_inc(e_ready, 1)

                    def store(i):
                        act.wait_ge(w_done, i + 1)
                        nc.scalar.copy(wT[:, i, :, :], pW[:, :, :]).then_inc(w_stored, 1)

                    turn(0, 0)
                    turn(1, 1)
                    exps(0, 0)

                    def body(i, par, _):
                        if not (isinstance(i, int) and i >= NB - 2):
                            turn(i + 2, par)
                        if not (isinstance(i, int) and i >= NB - 1):
                            exps(i + 1, 1 - par)
                        store(i)

                    pairs(act, NB, body)

                @block.gpsimd
                def _(pool):
                    def body(i, par, _):
                        pool.wait_ge(sums_done, i + 1)
                        if not isinstance(i, int) or i >= 2:
                            pool.wait_ge(w_done, i - 1)
                        nc.gpsimd.tensor_tensor(sw[:, par, :].rearrange("p (h g) -> p h g", h=H), ex[:, par, :, :],
                                                rs[:, par, :].unsqueeze(2).to_broadcast([P, H, G]), ALU.mult
                                                ).then_inc(sw_ready, 1)

                    pairs(pool, NB, body)

                @block.tensor
                def _(pe):
                    pe.wait_ge(bxw_ready, 1)
                    for h in range(H):
                        hs = slice(h * G, (h + 1) * G)
                        for t in range(KD):
                            nc.tensor.matmul(pL[t][:, hs], wxT[:, h, t * P:(t + 1) * P], wsl[:, :], start=True, stop=True)
                        last = nc.tensor.matmul(pW[:, :, :].rearrange("p a b -> p (a b)")[:, hs], bxw[:, h, :], wsl[:, :],
                                                start=True, stop=True)
                    last.then_inc(wc_ready, 1)
                    pe.wait_ge(w_scaled, 1)

                    def front(i, w):
                        par = w % 2
                        pe.wait_ge(xn_ready, i + 1)
                        pe.wait_ge(xnT_ready, i)
                        for t in range(KD):
                            last = nc.tensor.transpose(pT[:, t, :], xa[:, w, t * P:(t + 1) * P], k.ident[:, :])
                        last.then_inc(t_done, 1)
                        pe.wait_ge(xnT_ready, i + 1)
                        if not isinstance(i, int) or i >= 2:
                            pe.wait_ge(l_shifted, i - 1)
                        for t in range(KD):
                            last = nc.tensor.matmul(pL[par][:, :], xnT[:, par, t, :], wc[:, t, :],
                                                    start=(t == 0), stop=(t == KD - 1))
                        last.then_inc(l_ready, 1)

                    def back(i, w):
                        par = w % 2
                        pe.wait_ge(sw_ready, i + 1)
                        pe.wait_ge(w_stored, i)
                        for j in range(PT):
                            last = nc.tensor.matmul(pS[j][:, :], sw[:, par, j * P:(j + 1) * P], xa[:, w, :],
                                                    start=(isinstance(i, int) and i == 0),
                                                    stop=(isinstance(i, int) and i == NB - 1), skip_group_check=True)
                        last.then_inc(st_done, 1)
                        for j in range(PT):
                            last = nc.tensor.transpose(pW[:, j, :], sw[:, par, j * P:(j + 1) * P], k.ident[:, :])
                        last.then_inc(w_done, 1)

                    front(0, 0)
                    front(1, 1)

                    def body(i, w, _):
                        if not (isinstance(i, int) and i >= NB - 2):
                            front(i + 2, (w + 2) % 4)
                        back(i, w)

                    ring(pe, NB, body, 4)

        with ExitStack() as c2:
            tokT = k.sb(c2, "d_tokT", [C, HG], fp32)
            qT = k.sb(c2, "d_qT", [C, HG], fp32)
            kT = k.sb(c2, "d_kT", [C, HG], fp32)
            vv = k.sb(c2, "d_vv", [G, HG], fp32)
            att = k.sb(c2, "d_att", [G, H, G], fp32)
            attT = k.sb(c2, "d_attT", [G, HG], fp32)
            oT = k.sb(c2, "d_oT", [C, HG], fp32)
            sT = k.sb(c2, "d_sT", [P, KD, HG], fp32)
            nT = k.sb(c2, "d_nT", [1, HG], fp32)
            mx = k.sb(c2, "d_amx", [G, H], fp32)
            rn = k.sb(c2, "d_rn", [P, PT], fp32)
            pp = [k.ps(c2, f"dP{i}", [P, 512]) for i in range(8)]
            pe_done, other_done, vown = map(k.sem, ("d_pe_done", "d_other_done", "d_vown"))
            with nc.Block() as block:

                @block.vector
                def _(dve):
                    step = Own(dve, vown)
                    tt, ts = nc.vector.tensor_tensor, nc.vector.tensor_scalar

                    def after_pe(n):
                        dve.wait_ge(pe_done, n)

                    step(ts(rn[:, :], sums[:, :, D], 1e-5, None, ALU.add))
                    step(nc.vector.reciprocal(rn[:, :], rn[:, :]))
                    step(tt(sums[:, :, :], sums[:, :, :], rn[:, :].unsqueeze(2).to_broadcast([P, PT, D + 1]), ALU.mult))
                    dve.sem_inc(other_done, 1)
                    after_pe(1)
                    for t in range(KD):
                        nc.vector.tensor_copy(sT[:, t, :], pp[t][:, :])
                    step(nc.vector.tensor_copy(nT[:, :], pp[2][0:1, :]))
                    dve.sem_inc(other_done, 1)
                    after_pe(2)
                    step(nc.vector.tensor_copy(tokT[:, :], pp[3][0:C, :]))
                    dve.sem_inc(other_done, 1)
                    after_pe(3)
                    nc.vector.tensor_copy(qT[:, :], pp[4][0:C, :])
                    nc.vector.tensor_copy(kT[:, :], pp[5][0:C, :])
                    step(nc.vector.tensor_copy(vv[:, :], pp[6][0:G, :]))
                    dve.sem_inc(other_done, 1)
                    after_pe(4)
                    s3 = pp[7][0:G, :].rearrange("p (h g) -> p h g", h=H)
                    step(nc.vector.tensor_reduce(mx[:, :], s3, axis=AX.X, op=ALU.max))
                    step(tt(att[:, :, :], s3, mx[:, :].unsqueeze(2).to_broadcast([G, H, G]), ALU.subtract))
                    dve.sem_inc(other_done, 1)
                    dve.wait_ge(other_done, 6)
                    step(nc.vector.tensor_reduce(mx[:, :], att[:, :, :], axis=AX.X, op=ALU.add))
                    step(nc.vector.reciprocal(mx[:, :], mx[:, :]))
                    step(tt(att[:, :, :], att[:, :, :], mx[:, :].unsqueeze(2).to_broadcast([G, H, G]), ALU.mult))
                    dve.sem_inc(other_done, 1)
                    after_pe(5)
                    step(nc.vector.tensor_copy(attT[:, :], pp[0][0:G, :]))
                    dve.sem_inc(other_done, 1)
                    after_pe(6)
                    step(nc.vector.tensor_copy(oT[:, :], pp[1][0:C, :]))
                    dve.sem_inc(other_done, 1)
                    after_pe(7)
                    for j in range(PT):
                        nc.vector.tensor_copy(ow[:, j, :], pp[2 + j][:, 0:D])

                @block.scalar
                def _(act):
                    act.wait_ge(other_done, 5)
                    nc.scalar.activation(att[:, :, :], att[:, :, :], ACT.Exp, scale=float(C) ** -0.5).then_inc(other_done, 1)

                @block.tensor
                def _(pe):
                    mm = nc.tensor.matmul
                    hs = [slice(h * C, (h + 1) * C) for h in range(H)]
                    pe.wait_ge(other_done, 1)
                    for j in range(PT):
                        js = slice(j * P, (j + 1) * P)
                        for t in range(KD):
                            nc.tensor.transpose(pp[t][:, js], sums[:, j, t * P:(t + 1) * P], k.ident[:, :])
                        last = nc.tensor.transpose(pp[2][0:1, js], sums[:, j, D:D + 1], k.ident[:, :])
                    last.then_inc(pe_done, 1)
                    pe.wait_ge(other_done, 2)
                    for h in range(H):
                        for t in range(KD):
                            mm(pp[3][0:C, hs[h]], wfx[:, t, hs[h]], sT[:, t, hs[h]], start=(t == 0), stop=False)
                        last = mm(pp[3][0:C, hs[h]], bfx[:, hs[h]], nT[:, hs[h]], start=False, stop=True)
                    last.then_inc(pe_done, 1)
                    pe.wait_ge(other_done, 3)
                    mm(pp[4][0:C, :], wq[:, :], tokT[:, :], start=True, stop=True)
                    mm(pp[5][0:C, :], wk[:, :], tokT[:, :], start=True, stop=True)
                    for h in range(H):
                        last = mm(pp[6][0:G, hs[h]], tokT[:, hs[h]], wv[:, :], start=True, stop=True)
                    last.then_inc(pe_done, 1)
                    pe.wait_ge(other_done, 4)
                    for h in range(H):
                        last = mm(pp[7][0:G, hs[h]], qT[:, hs[h]], kT[:, hs[h]], start=True, stop=True)
                    last.then_inc(pe_done, 1)
                    pe.wait_ge(other_done, 7)
                    for h in range(H):
                        last = nc.tensor.transpose(pp[0][0:G, hs[h]], att[:, h, :], k.ident[0:G, 0:G])
                    last.then_inc(pe_done, 1)
                    pe.wait_ge(other_done, 8)
                    for h in range(H):
                        last = mm(pp[1][0:C, hs[h]], vv[:, hs[h]], attT[:, hs[h]], start=True, stop=True)
                    last.then_inc(pe_done, 1)
                    pe.wait_ge(other_done, 9)
                    for h in range(H):
                        o = (h % 2) * G
                        last = mm(pp[2 + h // 2][o:o + G, 0:D], oT[:, hs[h]], wout[:, h, :], start=True, stop=True)
                    last.then_inc(pe_done, 1)

        with ExitStack() as c3:
            st = k.sb(c3, "d_st", [P, 2, PT, P], fp32)
            tmp = k.sb(c3, "d_tmp", [P, 2, D], fp32)
            pO = [k.ps(c3, f"dO{i}", [P, D]) for i in range(2)]
            st_ready, o_ready, o_used, x_done, own3, x_out = map(k.sem, (
                "d_st_ready", "d_o_ready", "d_o_used", "d_x_done", "d_own3", "d_x_out"))
            with nc.Block() as block:

                @block.scalar
                def _(act):
                    def body(i, par, _):
                        if not isinstance(i, int) or i >= 2:
                            act.wait_ge(o_ready, i - 1)
                        nc.scalar.copy(st[:, par, :, :], wT[:, i, :, :]).then_inc(st_ready, 1)

                    pairs(act, NB, body)

                @block.tensor
                def _(pe):
                    def body(i, par, _):
                        pe.wait_ge(st_ready, i + 1)
                        if not isinstance(i, int) or i >= 2:
                            pe.wait_ge(o_used, i - 1)
                        for j in range(PT):
                            last = nc.tensor.matmul(pO[par][:, :], st[:, par, j, :], ow[:, j, :],
                                                    start=(j == 0), stop=(j == PT - 1))
                        last.then_inc(o_ready, 1)

                    pairs(pe, NB, body)

                @block.vector
                def _(dve):
                    tt = nc.vector.tensor_tensor

                    def body(i, par, _):
                        dve.wait_ge(o_ready, i + 1)
                        if not isinstance(i, int) or i >= 2:
                            dve.wait_ge(x_done, i - 1)
                        tt(tmp[:, par, :], pO[par][:, :], bout[:, :], ALU.add).then_inc(o_used, 1)
                        dve.wait_ge(o_used, i + 1)
                        tt(x[:, i, :], x[:, i, :], tmp[:, par, :], ALU.add).then_inc(x_done, 1)

                    pairs(dve, NB, body)

                @block.sync
                def _(sp):
                    for q in range(7):
                        bs = slice(q * NB // 7, (q + 1) * NB // 7)
                        sp.wait_ge(x_done, bs.stop)
                        sp.dma_start(k.x2.rearrange("(b p) d -> p b d", p=P)[:, bs, :], x[:, bs, :]).then_inc(x_out, 16)
                    sp.wait_ge(x_out, 16 * 7)


def stage_sage(k, n, hi, lo, residual, result):
    nc = k.nc
    HALF = [(0, (NB + 1) // 2), ((NB + 1) // 2, NB)]
    with ExitStack() as c:
        piece = [k.sb(c, f"f{n}_piece{i}", [P, HALF[0][1], SW], fp32r) for i in range(2)]
        piece_hi = k.sb(c, f"f{n}_piece_hi", [P, HALF[0][1], SW], fp32r)
        wl = k.sb(c, f"f{n}_wl", [P, KD, D], fp32)
        wr = k.sb(c, f"f{n}_wr", [P, KD, D], fp32)
        wlin = k.sb(c, f"f{n}_wlin", [P, KD, D], fp32)
        b0 = k.sb(c, f"f{n}_b0", [P, D], fp32)
        b1 = k.sb(c, f"f{n}_b1", [P, D], fp32)
        rdeg = k.sb(c, f"f{n}_rdeg", [P, NB], fp32)
        agg = k.sb(c, f"f{n}_agg", [P, KD, SW], fp32)
        rows = k.sb(c, f"f{n}_rows", [P, 2, D], fp32)
        rT = k.sb(c, f"f{n}_rowsT", [P, 2, KD, P], fp32)
        old = k.sb(c, f"f{n}_old", [P, 2, 2, D], fp32)
        mix = k.sb(c, f"f{n}_mix", [P, 2, 2, D], fp32)
        pA = [[k.ps(c, f"f{n}A{i}{t}", [P, SW]) for t in range(KD)] for i in range(2)]
        pT = k.ps(c, f"f{n}T", [P, 2, KD, P])
        pM = k.ps(c, f"f{n}M", [P, 2, D])
        pR = k.ps(c, f"f{n}R", [P, 2, D])
        piece_in = [k.sem(f"f{n}_piece_in{i}") for i in range(2)]
        piece_used = [k.sem(f"f{n}_piece_used{i}") for i in range(2)]
        piece_split = [k.sem(f"f{n}_piece_split{i}") for i in range(2)]
        old_in = [k.sem(f"f{n}_old_in{i}") for i in range(2)]
        stored = [k.sem(f"f{n}_stored{i}") for i in range(2)]
        (w_in, w_ready, agg_ready, rows_ready, t_done, rT_ready, m_done, m_used, own, mixed) = (
            k.sem(f"f{n}_{m}") for m in ("w_in", "w_ready", "agg_ready", "rows_ready", "t_done", "rT_ready", "m_done",
                                         "m_used", "own", "mixed"))
        slab_rows = lambda m, g, blocks: m.rearrange("(b p) d -> p b d", p=P)[:, bass.ds(2 * g, blocks), :]

        def width(g):
            return NB - 2 * (NSLAB - 1) if isinstance(g, int) and g == NSLAB - 1 else 2

        with nc.Block() as block:

            @block.sync
            def _(sp):
                for w, name in ((wl, f"L1_gnn_Wl{n}"), (wr, f"L1_gnn_Wr{n}"), (wlin, f"L1_gnn_Wlin{n}")):
                    sp.dma_start(w[:, :, :], k.ins[name].rearrange("(t p) n -> p t n", p=P)).then_inc(w_in, 16)
                sp.dma_start(b0[:, :], row(k.ins[f"L1_gnn_b{n}"])).then_inc(w_in, 16)
                sp.dma_start(b1[:, :], row(k.ins[f"L1_gnn_blin{n}"])).then_inc(w_in, 16)

                def body(g, par, t):
                    for j, (lo_b, hi_b) in enumerate(HALF):
                        sp.wait_ge(piece_used[j], g)
                        sp.dma_start(piece[j][:, 0:hi_b - lo_b, :].bitcast(fp32), counts_slab(k, g, lo_b, hi_b)
                                     ).then_inc(piece_in[j], 16)
                    if residual is not None:
                        if not isinstance(g, int) or g >= 2:
                            sp.wait_ge(mixed, g - 1)
                        sp.dma_start(old[:, par, 0:width(g), :], slab_rows(residual, g, width(g))).then_inc(old_in[par], 16)

                pairs(sp, NSLAB, body)

            @block.gpsimd
            def _(pool):
                def store(g, par, blocks):
                    pool.wait_ge(mixed, g + 1)
                    pool.dma_start(slab_rows(result, g, blocks), mix[:, par, 0:blocks, :]).then_inc(stored[par], 16)

                def body(g, par, t):
                    pool.wait_ge(t_done, g)
                    bs = bass.ds(2 * g, width(g))
                    nc.gpsimd.tensor_tensor(rows[:, 0:width(g), :], hi[:, bs, :].bitcast(fp32), lo[:, bs, :].bitcast(fp32),
                                            ALU.add).then_inc(rows_ready, 1)
                    if not isinstance(g, int) or g:
                        store(g - 1, 1 - par, 2)

                pairs(pool, NSLAB, body)
                store(NSLAB - 1, (NSLAB - 1) % 2, width(NSLAB - 1))
                pool.wait_ge(stored[0], 16 * ((NSLAB + 1) // 2))
                pool.wait_ge(stored[1], 16 * (NSLAB // 2))

            @block.vector
            def _(dve):
                step = Own(dve, own)
                tt, ts = nc.vector.tensor_tensor, nc.vector.tensor_scalar
                many = dve.value_load(k.many[0:1, 0:1], min_val=0, max_val=1)
                dve.wait_ge(w_in, 16 * 5)
                tt(b0[:, :], b0[:, :], b1[:, :], ALU.add)
                step(ts(rdeg[:, :], k.deg[:, 1, :], 1.0, None, ALU.max))
                step(nc.vector.reciprocal(rdeg[:, :], rdeg[:, :]))
                step(tt(wr[:, :, :], wr[:, :, :], wlin[:, :, :], ALU.add))
                dve.sem_inc(w_ready, 1)
                before = step.k

                def split(g, j):
                    lo_b, hi_b = HALF[j]
                    with dve.If(many > 0):
                        dve.wait_ge(piece_in[j], 16 * g + 16)
                        dve.wait_ge(piece_used[1 - j], g + j)
                        p, h = piece[j][:, 0:hi_b - lo_b, :], piece_hi[:, 0:hi_b - lo_b, :]
                        nc.vector.tensor_copy(h, p.bitcast(fp32)).then_inc(piece_split[j], 1)
                        dve.wait_ge(piece_split[j], 2 * g + 1)
                        tt(p, p.bitcast(fp32), h.bitcast(fp32), ALU.subtract).then_inc(piece_split[j], 1)

                def finish(g, par, t):
                    step.loop(before + 3 * g)
                    blocks = width(g)
                    dve.wait_ge(m_done, g + 1)
                    if not isinstance(g, int) or g >= 2:
                        dve.wait_ge(stored[par], 16 * t)
                    m = mix[:, par, :, :]
                    for j in range(blocks):
                        step(nc.vector.scalar_tensor_tensor(m[:, j, :], pM[:, j, :], rdeg[:, bass.ds(2 * g + j, 1)],
                                                            b0[:, :], ALU.mult, ALU.add))
                    step(tt(m[:, 0:blocks, :], m[:, 0:blocks, :], pR[:, 0:blocks, :], ALU.add))
                    dve.sem_inc(m_used, 1)
                    if residual is not None:
                        dve.wait_ge(old_in[par], 16 * t + 16)
                        tt(m[:, 0:blocks, :], m[:, 0:blocks, :], old[:, par, 0:blocks, :], ALU.add).then_inc(mixed, 1)
                    else:
                        ts(m[:, 0:blocks, :], m[:, 0:blocks, :], 0.0, None, ALU.max).then_inc(mixed, 1)

                def body(g, par, t):
                    split(g, 0)
                    if not isinstance(g, int) or g:
                        finish(g - 1, 1 - par, t if par else t - 1)
                    split(g, 1)

                ring(dve, NSLAB, body, peel=2)
                finish(NSLAB - 1, (NSLAB - 1) % 2, (NSLAB - 1) // 2)

            @block.scalar
            def _(act):
                def body(g, par, t):
                    blocks = width(g)
                    act.wait_ge(t_done, g + 1)
                    act.wait_ge(m_done, g)
                    nc.scalar.copy(rT[:, 0:blocks, :, :], pT[:, 0:blocks, :, :]).then_inc(rT_ready, 1)
                    act.wait_ge(piece_used[1], g + 1)
                    for t in range(KD):
                        last = nc.scalar.copy(agg[:, t, :], pA[par][t][:, :])
                    last.then_inc(agg_ready, 1)

                pairs(act, NSLAB, body)

            @block.tensor
            def _(pe):
                pe.wait_ge(w_ready, 1)
                many = pe.value_load(k.many[0:1, 0:1], min_val=0, max_val=1)

                def total(tile, j, par):
                    lo_b, hi_b = HALF[j]
                    for b in range(lo_b, hi_b):
                        for t in range(KD):
                            for part in (hi, lo):
                                nc.tensor.matmul(pA[par][t][:, :], part[:, b, t * P:(t + 1) * P], tile[:, b - lo_b, :],
                                                 start=(b == 0 and part is hi and tile is piece[j]), stop=False,
                                                 skip_group_check=True)

                def add(g, par, j):
                    pe.wait_ge(piece_in[j], 16 * g + 16)
                    with pe.If(many > 0):
                        pe.wait_ge(piece_split[j], 2 * g + 2)
                    total(piece[j], j, par)
                    with pe.If(many > 0):
                        total(piece_hi, j, par)
                    for t in range(KD):
                        last = nc.tensor.matmul(pA[par][t][0:2, 0:2], k.nought[:, 0:2], k.nought[:, 0:2], start=False,
                                                stop=(j == 1), skip_group_check=True)
                    last.then_inc(piece_used[j], 1)

                def products(g, blocks):
                    pe.wait_ge(rT_ready, g + 1)
                    pe.wait_ge(m_used, g)
                    for j in range(blocks):
                        for t in range(KD):
                            nc.tensor.matmul(pR[:, j, :], rT[:, j, t, :], wr[:, t, :], start=(t == 0), stop=(t == KD - 1))
                    pe.wait_ge(agg_ready, g + 1)
                    for j in range(blocks):
                        for t in range(KD):
                            last = nc.tensor.matmul(pM[:, j, :], agg[:, t, j * P:(j + 1) * P], wl[:, t, :],
                                                    start=(t == 0), stop=(t == KD - 1))
                    last.then_inc(m_done, 1)

                def body(g, par, _):
                    add(g, par, 0)
                    if not isinstance(g, int) or g:
                        products(g - 1, 2)
                    pe.wait_ge(rows_ready, g + 1)
                    for j in range(width(g)):
                        for t in range(KD):
                            last = nc.tensor.transpose(pT[:, j, t, :], rows[:, j, t * P:(t + 1) * P], k.ident[:, :])
                    last.then_inc(t_done, 1)
                    add(g, par, 1)

                pairs(pe, NSLAB, body)
                products(NSLAB - 1, width(NSLAB - 1))


def stage_route(k, x3, tok, where, weight):
    nc = k.nc
    with ExitStack() as c:
        stats = k.sb(c, "g_stats", [P, NB, 6], fp32)
        mv = k.sb(c, "g_mv", [P, 2, NB], fp32)
        sd = k.sb(c, "g_sd", [P, NB], fp32)
        rstd = k.sb(c, "g_rstd", [P, NB], fp32)
        tn = k.sb(c, "g_tn", [P, 2, D], fp32)
        tT = k.sb(c, "g_tT", [P, 2, KD, P], fp32)
        gw = k.sb(c, "g_gw", [P, KD, EX], fp32)
        gb = k.sb(c, "g_gb", [P, EX], fp32)
        lg = k.sb(c, "g_lg", [P, NB, EX], fp32)
        hot = k.sb(c, "g_hot", [P, NB, EX], fp32)
        cum = k.sb(c, "g_cum", [P, NB, EX], fp32)
        total = k.sb(c, "g_total", [P, NB, EX], fp32)
        a, b, e, pos, kept = (k.sb(c, f"g_{n}", [P, NB], fp32) for n in ("a", "b", "e", "pos", "kept"))
        rank = k.sb(c, "g_rank", [P, EX], fp32)
        token = k.sb(c, "g_token", [P, NB], fp32)
        upto = k.sb(c, "g_upto", [P, P], fp32)
        ones = k.sb(c, "g_ones", [P, P], fp32)
        pT = [k.ps(c, f"gT{i}", [P, KD, P]) for i in range(2)]
        pG = [k.ps(c, f"gG{i}", [P, EX]) for i in range(2)]
        pC = [k.ps(c, f"gC{i}", [P, NB * EX]) for i in range(2)]
        (x_in, w_in, stats_made, var_ready, sd_ready, own, consts, tn_ready, stored, t_done, tT_ready, g_done, g_used,
         shifted, e_ready, hot_ready, cum_done, pown) = map(k.sem, (
             "g_x_in", "g_w_in", "g_stats_made", "g_var", "g_sd_ready", "g_own", "g_consts", "g_tn_ready", "g_stored", "g_t_done",
             "g_tT_ready", "g_g_done", "g_g_used", "g_shifted", "g_e_ready", "g_hot_ready", "g_cum_done", "g_pown"))
        with nc.Block() as block:

            @block.sync
            def _(sp):
                sp.dma_start(x3[:, :, :], k.x3.rearrange("(b p) d -> p b d", p=P)).then_inc(x_in, 16)
                sp.dma_start(gw[:, :, :], k.ins["L1_ffn_gate_w"].rearrange("(t p) n -> p t n", p=P)).then_inc(w_in, 16)
                sp.dma_start(gb[:, :], row(k.ins["L1_ffn_gate_b"])).then_inc(w_in, 16)

            @block.gpsimd
            def _(pool):
                step = Own(pool, pown)
                pool.iota(rank[:, :], [[-1, EX]], base=EX, channel_multiplier=0, allow_small_or_imprecise_dtypes=True)
                pool.iota(token[:, :], [[P, NB]], base=0, channel_multiplier=1, allow_small_or_imprecise_dtypes=True)
                pool.memset(ones[:, :], 1.0)
                step(pool.memset(upto[:, :], 1.0))
                step(pool.affine_select(out=upto[:, :], in_=upto[:, :], compare_op=ALU.is_ge, fill=0.0, base=0,
                                        pattern=[[1, P]], channel_multiplier=-1))
                pool.sem_inc(consts, 1)

                def body(i, par, _):
                    pool.wait_ge(tn_ready, i + 1)
                    pool.tensor_copy(tok[:, i, :], tn[:, par, :]).then_inc(stored, 1)

                pairs(pool, NB, body)

            @block.vector
            def _(dve):
                step = Own(dve, own)
                tt, ts = nc.vector.tensor_tensor, nc.vector.tensor_scalar
                dve.wait_ge(x_in, 16)
                with dve.Fori(0, NB) as i:
                    nc.vector.bn_stats(stats[:, i, :], x3[:, i, :]).then_inc(stats_made, 1)
                dve.wait_ge(stats_made, NB)
                moments(nc, step, stats, mv, sd)
                dve.sem_inc(var_ready, 1)
                dve.wait_ge(sd_ready, 1)
                step(nc.vector.reciprocal(rstd[:, :], sd[:, :]))
                dve.wait_ge(w_in, 32)

                def norm(i, par):
                    dve.wait_ge(t_done, i)
                    dve.wait_ge(stored, i)
                    ts(tn[:, par, :], x3[:, i, :], mv[:, 0, bass.ts(i, 1)], rstd[:, bass.ts(i, 1)],
                       ALU.subtract, ALU.mult).then_inc(tn_ready, 1)

                def body(i, par, _):
                    norm(i, par)
                    dve.wait_ge(g_done, i + 1)
                    tt(lg[:, i, :], pG[par][:, :], gb[:, :], ALU.add).then_inc(g_used, 1)

                pairs(dve, NB, body)
                dve.wait_ge(g_used, NB)
                dve.wait_ge(consts, 1)
                wide = lambda v: v.unsqueeze(2).to_broadcast([P, NB, EX])
                step(nc.vector.tensor_reduce(a[:, :], lg[:, :, :], axis=AX.X, op=ALU.max))
                step(tt(lg[:, :, :], lg[:, :, :], wide(a[:, :]), ALU.subtract))
                dve.sem_inc(shifted, 1)
                dve.wait_ge(e_ready, 1)
                step(nc.vector.tensor_reduce(a[:, :], lg[:, :, :], axis=AX.X, op=ALU.add))
                step(nc.vector.reciprocal(weight[:, :], a[:, :]))
                step(ts(hot[:, :, :], lg[:, :, :], 1.0, None, ALU.is_ge))
                rk = rank[:, :].unsqueeze(1).to_broadcast([P, NB, EX])
                step(tt(hot[:, :, :], hot[:, :, :], rk, ALU.mult))
                step(nc.vector.tensor_reduce(e[:, :], hot[:, :, :], axis=AX.X, op=ALU.max))
                step(tt(hot[:, :, :], rk, wide(e[:, :]), ALU.is_equal))
                step(ts(e[:, :], e[:, :], -1.0, float(EX), ALU.mult, ALU.add))
                step(tt(hot[:, :, :], hot[:, :, :], wide(k.valid[:, :]), ALU.mult))
                dve.sem_inc(hot_ready, 1)
                dve.wait_ge(cum_done, 1)
                flat = lambda v: v[:, :, :].rearrange("p b e -> p (b e)")
                nc.vector.tensor_copy(flat(cum), pC[0][:, :])
                step(nc.vector.tensor_copy(flat(total), pC[1][:, :]))
                step(tt(flat(cum), flat(cum), flat(total), ALU.subtract))
                src, other = total, lg
                reach = 1
                while reach < NB:
                    nc.vector.tensor_copy(other[:, 0:reach, :], src[:, 0:reach, :])
                    step(tt(other[:, reach:NB, :], src[:, reach:NB, :], src[:, 0:NB - reach, :], ALU.add))
                    src, other = other, src
                    reach *= 2
                step(tt(flat(cum), flat(cum), flat(src), ALU.add))
                step(tt(cum[:, :, :], cum[:, :, :], hot[:, :, :], ALU.mult))
                step(nc.vector.tensor_reduce(pos[:, :], cum[:, :, :], axis=AX.X, op=ALU.add))
                step(ts(pos[:, :], pos[:, :], -1.0, None, ALU.add))
                step(ts(kept[:, :], pos[:, :], float(CAP), None, ALU.is_lt))
                tt(weight[:, :], weight[:, :], kept[:, :], ALU.mult)
                step(ts(pos[:, :], pos[:, :], float(CAP - 1), 0.0, ALU.min, ALU.max))
                step(ts(e[:, :], e[:, :], float(ROWS), None, ALU.mult))
                step(tt(pos[:, :], pos[:, :], e[:, :], ALU.add))
                nc.vector.tensor_copy(where[:, 1, :], pos[:, :])
                step(ts(a[:, :], token[:, :], float(EX * ROWS), None, ALU.add))
                step(tt(pos[:, :], pos[:, :], a[:, :], ALU.subtract))
                step(tt(pos[:, :], pos[:, :], kept[:, :], ALU.mult))
                step(tt(pos[:, :], pos[:, :], a[:, :], ALU.add))
                nc.vector.tensor_copy(where[:, 0, :], pos[:, :])

            @block.scalar
            def _(act):
                act.wait_ge(var_ready, 1)
                nc.scalar.activation(sd[:, :], sd[:, :], ACT.Sqrt, bias=k.eps[:, 0:1]).then_inc(sd_ready, 1)

                def body(i, par, _):
                    act.wait_ge(t_done, i + 1)
                    act.wait_ge(g_done, i)
                    nc.scalar.copy(tT[:, par, :, :], pT[par][:, :, :]).then_inc(tT_ready, 1)

                pairs(act, NB, body)
                act.wait_ge(shifted, 1)
                nc.scalar.activation(lg[:, :, :], lg[:, :, :], ACT.Exp).then_inc(e_ready, 1)

            @block.tensor
            def _(pe):
                pe.wait_ge(w_in, 32)

                def body(i, par, _):
                    pe.wait_ge(tn_ready, i + 1)
                    pe.wait_ge(tT_ready, i)
                    for t in range(KD):
                        last = nc.tensor.transpose(pT[par][:, t, :], tn[:, par, t * P:(t + 1) * P], k.ident[:, :])
                    last.then_inc(t_done, 1)
                    pe.wait_ge(tT_ready, i + 1)
                    pe.wait_ge(g_used, i)
                    for t in range(KD):
                        last = nc.tensor.matmul(pG[par][:, :], tT[:, par, t, :], gw[:, t, :], start=(t == 0),
                                                stop=(t == KD - 1))
                    last.then_inc(g_done, 1)

                pairs(pe, NB, body)
                pe.wait_ge(hot_ready, 1)
                h = hot[:, :, :].rearrange("p b e -> p (b e)")
                nc.tensor.matmul(pC[0][:, :], upto[:, :], h, start=True, stop=True)
                nc.tensor.matmul(pC[1][:, :], ones[:, :], h, start=True, stop=True).then_inc(cum_done, 1)


def stage_experts(k, x3, tok, where, weight):
    nc = k.nc
    FT = FF // P
    TT = ROWS // P
    LT = CAP - (TT - 1) * P
    SPLIT = [(0, (CAP + 1) // 2), ((CAP + 1) // 2, CAP)]
    inbox, outbox = k.inbox, k.outbox
    sent, = (k.sem("h_sent"),)
    with nc.Block() as block:

        @block.gpsimd
        def _(pool):
            for b in range(NB):
                n = P if b < NB - 1 else LAST
                pool.indirect_dma_start(out=inbox[:, :], out_offset=bass.IndirectOffsetOnAxis(ap=where[0:n, 0, b:b + 1], axis=0),
                                        in_=tok[0:n, b, :], in_offset=None).then_inc(sent, 16)
            pool.wait_ge(sent, 16 * NB)

    with ExitStack() as c:
        w1 = [k.sb(c, f"h_w1{i}", [P, KD, FF], fp32) for i in range(2)]
        w2 = [k.sb(c, f"h_w2{i}", [P, FT, D], fp32) for i in range(2)]
        b1 = [k.sb(c, f"h_b1{i}", [P, FT], fp32) for i in range(2)]
        b2 = k.sb(c, "h_b2", [P, EX, D], fp32)
        rows = k.sb(c, "h_rows", [P, TT, D], fp32)
        rT = k.sb(c, "h_rT", [P, KD, TT, P], fp32)
        hT = k.sb(c, "h_hT", [P, FT, CAP], fp32)
        y = k.sb(c, "h_y", [P, TT, D], fp32)
        pT = [k.ps(c, f"hT{i}", [P, KD, P]) for i in range(2)]
        pH = [k.ps(c, f"hH{i}", [P, 512]) for i in range(4)]
        pY = [k.ps(c, f"hY{i}", [P, D]) for i in range(2)]
        w_in = [k.sem(f"h_w_in{i}") for i in range(2)]
        (b_in, rows_in, t_done, rT_ready, h_done, h_ready, y_done, y_ready, y_out) = map(k.sem, (
            "h_b_in", "h_rows_in", "h_t_done", "h_rT_ready", "h_h_done", "h_h_ready", "h_y_done", "h_y_ready", "h_y_out"))
        NH = FT * 2
        with nc.Block() as block:

            @block.sync
            def _(sp):
                sp.dma_start(b2[:, :, :].rearrange("p e d -> p (e d)"), row(k.ins["L1_ffn_b2"].rearrange("e d -> (e d)"))
                             ).then_inc(b_in, 16)

                def body(e, par, _):
                    sp.wait_ge(t_done, TT * e)
                    sp.dma_start(rows[:, :, :], inbox[0:EX * ROWS, :].rearrange("(e t p) d -> p e t d", e=EX, p=P)[
                        :, e, :, :]).then_inc(rows_in, 16)
                    sp.wait_ge(y_ready, TT * e)
                    sp.dma_start(w1[par][:, :, :], k.ins["L1_ffn_w1"].rearrange("e (t p) f -> p e t f", p=P)[
                        :, e, :, :]).then_inc(w_in[par], 16)
                    sp.dma_start(w2[par][:, :, :], k.ins["L1_ffn_w2"].rearrange("e (t p) d -> p e t d", p=P)[
                        :, e, :, :]).then_inc(w_in[par], 16)
                    sp.dma_start(b1[par][:, :], k.ins["L1_ffn_b1t"][:, e, :]).then_inc(w_in[par], 16)

                pairs(sp, EX, body)

            @block.gpsimd
            def _(pool):
                def body(e, par, _):
                    pool.wait_ge(y_ready, TT * e + TT)
                    pool.dma_start(outbox.rearrange("(e t p) d -> p e t d", e=EX, p=P)[:, e, :, :], y[:, :, :]
                                   ).then_inc(y_out, 16)

                pairs(pool, EX, body)
                pool.wait_ge(y_out, 16 * EX)

            @block.vector
            def _(dve):
                dve.wait_ge(b_in, 16)
                nc.vector.memset(y[:, TT - 1, :], 0.0)

                def body(e, par, _):
                    for q in range(TT):
                        dve.wait_ge(t_done, TT * e + q + 1)
                        dve.wait_ge(h_done, NH * e)
                        nc.vector.tensor_copy(rT[:, :, q, :], pT[q % 2][:, :, :]).then_inc(rT_ready, 1)
                    dve.wait_ge(y_out, 16 * e)
                    for q in range(TT):
                        dve.wait_ge(y_done, TT * e + q + 1)
                        m = P if q < TT - 1 else LT
                        nc.vector.tensor_tensor(y[0:m, q, :], pY[q % 2][0:m, :], b2[0:m, e, :], ALU.add
                                                ).then_inc(y_ready, 1)

                pairs(dve, EX, body)

            @block.scalar
            def _(act):
                act.preload_act_table(ACT.Relu)

                def body(e, par, t):
                    act.wait_ge(w_in[par], 48 * t + 48)
                    act.wait_ge(y_done, TT * e)
                    for f in range(FT):
                        for j, (lo, hi) in enumerate(SPLIT):
                            n = 2 * f + j
                            act.wait_ge(h_done, NH * e + n + 1)
                            nc.scalar.activation(hT[:, f, lo:hi], pH[n % 4][:, 0:hi - lo], ACT.Relu,
                                                 bias=b1[par][:, f:f + 1]).then_inc(h_ready, 1)

                pairs(act, EX, body)

            @block.tensor
            def _(pe):
                def body(e, par, t_):
                    pe.wait_ge(rows_in, 16 * e + 16)
                    for q in range(TT):
                        pe.wait_ge(rT_ready, TT * e + max(q - 1, 0))
                        for t in range(KD):
                            last = nc.tensor.transpose(pT[q % 2][:, t, :], rows[:, q, t * P:(t + 1) * P], k.ident[:, :])
                        last.then_inc(t_done, 1)
                    pe.wait_ge(w_in[par], 48 * t_ + 48)
                    pe.wait_ge(rT_ready, TT * e + TT)
                    rv = rT[:, :, :, :].rearrange("p t q n -> p t (q n)")
                    for f in range(FT):
                        for j, (lo, hi) in enumerate(SPLIT):
                            n = 2 * f + j
                            pe.wait_ge(h_ready, NH * e + max(n - 3, 0))
                            for t in range(KD):
                                last = nc.tensor.matmul(pH[n % 4][:, 0:hi - lo], w1[par][:, t, f * P:(f + 1) * P],
                                                        rv[:, t, lo:hi], start=(t == 0), stop=(t == KD - 1))
                            last.then_inc(h_done, 1)
                    pe.wait_ge(h_ready, NH * e + NH)
                    for q in range(TT):
                        m = P if q < TT - 1 else LT
                        pe.wait_ge(y_ready, TT * e + max(q - 1, 0))
                        for f in range(FT):
                            last = nc.tensor.matmul(pY[q % 2][0:m, :], hT[:, f, q * P:q * P + m], w2[par][:, f, :],
                                                    start=(f == 0), stop=(f == FT - 1))
                        last.then_inc(y_done, 1)

                pairs(pe, EX, body)

    with ExitStack() as c:
        PB = 7
        rest = k.sb(c, "i_rest", [P, 2, PB, D], fp32)
        odd = k.sb(c, "i_odd", [P, 2, PB, D], i32)
        zero = k.sb(c, "i_zero", [P, PB, D], fp32)
        fetched = [k.sem(f"i_fetched{i}") for i in range(NB // PB)]
        own, ready, stored = map(k.sem, ("i_own", "i_ready", "i_stored"))
        assert NB % PB == 0
        with nc.Block() as block:

            @block.gpsimd
            def _(pool):
                for b in range(NB):
                    n = P if b < NB - 1 else LAST
                    pool.indirect_dma_start(out=tok[0:n, b, :], out_offset=None, in_=outbox[:, :],
                                            in_offset=bass.IndirectOffsetOnAxis(ap=where[0:n, 1, b:b + 1], axis=0)
                                            ).then_inc(fetched[b // PB], 16)

            @block.vector
            def _(dve):
                step = Own(dve, own)
                tt, ts = nc.vector.tensor_tensor, nc.vector.tensor_scalar
                step(nc.vector.memset(zero[:, :, :], 0.0))
                for q in range(NB // PB):
                    dve.wait_ge(fetched[q], 16 * PB)
                    bs = slice(q * PB, (q + 1) * PB)
                    y = tok[:, bs, :]
                    r, o = rest[:, q % 2, :, :], odd[:, q % 2, :, :]
                    step(tt(y, y, weight[:, bs].unsqueeze(2).to_broadcast([P, PB, D]), ALU.mult))
                    step(tt(r, y, y, ALU.subtract))
                    step(ts(o, r, 0.0, None, ALU.not_equal))
                    step(ts(r, y, 10000.0, -10000.0, ALU.min, ALU.max))
                    step(nc.vector.copy_predicated(y, o, r))
                    step(tt(o, y, y, ALU.not_equal))
                    step(nc.vector.copy_predicated(y, o, zero[:, :, :]))
                    tt(x3[:, bs, :], x3[:, bs, :], y, ALU.add).then_inc(ready, 1)

            @block.sync
            def _(sp):
                whole = k.out[0:(NB - 1) * P, :].rearrange("(b p) d -> p b d", p=P)
                for q in range(NB // PB):
                    sp.wait_ge(ready, q + 1)
                    hi = min((q + 1) * PB, NB - 1)
                    sp.dma_start(whole[:, q * PB:hi, :], x3[:, q * PB:hi, :]).then_inc(stored, 16)
                sp.dma_start(k.out[(NB - 1) * P:N, :], x3[0:LAST, NB - 1, :]).then_inc(stored, 16)
                sp.wait_ge(stored, 16 * (NB // PB + 1))


def program(nc, ins, out, limit=EXACT):
    with ExitStack() as ctx:
        k = Core(nc, ctx, ins, out)
        stage_linear(k)
        stage_count(k, limit)
        with ExitStack() as c:
            hi, lo = (k.sb(c, f"m_{n}", [P, NB, D], fp32r) for n in ("hi", "lo"))
            stage_split(k, "s0", k.h0, hi, lo, "degree")
            stage_sum_out(k, hi, lo)
        k.done()
        stage_slice(k)
        with ExitStack() as c:
            hi, lo = (k.sb(c, f"v_{n}", [P, NB, D], fp32r) for n in ("hi", "lo"))
            stage_split(k, "s1", k.x2, hi, lo, "norm")
            stage_sage(k, 1, hi, lo, None, k.h1)
            stage_split(k, "s2", k.h1, hi, lo, None)
            stage_sage(k, 2, hi, lo, k.x2, k.x3)
        k.done()
        with ExitStack() as c:
            x3, tok = (k.sb(c, n, [P, NB, D], fp32) for n in ("x3_rows", "tok"))
            where = k.sb(c, "where", [P, 2, NB], i32)
            weight = k.sb(c, "weight", [P, NB], fp32)
            stage_route(k, x3, tok, where, weight)
            stage_experts(k, x3, tok, where, weight)


def kernel(**inputs):
    import numpy as _np
    import concourse.bacc as _bacc
    from concourse import mybir as _mybir
    from concourse.bass_utils import run_bass_kernel_spmd as _run

    arrays = {n: _np.asarray(v) for n, v in inputs.items()}
    arrays["L0_gnn_Wt"] = arrays.pop("L0_gnn_W").T
    arrays["L0_ffn_W_xt"] = arrays.pop("L0_ffn_W_x").T
    arrays["L0_ffn_b_xt"] = arrays.pop("L0_ffn_b_x").reshape(H, C).T
    arrays["L1_ffn_b1t"] = arrays.pop("L1_ffn_b1").reshape(EX, FF // P, P).transpose(2, 0, 1)
    arrays = {n: _np.ascontiguousarray(v) for n, v in arrays.items()}
    nc = _bacc.Bacc("TRN2", target_bir_lowering=False, num_devices=1)
    ins = {n: nc.dram_tensor("in_" + n, a.shape, _mybir.dt.from_np(a.dtype), kind="ExternalInput").ap()
           for n, a in arrays.items()}
    out = nc.dram_tensor("out_x", (N, D), fp32, kind="ExternalOutput").ap()
    program(nc, ins, out)
    r = _run(nc, [{"in_" + n: a for n, a in arrays.items()}], core_ids=[0])
    return r.results[0]["out_x"]
```

```python
from contextlib import ExitStack

import numpy as np

import concourse.bass as bass
from concourse import mybir

fp32 = mybir.dt.float32
fp32r = mybir.dt.float32r
bf16 = mybir.dt.bfloat16
i32 = mybir.dt.int32
ALU = mybir.AluOpType
ACT = mybir.ActivationFunctionType
AX = mybir.AxisListType

P = 128
N = 6250
D = 256
E = 200000
NB = -(-N // P)
LAST = N - (NB - 1) * P
KD = D // P
EPS = 1e-5

CE = 125
GC = 8
GE = CE * GC
BG = 2
BC = BG * GC
BE = CE * BC
BATCHES = E // BE
BITS = 13
assert BATCHES * BE == E and BATCHES % 2 == 0 and N < 1 << BITS
EXACT = 1 << 12

SW = 256
NSLAB = -(-N // SW)
SH = 64
COUNTS = NSLAB * P * SH * SW
SPARE = COUNTS

H, G, C = 8, 64, 64
HG = H * G

EX = 8
FF = 1024
ROWS = 1024
CAP = max(1, -(-5 * N // (4 * EX)))


class Own:

    def __init__(self, eng, sem):
        self.eng, self.sem, self.at, self.k = eng, sem, 0, 0

    def loop(self, at):
        self.at, self.k = at, 0

    def __call__(self, ins):
        self.k += 1
        ins.then_inc(self.sem, 1)
        self.eng.wait_ge(self.sem, self.at + self.k)


def ring(eng, n, body, ways=2, peel=1):
    rounds = n // ways
    for i in range(ways * peel):
        body(i, i % ways, i // ways)
    if rounds > peel + 1:
        with eng.Fori(peel, rounds - 1) as t:
            for j in range(ways):
                body(ways * t + j, j, t)
    for i in range(ways * (rounds - 1), n):
        body(i, i % ways, i // ways)


def pairs(eng, n, body):
    ring(eng, n, body)


def moments(nc, step, stats, mv, var):
    n2 = float(D)
    step(nc.vector.tensor_tensor(mv[:, 1, :], stats[:, :, 1], stats[:, :, 4], ALU.subtract))
    step(nc.vector.tensor_tensor(mv[:, 0, :], stats[:, :, 1], stats[:, :, 4], ALU.add))
    step(nc.vector.tensor_scalar(mv[:, 0, :], mv[:, 0, :], 0.5, None, ALU.mult))
    step(nc.vector.tensor_tensor(mv[:, 1, :], mv[:, 1, :], mv[:, 1, :], ALU.mult))
    step(nc.vector.tensor_tensor(var[:, :], stats[:, :, 2], stats[:, :, 5], ALU.add))
    step(nc.vector.tensor_scalar(mv[:, 1, :], mv[:, 1, :], n2 / 4, None, ALU.mult))
    step(nc.vector.tensor_tensor(var[:, :], var[:, :], mv[:, 1, :], ALU.add))
    step(nc.vector.tensor_scalar(var[:, :], var[:, :], 1 / n2, None, ALU.mult))


class Core:

    def __init__(self, nc, ctx, ins, out):
        self.nc, self.ctx, self.ins, self.out = nc, ctx, ins, out
        self.sems = []
        self.ident = self.sb(ctx, "ident", [P, P], fp32)
        self.valid = self.sb(ctx, "valid", [P, NB], fp32)
        self.eps = self.sb(ctx, "eps", [P, 1], fp32)
        self.deg = self.sb(ctx, "deg", [P, 2, NB], fp32)
        self.dinv = self.sb(ctx, "dinv", [P, NB], fp32)
        self.stats = self.sb(ctx, "stats", [P, NB, 6], fp32)
        self.many = self.sb(ctx, "many", [1, 1], i32)
        self.odd = self.sb(ctx, "odd", [1, 1], i32)
        scratch = lambda name: nc.dram_tensor(name, [NB * P, D], fp32).ap()
        self.x1, self.x2, self.rest, self.h1, self.x3 = map(scratch, ("x1", "x2", "rest", "h1", "x3"))
        self.inbox = nc.dram_tensor("inbox", [EX * ROWS + NB * P, D], fp32).ap()
        self.outbox = nc.dram_tensor("outbox", [EX * ROWS, D], fp32).ap()
        self.counts = nc.dram_tensor("counts", [COUNTS + GE, 1], fp32).ap()

    def sb(self, ctx, name, shape, dt):
        return ctx.enter_context(self.nc.sbuf_tensor(name, shape, dt))

    def ps(self, ctx, name, shape, dt=fp32):
        return ctx.enter_context(self.nc.psum_tensor(name, shape, dt))

    def sem(self, name):
        s = self.nc.alloc_semaphore(name)
        self.sems.append(s)
        return s

    def done(self):
        self.nc.clear_and_free_semaphores(self.sems)
        self.nc.all_engine_barrier()
        self.sems = []


def counts_slab(k, slab, b0, b1):
    v = k.counts[0:COUNTS, :].rearrange("(g p h w) o -> g p h (w o)", g=NSLAB, p=P, h=SH)
    return v[slab, :, b0:b1, :]


def row(vec, n=P):
    return vec.rearrange("(o n) -> o n", o=1).to_broadcast([n, vec.shape[0]])


def stage_linear(k, x):
    nc = k.nc
    with ExitStack() as c:
        zero = k.sb(c, "zero", [P, NB * SW], fp32)
        wt = k.sb(c, "wt", [P, KD, D], fp32)
        bias = k.sb(c, "bias", [P, D], fp32)
        mv = k.sb(c, "mv", [P, 2, NB], fp32)
        sd = k.sb(c, "sd", [P, NB], fp32)
        rstd = k.sb(c, "rstd", [P, NB], fp32)
        xn = k.sb(c, "xn", [P, 2, D], fp32)
        xnT = k.sb(c, "xnT", [P, 2, KD, P], fp32)
        pT = [k.ps(c, f"pT{i}", [P, KD, P]) for i in range(2)]
        pH = [k.ps(c, f"pH{i}", [P, D]) for i in range(2)]
        x_zeroed, stats_made, x_in, w_in, zeros, mask_made, counts_zeroed = map(
            k.sem, ("a_x_zeroed", "a_stats_made", "a_x_in", "a_w_in", "a_zeros", "a_mask_made", "counts_zeroed"))
        var_ready, sd_ready, xn_ready, t_done, xnT_ready, h_done, h_used, own, pown = map(
            k.sem, ("a_var", "a_sd", "a_xn", "a_t", "a_xnT", "a_h", "a_h_used", "a_own", "a_pown"))
        with nc.Block() as block:

            @block.sync
            def _(sp):
                sp.wait_ge(x_zeroed, 1)
                sp.dma_start(x[:, 0:NB - 1, :], k.ins["x"][0:(NB - 1) * P, :].rearrange(
                    "(b p) d -> p b d", p=P)).then_inc(x_in, 16)
                sp.dma_start(x[0:LAST, NB - 1, :], k.ins["x"][(NB - 1) * P:N, :]).then_inc(x_in, 16)
                sp.dma_start(wt[:, :, :], k.ins["L0_gnn_Wt"].rearrange("(t p) n -> p t n", p=P)).then_inc(w_in, 16)
                sp.dma_start(bias[:, :], row(k.ins["L0_gnn_b"])).then_inc(w_in, 16)
                sp.wait_ge(zeros, 1)
                for g in range(NSLAB):
                    sp.dma_start(counts_slab(k, g, 0, NB), zero[:, :].rearrange("p (h w) -> p h w", w=SW)
                                 ).then_inc(counts_zeroed, 16)
                sp.dma_start(k.counts[COUNTS:COUNTS + GE, :].rearrange("(p w) o -> p (w o)", p=CE),
                             zero[0:CE, 0:GC]).then_inc(counts_zeroed, 16)
                sp.wait_ge(counts_zeroed, 16 * (NSLAB + 1))

            @block.gpsimd
            def _(pool):
                step = Own(pool, pown)
                pool.memset(x[:, NB - 1, :], 0.0).then_inc(x_zeroed, 1)
                pool.memset(k.eps[:, :], EPS)
                step(pool.memset(k.ident[:, :], 0.0))
                step(pool.affine_select(out=k.ident[:, :], in_=k.ident[:, :], compare_op=ALU.not_equal, fill=1.0,
                                        base=0, pattern=[[-1, P]], channel_multiplier=1))
                step(pool.memset(k.valid[:, :], 1.0))
                pool.affine_select(out=k.valid[:, NB - 1:NB], in_=k.valid[:, NB - 1:NB], compare_op=ALU.is_ge,
                                   fill=0.0, base=LAST - 1, pattern=[[0, 1]], channel_multiplier=-1
                                   ).then_inc(mask_made, 1)

            @block.vector
            def _(dve):
                step = Own(dve, own)
                nc.vector.memset(zero[:, :], 0.0).then_inc(zeros, 1)
                dve.wait_ge(x_in, 32)
                with dve.Fori(0, NB) as i:
                    nc.vector.bn_stats(k.stats[:, i, :], x[:, i, :]).then_inc(stats_made, 1)
                dve.wait_ge(stats_made, NB)
                moments(nc, step, k.stats, mv, sd)
                dve.sem_inc(var_ready, 1)
                dve.wait_ge(sd_ready, 1)
                step(nc.vector.reciprocal(rstd[:, :], sd[:, :]))

                def norm(i, par):
                    dve.wait_ge(t_done, i)
                    nc.vector.tensor_scalar(xn[:, par, :], x[:, i, :], mv[:, 0, bass.ts(i, 1)], rstd[:, bass.ts(i, 1)],
                                            ALU.subtract, ALU.mult).then_inc(xn_ready, 1)

                def add_bias(i, par):
                    dve.wait_ge(h_done, i + 1)
                    nc.vector.tensor_tensor(x[:, i, :], pH[par][:, :], bias[:, :], ALU.add).then_inc(h_used, 1)

                dve.wait_ge(w_in, 32)

                norm(0, 0)

                def body(i, par, _):
                    if not (isinstance(i, int) and i == NB - 1):
                        norm(i + 1, 1 - par)
                    add_bias(i, par)

                pairs(dve, NB, body)

            @block.scalar
            def _(act):
                act.wait_ge(var_ready, 1)
                act.wait_ge(x_zeroed, 1)
                act.wait_ge(mask_made, 1)
                nc.scalar.activation(sd[:, :], sd[:, :], ACT.Sqrt, bias=k.eps[:, 0:1]).then_inc(sd_ready, 1)

                def body(i, par, _):
                    act.wait_ge(t_done, i + 1)
                    act.wait_ge(h_used, i)
                    nc.scalar.copy(xnT[:, par, :, :], pT[par][:, :, :]).then_inc(xnT_ready, 1)

                pairs(act, NB, body)

            @block.tensor
            def _(pe):
                pe.wait_ge(w_in, 32)
                pe.wait_ge(mask_made, 1)

                def turn(i, par):
                    pe.wait_ge(xn_ready, i + 1)
                    for t in range(KD):
                        last = nc.tensor.transpose(pT[par][:, t, :], xn[:, par, t * P:(t + 1) * P], k.ident[:, :])
                    last.then_inc(t_done, 1)

                turn(0, 0)

                def body(i, par, _):
                    if not (isinstance(i, int) and i == NB - 1):
                        turn(i + 1, 1 - par)
                    pe.wait_ge(xnT_ready, i + 1)
                    pe.wait_ge(h_used, i)
                    for t in range(KD):
                        last = nc.tensor.matmul(pH[par][:, :], xnT[:, par, t, :], wt[:, t, :],
                                                start=(t == 0), stop=(t == KD - 1))
                    last.then_inc(h_done, 1)

                pairs(pe, NB, body)


def stage_count(k, limit):
    nc = k.nc
    delta = 2.0 ** -11
    assert GE * delta < 0.5
    MARK = 32
    KC = MARK + GC
    with ExitStack() as c:
        node = k.sb(c, "node", [CE, 2, 2, BC], i32)
        raw = k.sb(c, "raw", [2 * BITS, 2, BE], i32)
        bit = k.sb(c, "bit", [2 * BITS, BE], i32)
        theirs = k.sb(c, "theirs", [KC, 2, BE], bf16)
        mine = k.sb(c, "mine", [KC, 2, BE], bf16)
        shift = k.sb(c, "shift", [2 * BITS, 1], i32)
        identb = k.sb(c, "identb", [CE, CE], bf16)
        earlier = k.sb(c, "earlier", [CE, CE], bf16)
        lane = k.sb(c, "lane", [CE, P], bf16)
        spare = k.sb(c, "spare", [CE, GC], i32)
        part = k.sb(c, "part", [CE, 7, BC], i32)
        cell = k.sb(c, "cell", [CE, 2, BC], i32)
        lowi = k.sb(c, "lowi", [CE, 4, BC], i32)
        low = k.sb(c, "low", [CE, 2, 4, BC], bf16)
        hot = k.sb(c, "hot", [CE, 2, 2, GC, P], bf16)
        hoth = k.sb(c, "hoth", [CE, 2, 2, GC, NB], bf16)
        junk = k.sb(c, "junk", [CE, 3, 2, GE // 2], bf16)
        score = k.sb(c, "score", [CE, 2, GC], fp32)
        whole = k.sb(c, "whole", [CE, GC], i32)
        first = k.sb(c, "first", [CE, GC], i32)
        value = k.sb(c, "value", [CE, 2, GC], fp32)
        index = k.sb(c, "index", [CE, 2, GC], i32)
        neg = k.sb(c, "neg", [CE, 1], fp32)
        top = k.sb(c, "top", [P, 2], fp32)
        alltop = k.sb(c, "alltop", [P, 2], fp32)
        zb = k.sb(c, "zb", [CE, P], bf16)
        blank = k.sb(c, "blank", [P, EX * ROWS * D // P // 8], fp32)
        agree = [k.ps(c, f"agree{i}", [P, 2, 512]) for i in range(3)]
        degp = k.ps(c, "degp", [P, 512])
        edges_in = [k.sem(f"edges_in{i}") for i in range(2)]
        edges_used = [k.sem(f"edges_used{i}") for i in range(2)]
        (consts, codes_ready, hot_ready, hot_used, agree_ready, score_ready, score_used,
         slots_ready, slots_free, scattered, deg_done, deg_ready, top_ready, own, pown, inbox_zeroed) = map(k.sem, (
             "b_consts", "b_codes_ready", "b_hot_ready", "b_hot_used", "b_agree_ready",
             "b_score_ready", "b_score_used", "b_slots_ready", "b_slots_free", "b_scattered",
             "b_deg_done", "b_deg_ready", "b_top_ready", "b_own", "b_pown", "b_inbox_zeroed"))
        with nc.Block() as block:

            @block.sync
            def _(sp):
                def batch(b, par, t):
                    if not isinstance(t, int) or t:
                        sp.wait_ge(edges_used[par], t)
                    for j, name in enumerate(("src", "dst")):
                        v = k.ins[name].rearrange("(b n) -> b n", n=BE)[2 * t + par, :]
                        sp.dma_start(node[:, par, j, :], v.rearrange("(p k) -> p k", k=BC)).then_inc(edges_in[par], 16)
                        sp.dma_start(raw[j * BITS:(j + 1) * BITS, par, :], row(v, BITS)).then_inc(edges_in[par], 16)
                    if isinstance(b, int) and b == 1:
                        sp.wait_ge(consts, 1)
                        rows = k.inbox[0:EX * ROWS, :].rearrange("(p q r) d -> p q (r d)", p=P, q=8)
                        for q in range(8):
                            sp.dma_start(rows[:, q, :], blank[:, :]).then_inc(inbox_zeroed, 16)

                pairs(sp, BATCHES, batch)
                sp.wait_ge(inbox_zeroed, 16 * 8)

            @block.gpsimd
            def _(pool):
                step = Own(pool, pown)
                pool.iota(shift[:, :], [[0, 1]], base=0, channel_multiplier=1)
                pool.iota(lane[:, :], [[1, P]], base=0, channel_multiplier=0, allow_small_or_imprecise_dtypes=True)
                pool.iota(spare[:, :], [[1, GC]], base=SPARE, channel_multiplier=GC)
                pool.memset(neg[:, :], 1.0 - 2 * BITS)
                pool.memset(zb[:, :], 0.0)
                pool.memset(blank[:, :], 0.0)
                step(pool.memset(identb[:, :], 0.0))
                step(pool.affine_select(out=identb[:, :], in_=identb[:, :], compare_op=ALU.not_equal, fill=1.0,
                                        base=0, pattern=[[-1, CE]], channel_multiplier=1))
                step(pool.memset(earlier[:, :], delta))
                pool.memset(mine[:, :, :], 0.0)
                step(pool.memset(theirs[:, :, :], 0.0))
                step(pool.memset(mine[MARK:KC, :, :], delta))
                step(pool.memset(theirs[MARK:KC, :, :], 1.0))
                step(pool.affine_select(out=earlier[:, :], in_=earlier[:, :], compare_op=ALU.is_gt, fill=0.0, base=0,
                                        pattern=[[-1, CE]], channel_multiplier=1))
                for i in range(2):
                    for v, keep in ((mine, ALU.is_gt), (theirs, ALU.is_equal)):
                        of = v[MARK:KC, i, :].rearrange("r (n j) -> r n j", j=GC)
                        step(pool.affine_select(out=of, in_=of, compare_op=keep, fill=0.0, base=0,
                                                pattern=[[0, BE // GC], [1, GC]], channel_multiplier=-1))
                pool.drain().then_inc(consts, 1)

                def group(n, par, _):
                    pool.wait_ge(slots_ready, n + 1)
                    pool.wait_ge(scattered, 16 * GC * n)
                    pool.sem_inc(slots_free, 1)
                    for j in range(GC):
                        pool.indirect_dma_start(
                            out=k.counts[:, :], out_offset=bass.IndirectOffsetOnAxis(ap=index[:, par, j:j + 1], axis=0),
                            in_=value[:, par, j:j + 1], in_offset=None, compute_op=ALU.add).then_inc(scattered, 16)

                pairs(pool, BATCHES * BG, group)
                pool.wait_ge(scattered, 16 * GC * BATCHES * BG)
                pool.wait_ge(deg_ready, 1)
                pool.partition_all_reduce(alltop[:, :], top[:, :], P, bass.bass_isa.ReduceOp.max).then_inc(top_ready, 1)

            @block.vector
            def _(dve):
                step = Own(dve, own)
                PER = 4 + 4 * BG
                dve.wait_ge(consts, 1)
                step(nc.vector.tensor_scalar(bit[:, 0:1], shift[:, :], float(BITS), float(BITS), ALU.is_ge, ALU.mult))
                step(nc.vector.tensor_tensor(shift[:, :], shift[:, :], bit[:, 0:1], ALU.subtract))
                tt = nc.vector.tensor_tensor
                ts = nc.vector.tensor_scalar

                def prepare(t, par, before):
                    dve.wait_ge(edges_in[par], 64 * t + 64)
                    step(ts(bit[:, :], raw[:, par, :], shift[:, 0:1], 1, ALU.logical_shift_right, ALU.bitwise_and))
                    dve.wait_ge(hot_used, BG * before)
                    ts(mine[0:2 * BITS, par, :], bit[:, :], 2.0, -1.0, ALU.mult, ALU.add).then_inc(codes_ready, 1)
                    ts(theirs[0:2 * BITS, par, :], bit[:, :], 2.0, -1.0, ALU.mult, ALU.add).then_inc(codes_ready, 1)
                    src, dst = node[:, par, 0, :], node[:, par, 1, :]
                    ts(part[:, 0, :], dst, 8, 21, ALU.logical_shift_right, ALU.logical_shift_left)
                    ts(part[:, 1, :], dst, SW - 1, None, ALU.bitwise_and)
                    ts(part[:, 2, :], src, P - 1, 14, ALU.bitwise_and, ALU.logical_shift_left)
                    ts(part[:, 3, :], src, 7, 8, ALU.logical_shift_right, ALU.logical_shift_left)
                    ts(lowi[:, 0, :], src, P - 1, None, ALU.bitwise_and)
                    ts(lowi[:, 1, :], dst, P - 1, None, ALU.bitwise_and)
                    ts(lowi[:, 2, :], src, 7, None, ALU.logical_shift_right)
                    step(ts(lowi[:, 3, :], dst, 7, None, ALU.logical_shift_right))
                    dve.sem_inc(edges_used[par], 1)
                    tt(part[:, 4, :], part[:, 0, :], part[:, 1, :], ALU.bitwise_or)
                    nc.vector.tensor_copy(low[:, par, :, :], lowi[:, :, :])
                    step(tt(part[:, 5, :], part[:, 2, :], part[:, 3, :], ALU.bitwise_or))
                    step(tt(cell[:, par, :], part[:, 4, :], part[:, 5, :], ALU.bitwise_or))

                def groups(b, par):
                    for g in range(BG):
                        n = BG * b + g
                        gp = g % 2
                        js = slice(g * GC, (g + 1) * GC)
                        dve.wait_ge(hot_used, n)
                        tt(hot[:, gp, :, :, :],
                           lane[:, :].rearrange("p (a b l) -> p a b l", a=1, b=1).to_broadcast([CE, 2, GC, P]),
                           low[:, par, 0:2, js].unsqueeze(3).to_broadcast([CE, 2, GC, P]), ALU.is_equal)
                        tt(hoth[:, gp, :, :, :],
                           lane[:, 0:NB].rearrange("p (a b l) -> p a b l", a=1, b=1).to_broadcast([CE, 2, GC, NB]),
                           low[:, par, 2:4, js].unsqueeze(3).to_broadcast([CE, 2, GC, NB]), ALU.is_equal
                           ).then_inc(hot_ready, 1)
                        dve.wait_ge(score_ready, GC * n + GC + 2)
                        dve.wait_ge(slots_free, n)
                        step(nc.vector.tensor_copy(whole[:, :], score[:, gp, :]))
                        step(tt(first[:, :], score[:, gp, :], whole[:, :], ALU.is_equal))
                        nc.vector.tensor_copy(index[:, gp, :], spare[:, :])
                        step(tt(value[:, gp, :], score[:, gp, :], first[:, :], ALU.mult))
                        dve.sem_inc(score_used, 1)
                        step(nc.vector.copy_predicated(index[:, gp, :], first[:, :], cell[:, par, js]))
                        dve.sem_inc(slots_ready, 1)

                prepare(0, 0, 0)
                first_step = step.k

                def both(t, more):
                    step.loop(first_step + 2 * PER * t)
                    prepare(t, 1, 2 * t)
                    groups(2 * t, 0)
                    if more:
                        prepare(t + 1, 0, 2 * t + 1)
                    groups(2 * t + 1, 1)

                both(0, True)
                with dve.Fori(1, BATCHES // 2 - 1) as t:
                    both(t, True)
                both(BATCHES // 2 - 1, False)
                dve.wait_ge(deg_done, 1)
                step(nc.vector.tensor_copy(k.deg[:, :, :], degp[:, 0:2 * NB].rearrange("p (s b) -> p s b", s=2)))
                step(nc.vector.tensor_reduce(top[:, :], k.deg[:, :, :], axis=AX.X, op=ALU.max))
                dve.sem_inc(deg_ready, 1)
                dve.wait_ge(top_ready, 1)
                step(tt(top[0:1, 0:1], alltop[0:1, 0:1], alltop[0:1, 1:2], ALU.min))
                ts(k.many[:, :], top[0:1, 0:1], float(limit), None, ALU.is_gt)

            @block.scalar
            def _(act):
                act.wait_ge(consts, 1)
                act.preload_act_table(ACT.Relu)
                act.sem_inc(score_ready, 2)

                def group(n, par, _):
                    act.wait_ge(score_used, n)
                    for j in range(GC):
                        act.wait_ge(agree_ready, GC * n + j + 1)
                        nc.scalar.activation(junk[:, j % 3, :, :], agree[j % 3][0:CE, :, 0:GE // 2], ACT.Relu,
                                             bias=neg[:, 0:1], accum_out=score[:, par, j:j + 1]
                                             ).then_inc(score_ready, 1)

                pairs(act, BATCHES * BG, group)

            @block.tensor
            def _(pe):
                pe.wait_ge(consts, 1)
                nc.tensor.matmul(degp[:, 0:2 * NB], zb[:, :], zb[:, 0:2 * NB], start=True, stop=False,
                                 skip_group_check=True)

                def batch(b, par, t):
                    pe.wait_ge(codes_ready, 2 * b + 2)
                    by_chunk = [v[:, par, :].rearrange("b (p k) -> b k p", k=BC) for v in (mine, theirs)]
                    for g in range(BG):
                        n = BG * b + g
                        for j in range(GC):
                            pe.wait_ge(score_ready, GC * n + j + (1 if j < 2 else 0))
                            me = by_chunk[0][:, g * GC + j, :]
                            for h in range(2):
                                half = g * GC + h * GC // 2
                                holds = j // (GC // 2) == h
                                o = agree[j % 3][0:CE, h, 0:GE // 2]
                                last = nc.tensor.matmul(o, me, by_chunk[1][:, half:half + GC // 2, :],
                                                        start=True, stop=not holds)
                                if holds:
                                    at = j % (GC // 2) * CE
                                    last = nc.tensor.matmul(o[:, at:at + CE], identb[:, :], earlier[:, :],
                                                            start=False, stop=True)
                            last.then_inc(agree_ready, 1)
                        pe.wait_ge(hot_ready, n + 1)
                        for s in range(2):
                            for j in range(GC):
                                last = nc.tensor.matmul(degp[:, s * NB:(s + 1) * NB], hot[:, g % 2, s, j, :],
                                                        hoth[:, g % 2, s, j, :], start=False, stop=False,
                                                        skip_group_check=True)
                        last.then_inc(hot_used, 1)

                pairs(pe, BATCHES, batch)
                nc.tensor.matmul(degp[:, 0:2 * NB], zb[:, :], zb[:, 0:2 * NB], start=False, stop=True,
                                 skip_group_check=True).then_inc(deg_done, 1)


def stage_scale(k, h, m_parts):
    nc = k.nc
    deg1, root_ready, dinv_ready, hi_ready, own = map(k.sem, ("s_deg1", "s_root", "s_dinv", "s_hi", "s_own"))
    with nc.Block() as block:

        @block.vector
        def _(dve):
            step = Own(dve, own)
            step(nc.vector.tensor_scalar(k.dinv[:, :], k.deg[:, 0, :], 1.0, None, ALU.add))
            dve.sem_inc(deg1, 1)
            dve.wait_ge(root_ready, 1)
            step(nc.vector.reciprocal(k.dinv[:, :], k.dinv[:, :]))
            dve.sem_inc(dinv_ready, 1)
            for i in range(NB):
                dve.wait_ge(hi_ready, i + 1)
                nc.vector.scalar_tensor_tensor(m_parts[:, i, 1, :], h[:, i, :], k.dinv[:, i:i + 1],
                                               m_parts[:, i, 0, :].bitcast(fp32), ALU.mult, ALU.subtract)

        @block.scalar
        def _(act):
            act.preload_act_table(ACT.Sqrt)
            act.wait_ge(deg1, 1)
            nc.scalar.activation(k.dinv[:, :], k.dinv[:, :], ACT.Sqrt).then_inc(root_ready, 1)
            act.wait_ge(dinv_ready, 1)
            for i in range(NB):
                nc.scalar.mul(m_parts[:, i, 0, :], h[:, i, :], k.dinv[:, i:i + 1]).then_inc(hi_ready, 1)


def stage_sum_out(k, m_parts, rows):
    nc = k.nc
    Q = 4
    groups = [list(range(q, min(q + Q, NB))) for q in range(0, NB, Q)]
    NQ = len(groups)
    EVEN, ODD = (NQ + 1) // 2, NQ // 2
    AHEAD = 2
    assert NQ % Q == 1
    place = lambda q: Q if q == NQ - 1 else q % Q

    def before(i, q):
        if q == NQ - 1:
            return i - 1, q
        return (i, q - Q) if q >= Q else (i - 1, q - Q + NQ - 1)

    def number(i, q):
        return NQ * i + q + 1

    with ExitStack() as c:
        turned = [k.sb(c, f"turned{i}", [P, Q, P], fp32r) for i in range(Q + 1)]
        turned_lo = [k.sb(c, f"turned_lo{i}", [P, Q, P], fp32r) for i in range(Q + 1)]
        old = k.sb(c, "c_old", [P, 2, D], fp32)
        new = k.sb(c, "c_new", [P, 2, D], fp32)
        pT = [k.ps(c, f"cT{i}", [P, Q, P]) for i in range(Q + 1)]
        pS = [k.ps(c, f"cS{i}", [P, 2, D]) for i in range(2)]
        rows_in = [k.sem(f"c_rows_in{i}") for i in range(2)]
        old_in = [k.sem(f"c_old_in{i}") for i in range(2)]
        new_out = [k.sem(f"c_new_out{i}") for i in range(2)]
        t_done, act_out, dve_out, lo_out, mm_done, sum_used, new_ready, own = map(k.sem, (
            "c_t_done", "c_act_out", "c_dve_out", "c_lo_out", "c_mm_done", "c_sum_used", "c_new_ready", "c_own"))
        by_block = k.counts[0:COUNTS, :].rearrange("(g p h w) o -> p h g (w o)", g=NSLAB, p=P, h=SH)
        x_rows = k.ins["x"]

        def used(eng, i, q):
            b, last = before(i, q)
            if not isinstance(b, int) or b >= 0:
                eng.wait_ge(mm_done, number(b, last))

        with nc.Block() as block:

            @block.sync
            def _(sp):
                def body(i, par, _):
                    if not isinstance(i, int) or i >= 2:
                        sp.wait_ge(t_done, NQ * (i - 1))
                    sp.dma_start(rows[par][:, :, :], by_block[:, i, :, :]).then_inc(rows_in[par], 16)

                pairs(sp, NB, body)

            @block.gpsimd
            def _(pool):
                def load(i, par):
                    if isinstance(i, int) and i == NB - 1:
                        pool.dma_start(old[0:LAST, par, :], x_rows[i * P:N, :]).then_inc(old_in[par], 16)
                    else:
                        pool.dma_start(old[:, par, :], x_rows[bass.ts(i, P), :]).then_inc(old_in[par], 16)

                load(0, 0)
                load(1, 1)

                def body(i, par, _):
                    pool.wait_ge(new_ready, i + 1)
                    pool.dma_start(k.x1[bass.ts(i, P), :], new[:, par, :]).then_inc(new_out[par], 16)
                    if not (isinstance(i, int) and i >= NB - 2):
                        load(i + 2, par)

                pairs(pool, NB, body)
                pool.wait_ge(new_out[0], 16 * ((NB + 1) // 2))
                pool.wait_ge(new_out[1], 16 * (NB // 2))

            @block.vector
            def _(dve):
                step = Own(dve, own)
                tt = nc.vector.tensor_tensor
                many = dve.value_load(k.many[0:1, 0:1], min_val=0, max_val=1)

                def finish(i, par, t):
                    step.loop(3 * i)
                    dve.wait_ge(mm_done, NQ * i + NQ)
                    if not isinstance(i, int) or i >= 2:
                        dve.wait_ge(new_out[par], 16 * t)
                    n = new[:, par, :]
                    step(tt(n, pS[par][:, 0, :], m_parts[:, i, 0, :].bitcast(fp32), ALU.add))
                    step(tt(n, n, pS[par][:, 1, :], ALU.add))
                    dve.sem_inc(sum_used, 1)
                    step(tt(n, n, m_parts[:, i, 1, :].bitcast(fp32), ALU.add))
                    dve.wait_ge(old_in[par], 16 * t + 16)
                    last = nc.vector.scalar_tensor_tensor(n, n, k.dinv[:, bass.ts(i, 1)], old[:, par, :], ALU.mult, ALU.add)
                    if isinstance(i, int) and i == NB - 1:
                        step(last)
                        last = nc.vector.tensor_scalar(n, n, k.valid[:, i:i + 1], None, ALU.mult)
                    last.then_inc(new_ready, 1)
                    dve.wait_ge(new_ready, i + 1)
                    nc.vector.bn_stats(k.stats[:, i, :], n)

                def rows_body(large):
                    def body(i, par, t):
                        for q in range(NQ):
                            if q == 2 and (not isinstance(i, int) or i):
                                finish(i - 1, 1 - par, t if par else t - 1)
                            m = len(groups[q])
                            hi_part, bank = turned[place(q)][:, 0:m, :], pT[place(q)][:, 0:m, :]
                            if q % 2:
                                dve.wait_ge(t_done, number(i, q))
                                used(dve, i, q)
                                nc.vector.tensor_copy(hi_part, bank).then_inc(dve_out, 1)
                            if large:
                                dve.wait_ge(act_out, EVEN * i + (q + 2) // 2)
                                dve.wait_ge(dve_out, ODD * i + (q + 1) // 2)
                                used(dve, i, q)
                                tt(turned_lo[place(q)][:, 0:m, :], bank, hi_part.bitcast(fp32), ALU.subtract
                                   ).then_inc(lo_out, 1)
                    ring(dve, NB, body, peel=2)

                with dve.If(many < 1):
                    rows_body(False)
                with dve.If(many > 0):
                    rows_body(True)
                finish(NB - 1, (NB - 1) % 2, (NB - 1) // 2)

            @block.scalar
            def _(act):
                def body(i, par, _):
                    for q in range(0, NQ, 2):
                        act.wait_ge(t_done, number(i, q))
                        used(act, i, q)
                        nc.scalar.copy(turned[place(q)][:, 0:len(groups[q]), :],
                                       pT[place(q)][:, 0:len(groups[q]), :]).then_inc(act_out, 1)

                pairs(act, NB, body)

            @block.tensor
            def _(pe):
                many = pe.value_load(k.many[0:1, 0:1], min_val=0, max_val=1)

                def rows_body(large):
                    def copied(i, q):
                        if q % 2:
                            pe.wait_ge(dve_out, ODD * i + (q + 1) // 2)
                        else:
                            pe.wait_ge(act_out, EVEN * i + q // 2 + 1)
                        if large:
                            pe.wait_ge(lo_out, number(i, q))

                    def turn(i, par, q):
                        b, last = before(i, q)
                        if not isinstance(b, int) or b >= 0:
                            copied(b, last)
                        for n, b in enumerate(groups[q]):
                            last = nc.tensor.transpose(pT[place(q)][:, n, :],
                                                       rows[par][:, b // 2, (b % 2) * P:(b % 2 + 1) * P], k.ident[:, :])
                        last.then_inc(t_done, 1)

                    def add(par, tile, q, start, stop):
                        for n, b in enumerate(groups[q]):
                            last = nc.tensor.matmul(pS[par][:, :, :].rearrange("p a d -> p (a d)"), tile[:, n, :],
                                                    m_parts[:, b, :, :].rearrange("p a d -> p (a d)"),
                                                    start=(start and b == 0), stop=(stop and b == NB - 1))
                        return last

                    def body(i, par, t):
                        if isinstance(i, int) and i == 0:
                            pe.wait_ge(rows_in[0], 16)
                            for q in range(AHEAD):
                                turn(i, par, q)
                        if not isinstance(i, int) or i >= 2:
                            pe.wait_ge(sum_used, i - 1)
                        for q in range(NQ):
                            if q + AHEAD < NQ:
                                turn(i, par, q + AHEAD)
                            elif not (isinstance(i, int) and i == NB - 1):
                                if q + AHEAD == NQ:
                                    pe.wait_ge(rows_in[1 - par], 16 * (t + par) + 16)
                                turn(i + 1, 1 - par, q + AHEAD - NQ)
                            copied(i, q)
                            last = add(par, turned[place(q)], q, True, not large)
                            if large:
                                last = add(par, turned_lo[place(q)], q, False, True)
                            last.then_inc(mm_done, 1)
                    pairs(pe, NB, body)

                with pe.If(many < 1):
                    rows_body(False)
                with pe.If(many > 0):
                    rows_body(True)


def stage_slice(k):
    nc = k.nc
    PT = HG // P
    with ExitStack() as c:
        x = k.sb(c, "d_x", [P, NB, D], fp32)
        wT = k.sb(c, "d_wT", [P, NB, PT, P], fp32)
        mv = k.sb(c, "d_mv", [P, 2, NB], fp32)
        sd = k.sb(c, "d_sd", [P, NB], fp32)
        rstd = k.sb(c, "d_rstd", [P, NB], fp32)
        ow = k.sb(c, "d_ow", [P, PT, D], fp32)
        bout = k.sb(c, "d_bout", [P, D], fp32)
        wfx = k.sb(c, "d_wfx", [P, KD, HG], fp32)
        bfx = k.sb(c, "d_bfx", [1, HG], fp32)
        wq, wk, wv = (k.sb(c, f"d_w{n}", [C, C], fp32) for n in "qkv")
        wout = k.sb(c, "d_wout", [C, H, D], fp32)
        sums = k.sb(c, "d_sums", [P, PT, D + 1], fp32)
        var_ready, sd_ready, own, w_in = map(k.sem, ("d_var", "d_sd", "d_own", "d_w_in"))
        NW = 8

        with ExitStack() as c1:
            wxT = k.sb(c1, "d_wxT", [C, H, D], fp32)
            wsl = k.sb(c1, "d_wsl", [C, G], fp32)
            bx = k.sb(c1, "d_bx", [C, H], fp32)
            bsl = k.sb(c1, "d_bsl", [P, G], fp32)
            temp = k.sb(c1, "d_temp", [P, H], fp32)
            wc = k.sb(c1, "d_wc", [P, KD, HG], fp32)
            bc = k.sb(c1, "d_bc", [P, H, G], fp32)
            xa = k.sb(c1, "d_xa", [P, 4, D + 1], fp32)
            xnT = k.sb(c1, "d_xnT", [P, 2, KD, P], fp32)
            lg = k.sb(c1, "d_lg", [P, 2, H, G], fp32)
            bxw = lg[0:C, :, :, :].rearrange("p a h g -> p (a h g)").rearrange("p (h n) -> p h n", n=P)
            ex = k.sb(c1, "d_ex", [P, 2, H, G], fp32)
            sw = k.sb(c1, "d_sw", [P, 2, HG], fp32)
            mx = k.sb(c1, "d_mx", [P, 2, H], fp32)
            es = k.sb(c1, "d_es", [P, 2, H], fp32)
            rs = k.sb(c1, "d_rs", [P, 2, H], fp32)
            pS = [k.ps(c1, f"dS{i}", [P, D + 1]) for i in range(PT)]
            pT = k.ps(c1, "dT", [P, KD, P])
            pL = [k.ps(c1, f"dL{i}", [P, HG]) for i in range(2)]
            pW = k.ps(c1, "dW", [P, PT, P])
            (wc_ready, w_scaled, bxw_ready, xn_ready, t_done, xnT_ready, l_ready, l_shifted, e_ready, sums_done, sw_ready, st_done,
             w_done, w_stored, c_in) = map(k.sem, (
                 "d_wc_ready", "d_w_scaled", "d_bxw_ready", "d_xn_ready", "d_t_done", "d_xnT_ready", "d_l_ready",
                 "d_l_shifted", "d_e_ready", "d_sums_done", "d_sw_ready", "d_st_done", "d_w_done", "d_w_stored", "d_c_in"))
            x_in = [k.sem(f"d_x_in{i}") for i in range(2)]
            with nc.Block() as block:

                @block.sync
                def _(sp):
                    rows = k.x1.rearrange("(b p) d -> p b d", p=P)
                    sp.dma_start(x[:, 0:4, :], rows[:, 0:4, :]).then_inc(x_in[0], 16)
                    ld = lambda o, i: sp.dma_start(o, i).then_inc(c_in, 16)
                    ld(wxT[:, :, :], k.ins["L0_ffn_W_xt"].rearrange("(h c) f -> c h f", c=C))
                    ld(wsl[:, :], k.ins["L0_ffn_W_slice"])
                    ld(bx[:, :], k.ins["L0_ffn_b_xt"])
                    ld(bsl[:, :], row(k.ins["L0_ffn_b_slice"]))
                    ld(temp[:, :], k.ins["L0_ffn_temperature"].rearrange("a h b c -> a (h b c)").to_broadcast([P, H]))
                    sp.dma_start(x[:, 4:NB, :], rows[:, 4:NB, :]).then_inc(x_in[1], 16)
                    sp.wait_ge(c_in, 16 * 5)
                    ld = lambda o, i: sp.dma_start(o, i).then_inc(w_in, 16)
                    ld(wfx[:, :, :], k.ins["L0_ffn_W_fx"].rearrange("(t p) n -> p t n", p=P))
                    ld(bfx[:, :], row(k.ins["L0_ffn_b_fx"], 1))
                    ld(wq[:, :], k.ins["L0_ffn_W_q"])
                    ld(wk[:, :], k.ins["L0_ffn_W_k"])
                    ld(wv[:, :], k.ins["L0_ffn_W_v"])
                    ld(wout[:, :, :], k.ins["L0_ffn_W_out"].rearrange("(h c) n -> c h n", c=C))
                    ld(bout[:, :], row(k.ins["L0_ffn_b_out"]))
                    sp.wait_ge(w_in, 16 * 7)

                @block.vector
                def _(dve):
                    step = Own(dve, own)
                    tt, ts = nc.vector.tensor_tensor, nc.vector.tensor_scalar
                    moments(nc, step, k.stats, mv, sd)
                    dve.sem_inc(var_ready, 1)
                    dve.wait_ge(c_in, 16 * 5)
                    nc.vector.tensor_copy(bxw[:, :, :], bx[:, :].unsqueeze(2).to_broadcast([C, H, P])
                                          ).then_inc(bxw_ready, 1)
                    step(ts(temp[:, :], temp[:, :], 0.1, 5.0, ALU.max, ALU.min))
                    step(nc.vector.reciprocal(temp[:, :], temp[:, :]))
                    dve.wait_ge(wc_ready, 1)
                    rt = temp[:, :].unsqueeze(2).to_broadcast([P, H, G])
                    for t in range(KD):
                        tt(wc[:, t, :].rearrange("p (h g) -> p h g", h=H), pL[t][:, :].rearrange("p (h g) -> p h g", h=H),
                           rt, ALU.mult)
                    step(tt(bc[:, :, :], pW[:, :, :].rearrange("p a b -> p (a b)").rearrange("p (h g) -> p h g", h=H),
                            bsl[:, :].unsqueeze(1).to_broadcast([P, H, G]), ALU.add))
                    step(tt(bc[:, :, :], bc[:, :, :], rt, ALU.mult))
                    dve.sem_inc(w_scaled, 1)
                    dve.wait_ge(sd_ready, 1)
                    step(nc.vector.reciprocal(rstd[:, :], sd[:, :]))

                    def norm(i, w):
                        if not isinstance(i, int) or i >= 4:
                            dve.wait_ge(st_done, i - 3)
                        ts(xa[:, w, 0:D], x[:, i, :], mv[:, 0, bass.ts(i, 1)], rstd[:, bass.ts(i, 1)],
                           ALU.subtract, ALU.mult)
                        nc.vector.tensor_copy(xa[:, w, D:D + 1], k.valid[:, bass.ts(i, 1)]).then_inc(xn_ready, 1)

                    def shift(i, par):
                        dve.wait_ge(l_ready, i + 1)
                        if not isinstance(i, int) or i >= 2:
                            dve.wait_ge(e_ready, i - 1)
                        l = lg[:, par, :, :]
                        step(tt(l, pL[par][:, :].rearrange("p (h g) -> p h g", h=H), bc[:, :, :], ALU.add))
                        step(nc.vector.tensor_reduce(mx[:, par, :], l, axis=AX.X, op=ALU.max))
                        tt(l, l, mx[:, par, :].unsqueeze(2).to_broadcast([P, H, G]), ALU.subtract).then_inc(l_shifted, 1)

                    def total(i, par):
                        dve.wait_ge(e_ready, i + 1)
                        step(nc.vector.tensor_reduce(es[:, par, :], ex[:, par, :, :], axis=AX.X, op=ALU.add))
                        if not isinstance(i, int) or i >= 2:
                            dve.wait_ge(sw_ready, i - 1)
                        nc.vector.reciprocal(rs[:, par, :], es[:, par, :]).then_inc(sums_done, 1)

                    dve.wait_ge(x_in[0], 16)
                    norm(0, 0)
                    norm(1, 1)
                    norm(2, 2)
                    shift(0, 0)
                    dve.wait_ge(x_in[1], 16)
                    before = step.k

                    def body(i, w, _):
                        step.loop(before + 3 * i)
                        if not (isinstance(i, int) and i >= NB - 1):
                            shift(i + 1, (w + 1) % 2)
                        total(i, w % 2)
                        if not (isinstance(i, int) and i >= NB - 3):
                            norm(i + 3, (w + 3) % 4)

                    ring(dve, NB, body, 4)
                    dve.wait_ge(st_done, NB)
                    for j in range(PT):
                        nc.vector.tensor_copy(sums[:, j, :], pS[j][:, :])

                @block.scalar
                def _(act):
                    act.wait_ge(var_ready, 1)
                    nc.scalar.activation(sd[:, :], sd[:, :], ACT.Sqrt, bias=k.eps[:, 0:1]).then_inc(sd_ready, 1)
                    act.preload_act_table(ACT.Exp)

                    def turn(i, par):
                        act.wait_ge(t_done, i + 1)
                        if not isinstance(i, int) or i >= 2:
                            act.wait_ge(l_ready, i - 1)
                        nc.scalar.copy(xnT[:, par, :, :], pT[:, :, :]).then_inc(xnT_ready, 1)

                    def exps(i, par):
                        act.wait_ge(l_shifted, i + 1)
                        if not isinstance(i, int) or i >= 2:
                            act.wait_ge(sw_ready, i - 1)
                        nc.scalar.activation(ex[:, par, :, :], lg[:, par, :, :], ACT.Exp).then_inc(e_ready, 1)

                    def store(i):
                        act.wait_ge(w_done, i + 1)
                        nc.scalar.copy(wT[:, i, :, :], pW[:, :, :]).then_inc(w_stored, 1)

                    turn(0, 0)
                    turn(1, 1)
                    exps(0, 0)
                    turn(2, 0)

                    def body(i, par, _):
                        if not (isinstance(i, int) and i >= NB - 1):
                            exps(i + 1, 1 - par)
                        if not (isinstance(i, int) and i >= NB - 3):
                            turn(i + 3, 1 - par)
                        store(i)

                    pairs(act, NB, body)

                @block.gpsimd
                def _(pool):
                    def body(i, par, _):
                        pool.wait_ge(sums_done, i + 1)
                        if not isinstance(i, int) or i >= 2:
                            pool.wait_ge(w_done, i - 1)
                        nc.gpsimd.tensor_tensor(sw[:, par, :].rearrange("p (h g) -> p h g", h=H), ex[:, par, :, :],
                                                rs[:, par, :].unsqueeze(2).to_broadcast([P, H, G]), ALU.mult
                                                ).then_inc(sw_ready, 1)

                    pairs(pool, NB, body)

                @block.tensor
                def _(pe):
                    pe.wait_ge(bxw_ready, 1)
                    for h in range(H):
                        hs = slice(h * G, (h + 1) * G)
                        for t in range(KD):
                            nc.tensor.matmul(pL[t][:, hs], wxT[:, h, t * P:(t + 1) * P], wsl[:, :], start=True, stop=True)
                        last = nc.tensor.matmul(pW[:, :, :].rearrange("p a b -> p (a b)")[:, hs], bxw[:, h, :], wsl[:, :],
                                                start=True, stop=True)
                    last.then_inc(wc_ready, 1)
                    pe.wait_ge(w_scaled, 1)

                    def turn(i, w):
                        pe.wait_ge(xn_ready, i + 1)
                        if not isinstance(i, int) or i:
                            pe.wait_ge(xnT_ready, i)
                        for t in range(KD):
                            last = nc.tensor.transpose(pT[:, t, :], xa[:, w, t * P:(t + 1) * P], k.ident[:, :])
                        last.then_inc(t_done, 1)

                    def logits(i, par):
                        pe.wait_ge(xnT_ready, i + 1)
                        if not isinstance(i, int) or i >= 2:
                            pe.wait_ge(l_shifted, i - 1)
                        for t in range(KD):
                            last = nc.tensor.matmul(pL[par][:, :], xnT[:, par, t, :], wc[:, t, :],
                                                    start=(t == 0), stop=(t == KD - 1))
                        last.then_inc(l_ready, 1)

                    for i in range(2):
                        turn(i, i)
                        logits(i, i)
                    turn(2, 2)

                    def body(i, w, _):
                        par = w % 2
                        if not (isinstance(i, int) and i >= NB - 2):
                            logits(i + 2, par)
                        pe.wait_ge(sw_ready, i + 1)
                        for j in range(PT):
                            last = nc.tensor.matmul(pS[j][:, :], sw[:, par, j * P:(j + 1) * P], xa[:, w, :],
                                                    start=(isinstance(i, int) and i == 0),
                                                    stop=(isinstance(i, int) and i == NB - 1), skip_group_check=True)
                        last.then_inc(st_done, 1)
                        if not (isinstance(i, int) and i >= NB - 3):
                            turn(i + 3, (w + 3) % 4)
                        if not isinstance(i, int) or i:
                            pe.wait_ge(w_stored, i)
                        for j in range(PT):
                            last = nc.tensor.transpose(pW[:, j, :], sw[:, par, j * P:(j + 1) * P], k.ident[:, :])
                        last.then_inc(w_done, 1)

                    ring(pe, NB, body, 4)

        with ExitStack() as c2:
            tokT = k.sb(c2, "d_tokT", [C, HG], fp32)
            qT = k.sb(c2, "d_qT", [C, HG], fp32)
            kT = k.sb(c2, "d_kT", [C, HG], fp32)
            vv = k.sb(c2, "d_vv", [G, HG], fp32)
            att = k.sb(c2, "d_att", [G, H, G], fp32)
            attT = k.sb(c2, "d_attT", [G, HG], fp32)
            oT = k.sb(c2, "d_oT", [C, HG], fp32)
            sT = k.sb(c2, "d_sT", [P, KD, HG], fp32)
            nT = k.sb(c2, "d_nT", [1, HG], fp32)
            mx = k.sb(c2, "d_amx", [G, H], fp32)
            rn = k.sb(c2, "d_rn", [P, PT], fp32)
            pp = [k.ps(c2, f"dP{i}", [P, 512]) for i in range(8)]
            pe_done, other_done, vown = map(k.sem, ("d_pe_done", "d_other_done", "d_vown"))
            with nc.Block() as block:

                @block.vector
                def _(dve):
                    step = Own(dve, vown)
                    tt, ts = nc.vector.tensor_tensor, nc.vector.tensor_scalar

                    def after_pe(n):
                        dve.wait_ge(pe_done, n)

                    step(ts(rn[:, :], sums[:, :, D], 1e-5, None, ALU.add))
                    step(nc.vector.reciprocal(rn[:, :], rn[:, :]))
                    step(tt(sums[:, :, :], sums[:, :, :], rn[:, :].unsqueeze(2).to_broadcast([P, PT, D + 1]), ALU.mult))
                    dve.sem_inc(other_done, 1)
                    after_pe(1)
                    for t in range(KD):
                        nc.vector.tensor_copy(sT[:, t, :], pp[t][:, :])
                    step(nc.vector.tensor_copy(nT[:, :], pp[2][0:1, :]))
                    dve.sem_inc(other_done, 1)
                    after_pe(2)
                    step(nc.vector.tensor_copy(tokT[:, :], pp[3][0:C, :]))
                    dve.sem_inc(other_done, 1)
                    after_pe(3)
                    nc.vector.tensor_copy(qT[:, :], pp[4][0:C, :])
                    nc.vector.tensor_copy(kT[:, :], pp[5][0:C, :])
                    step(nc.vector.tensor_copy(vv[:, :], pp[6][0:G, :]))
                    dve.sem_inc(other_done, 1)
                    after_pe(4)
                    s3 = pp[7][0:G, :].rearrange("p (h g) -> p h g", h=H)
                    step(nc.vector.tensor_reduce(mx[:, :], s3, axis=AX.X, op=ALU.max))
                    step(tt(att[:, :, :], s3, mx[:, :].unsqueeze(2).to_broadcast([G, H, G]), ALU.subtract))
                    dve.sem_inc(other_done, 1)
                    dve.wait_ge(other_done, 6)
                    step(nc.vector.tensor_reduce(mx[:, :], att[:, :, :], axis=AX.X, op=ALU.add))
                    step(nc.vector.reciprocal(mx[:, :], mx[:, :]))
                    step(tt(att[:, :, :], att[:, :, :], mx[:, :].unsqueeze(2).to_broadcast([G, H, G]), ALU.mult))
                    dve.sem_inc(other_done, 1)
                    after_pe(5)
                    step(nc.vector.tensor_copy(attT[:, :], pp[0][0:G, :]))
                    dve.sem_inc(other_done, 1)
                    after_pe(6)
                    step(nc.vector.tensor_copy(oT[:, :], pp[1][0:C, :]))
                    dve.sem_inc(other_done, 1)
                    after_pe(7)
                    for j in range(PT):
                        nc.vector.tensor_copy(ow[:, j, :], pp[2 + j][:, 0:D])

                @block.scalar
                def _(act):
                    act.wait_ge(other_done, 5)
                    nc.scalar.activation(att[:, :, :], att[:, :, :], ACT.Exp, scale=float(C) ** -0.5).then_inc(other_done, 1)

                @block.tensor
                def _(pe):
                    mm = nc.tensor.matmul
                    hs = [slice(h * C, (h + 1) * C) for h in range(H)]
                    pe.wait_ge(other_done, 1)
                    for j in range(PT):
                        js = slice(j * P, (j + 1) * P)
                        for t in range(KD):
                            nc.tensor.transpose(pp[t][:, js], sums[:, j, t * P:(t + 1) * P], k.ident[:, :])
                        last = nc.tensor.transpose(pp[2][0:1, js], sums[:, j, D:D + 1], k.ident[:, :])
                    last.then_inc(pe_done, 1)
                    pe.wait_ge(other_done, 2)
                    for h in range(H):
                        for t in range(KD):
                            mm(pp[3][0:C, hs[h]], wfx[:, t, hs[h]], sT[:, t, hs[h]], start=(t == 0), stop=False)
                        last = mm(pp[3][0:C, hs[h]], bfx[:, hs[h]], nT[:, hs[h]], start=False, stop=True)
                    last.then_inc(pe_done, 1)
                    pe.wait_ge(other_done, 3)
                    mm(pp[4][0:C, :], wq[:, :], tokT[:, :], start=True, stop=True)
                    mm(pp[5][0:C, :], wk[:, :], tokT[:, :], start=True, stop=True)
                    for h in range(H):
                        last = mm(pp[6][0:G, hs[h]], tokT[:, hs[h]], wv[:, :], start=True, stop=True)
                    last.then_inc(pe_done, 1)
                    pe.wait_ge(other_done, 4)
                    for h in range(H):
                        last = mm(pp[7][0:G, hs[h]], qT[:, hs[h]], kT[:, hs[h]], start=True, stop=True)
                    last.then_inc(pe_done, 1)
                    pe.wait_ge(other_done, 7)
                    for h in range(H):
                        last = nc.tensor.transpose(pp[0][0:G, hs[h]], att[:, h, :], k.ident[0:G, 0:G])
                    last.then_inc(pe_done, 1)
                    pe.wait_ge(other_done, 8)
                    for h in range(H):
                        last = mm(pp[1][0:C, hs[h]], vv[:, hs[h]], attT[:, hs[h]], start=True, stop=True)
                    last.then_inc(pe_done, 1)
                    pe.wait_ge(other_done, 9)
                    for h in range(H):
                        o = (h % 2) * G
                        last = mm(pp[2 + h // 2][o:o + G, 0:D], oT[:, hs[h]], wout[:, h, :], start=True, stop=True)
                    last.then_inc(pe_done, 1)

        with ExitStack() as c3:
            st = k.sb(c3, "d_st", [P, 2, PT, P], fp32)
            tmp = k.sb(c3, "d_tmp", [P, 2, D], fp32)
            pO = [k.ps(c3, f"dO{i}", [P, D]) for i in range(2)]
            st_ready, o_ready, o_used, x_done, x_out = map(k.sem, (
                "d_st_ready", "d_o_ready", "d_o_used", "d_x_done", "d_x_out"))
            with nc.Block() as block:

                @block.scalar
                def _(act):
                    def body(i, par, _):
                        if not isinstance(i, int) or i >= 2:
                            act.wait_ge(o_ready, i - 1)
                        nc.scalar.copy(st[:, par, :, :], wT[:, i, :, :]).then_inc(st_ready, 1)

                    pairs(act, NB, body)

                @block.tensor
                def _(pe):
                    def body(i, par, _):
                        pe.wait_ge(st_ready, i + 1)
                        if not isinstance(i, int) or i >= 2:
                            pe.wait_ge(o_used, i - 1)
                        for j in range(PT):
                            last = nc.tensor.matmul(pO[par][:, :], st[:, par, j, :], ow[:, j, :],
                                                    start=(j == 0), stop=(j == PT - 1))
                        last.then_inc(o_ready, 1)

                    pairs(pe, NB, body)

                @block.vector
                def _(dve):
                    tt = nc.vector.tensor_tensor

                    def body(i, par, _):
                        dve.wait_ge(o_ready, i + 1)
                        if not isinstance(i, int) or i >= 2:
                            dve.wait_ge(x_done, i - 1)
                        tt(tmp[:, par, :], pO[par][:, :], bout[:, :], ALU.add).then_inc(o_used, 1)
                        dve.wait_ge(o_used, i + 1)
                        tt(x[:, i, :], x[:, i, :], tmp[:, par, :], ALU.add).then_inc(x_done, 1)
                        dve.wait_ge(x_done, i + 1)
                        nc.vector.bn_stats(k.stats[:, i, :], x[:, i, :])

                    pairs(dve, NB, body)

                @block.sync
                def _(sp):
                    for q in range(7):
                        bs = slice(q * NB // 7, (q + 1) * NB // 7)
                        sp.wait_ge(x_done, bs.stop)
                        sp.dma_start(k.x2.rearrange("(b p) d -> p b d", p=P)[:, bs, :], x[:, bs, :]).then_inc(x_out, 16)
                    sp.wait_ge(x_out, 16 * 7)


def stage_project(k, n, source, u_parts, rest):
    nc = k.nc
    PB = 7
    assert NB % PB == 0
    parts = NB // PB
    RING = 3
    with ExitStack() as c:
        buf = k.sb(c, f"p{n}_buf", [P, RING, PB, D], fp32)
        res = k.sb(c, f"p{n}_res", [P, RING, PB, D], fp32)
        w = k.sb(c, f"p{n}_w", [P, KD, 2, D], fp32)
        wlin = k.sb(c, f"p{n}_wlin", [P, KD, D], fp32)
        b0 = k.sb(c, f"p{n}_b0", [P, D], fp32)
        b1 = k.sb(c, f"p{n}_b1", [P, D], fp32)
        xT = k.sb(c, f"p{n}_xT", [P, 2, KD, P], fp32)
        mv = k.sb(c, f"p{n}_mv", [P, 2, NB], fp32)
        sd = k.sb(c, f"p{n}_sd", [P, NB], fp32)
        rstd = k.sb(c, f"p{n}_rstd", [P, NB], fp32)
        pT = [k.ps(c, f"p{n}T{i}", [P, KD, P]) for i in range(2)]
        pU = [k.ps(c, f"p{n}U{i}", [P, 2, D]) for i in range(2)]
        loaded = [k.sem(f"p{n}_loaded{i}") for i in range(parts)]
        stored = [k.sem(f"p{n}_stored{i}") for i in range(RING)]
        w_in, w_ready, var_ready, sd_ready, rstd_ready, row_ready, rest_ready, t_done, xT_ready, u_done, hi_ready, u_used, own = (
            k.sem(f"p{n}_{m}") for m in (
                "w_in", "w_ready", "var_ready", "sd_ready", "rstd_ready", "row_ready", "rest_ready", "t_done", "xT_ready",
                "u_done", "hi_ready", "u_used", "own"))
        part = lambda m, q: m.rearrange("(b p) d -> p b d", p=P)[:, q * PB:(q + 1) * PB, :]
        with nc.Block() as block:

            @block.sync
            def _(sp):
                for q in range(parts):
                    if q == 1:
                        for i, name in enumerate(("Wl", "Wr")):
                            sp.dma_start(w[:, :, i, :], k.ins[f"L1_gnn_{name}{n}"].rearrange("(t p) n -> p t n", p=P)
                                         ).then_inc(w_in, 16)
                        sp.dma_start(wlin[:, :, :], k.ins[f"L1_gnn_Wlin{n}"].rearrange("(t p) n -> p t n", p=P)
                                     ).then_inc(w_in, 16)
                        sp.dma_start(b0[:, :], row(k.ins[f"L1_gnn_b{n}"])).then_inc(w_in, 16)
                        sp.dma_start(b1[:, :], row(k.ins[f"L1_gnn_blin{n}"])).then_inc(w_in, 16)
                    if q >= RING:
                        sp.wait_ge(u_used, PB * (q - RING + 1))
                        if n == 2:
                            sp.wait_ge(stored[q % RING], 16 * (q // RING))
                    sp.dma_start(buf[:, q % RING, :, :], part(source, q)).then_inc(loaded[q], 16)
                    if n == 2:
                        sp.dma_start(res[:, q % RING, :, :], part(k.x2, q)).then_inc(loaded[q], 16)

            @block.gpsimd
            def _(pool):
                def prepare(q):
                    at = q % RING
                    if n == 1:
                        pool.wait_ge(rstd_ready, 1)
                        pool.wait_ge(loaded[q], 16 * n)
                        for j in range(PB):
                            i = PB * q + j
                            pool.tensor_scalar(buf[:, at, j, :], buf[:, at, j, :], mv[:, 0, i:i + 1],
                                               rstd[:, i:i + 1], ALU.subtract, ALU.mult).then_inc(row_ready, 1)
                    else:
                        pool.wait_ge(w_ready, 1)
                        pool.wait_ge(loaded[q], 16 * n)
                        pool.tensor_tensor(res[:, at, :, :], res[:, at, :, :],
                                           b0[:, :].unsqueeze(1).to_broadcast([P, PB, D]), ALU.add).then_inc(rest_ready, 1)

                prepare(0)
                for q in range(parts):
                    if q < parts - 1:
                        prepare(q + 1)
                    pool.wait_ge(u_used, PB * (q + 1))
                    pool.dma_start(part(rest, q), res[:, q % RING, :, :]).then_inc(stored[q % RING], 16)
                for i in range(RING):
                    pool.wait_ge(stored[i], 16 * len(range(i, parts, RING)))

            @block.vector
            def _(dve):
                step = Own(dve, own)
                tt, ts = nc.vector.tensor_tensor, nc.vector.tensor_scalar

                if n == 1:
                    moments(nc, step, k.stats, mv, sd)
                    dve.sem_inc(var_ready, 1)
                    dve.wait_ge(sd_ready, 1)
                    step(nc.vector.reciprocal(rstd[:, :], sd[:, :]))
                    dve.sem_inc(rstd_ready, 1)
                dve.wait_ge(w_in, 16 * 5)
                tt(b0[:, :], b0[:, :], b1[:, :], ALU.add)
                step(tt(w[:, :, 1, :], w[:, :, 1, :], wlin[:, :, :], ALU.add))
                dve.sem_inc(w_ready, 1)
                for q in range(parts):
                    if n == 2:
                        dve.wait_ge(rest_ready, q + 1)
                    elif q >= RING:
                        dve.wait_ge(stored[q % RING], 16 * (q // RING))
                    for j in range(PB):
                        i = PB * q + j
                        r = res[:, q % RING, j, :]
                        dve.wait_ge(hi_ready, i + 1)
                        tt(r, r if n == 2 else b0[:, :], pU[i % 2][:, 1, :], ALU.add)
                        tt(u_parts[:, i, 1, :], pU[i % 2][:, 0, :], u_parts[:, i, 0, :].bitcast(fp32), ALU.subtract
                           ).then_inc(u_used, 1)

            @block.scalar
            def _(act):
                if n == 1:
                    act.preload_act_table(ACT.Sqrt)
                    act.wait_ge(var_ready, 1)
                    nc.scalar.activation(sd[:, :], sd[:, :], ACT.Sqrt, bias=k.eps[:, 0:1]).then_inc(sd_ready, 1)

                def turned(i):
                    act.wait_ge(t_done, i + 1)
                    if i >= 2:
                        act.wait_ge(u_done, i - 1)
                    nc.scalar.copy(xT[:, i % 2, :, :], pT[i % 2][:, :, :]).then_inc(xT_ready, 1)

                turned(0)
                for i in range(NB):
                    if i < NB - 1:
                        turned(i + 1)
                    act.wait_ge(u_done, i + 1)
                    nc.scalar.copy(u_parts[:, i, 0, :], pU[i % 2][:, 0, :]).then_inc(hi_ready, 1)

            @block.tensor
            def _(pe):
                def turn(i):
                    if n == 1:
                        pe.wait_ge(row_ready, i + 1)
                    else:
                        pe.wait_ge(loaded[i // PB], 16 * n)
                    if i >= 2:
                        pe.wait_ge(xT_ready, i - 1)
                    for t in range(KD):
                        last = nc.tensor.transpose(pT[i % 2][:, t, :], buf[:, i // PB % RING, i % PB, t * P:(t + 1) * P],
                                                   k.ident[:, :])
                    last.then_inc(t_done, 1)

                turn(0)
                pe.wait_ge(w_ready, 1)
                for i in range(NB):
                    if i < NB - 1:
                        turn(i + 1)
                    pe.wait_ge(xT_ready, i + 1)
                    if i >= 2:
                        pe.wait_ge(u_used, i - 1)
                    for t in range(KD):
                        last = nc.tensor.matmul(pU[i % 2][:, :, :].rearrange("p a d -> p (a d)"), xT[:, i % 2, t, :],
                                                w[:, t, :, :].rearrange("p a d -> p (a d)"),
                                                start=(t == 0), stop=(t == KD - 1))
                    last.then_inc(u_done, 1)


def stage_mean_in(k, n, u_parts, rest, result):
    nc = k.nc
    HALF = [(0, (NB + 1) // 2), ((NB + 1) // 2, NB)]
    SB = SW // P
    with ExitStack() as c:
        piece = [k.sb(c, f"f{n}_piece{i}", [P, HALF[0][1], SW], fp32r) for i in range(2)]
        piece_hi = k.sb(c, f"f{n}_piece_hi", [P, HALF[0][1], SW], fp32r)
        rdeg = k.sb(c, f"f{n}_rdeg", [P, NB], fp32)
        old = k.sb(c, f"f{n}_old", [P, 2, SB, D], fp32)
        mix = k.sb(c, f"f{n}_mix", [P, 2, SB, D], fp32)
        pA = [[k.ps(c, f"f{n}A{i}{j}", [P, 2, D]) for j in range(SB)] for i in range(2)]
        piece_in = [k.sem(f"f{n}_piece_in{i}") for i in range(2)]
        piece_used = [k.sem(f"f{n}_piece_used{i}") for i in range(2)]
        piece_split = [k.sem(f"f{n}_piece_split{i}") for i in range(2)]
        old_in = [k.sem(f"f{n}_old_in{i}") for i in range(2)]
        stored = [k.sem(f"f{n}_stored{i}") for i in range(2)]
        own, sum_used, mixed = (k.sem(f"f{n}_{m}") for m in ("own", "sum_used", "mixed"))
        slab_rows = lambda m, g, blocks: m.rearrange("(b p) d -> p b d", p=P)[:, bass.ds(SB * g, blocks), :]

        def width(g):
            return NB - SB * (NSLAB - 1) if isinstance(g, int) and g == NSLAB - 1 else SB

        with nc.Block() as block:

            @block.sync
            def _(sp):
                def body(g, par, t):
                    for j, (lo_b, hi_b) in enumerate(HALF):
                        if not isinstance(g, int) or g:
                            sp.wait_ge(piece_used[j], g)
                        sp.dma_start(piece[j][:, 0:hi_b - lo_b, :].bitcast(fp32), counts_slab(k, g, lo_b, hi_b)
                                     ).then_inc(piece_in[j], 16)
                    if not isinstance(g, int) or g >= 2:
                        sp.wait_ge(mixed, g - 1)
                    sp.dma_start(old[:, par, 0:width(g), :], slab_rows(rest, g, width(g))).then_inc(old_in[par], 16)

                pairs(sp, NSLAB, body)

            @block.gpsimd
            def _(pool):
                def body(g, par, t):
                    pool.wait_ge(mixed, g + 1)
                    pool.dma_start(slab_rows(result, g, width(g)), mix[:, par, 0:width(g), :]).then_inc(stored[par], 16)

                pairs(pool, NSLAB, body)
                pool.wait_ge(stored[0], 16 * ((NSLAB + 1) // 2))
                pool.wait_ge(stored[1], 16 * (NSLAB // 2))

            @block.vector
            def _(dve):
                step = Own(dve, own)
                tt, ts = nc.vector.tensor_tensor, nc.vector.tensor_scalar
                many = dve.value_load(k.many[0:1, 0:1], min_val=0, max_val=1)
                step(ts(rdeg[:, :], k.deg[:, 1, :], 1.0, None, ALU.max))
                step(nc.vector.reciprocal(rdeg[:, :], rdeg[:, :]))
                first_step = step.k

                def split(g, j):
                    lo_b, hi_b = HALF[j]
                    dve.wait_ge(piece_in[j], 16 * g + 16)
                    if not isinstance(g, int) or g + j:
                        dve.wait_ge(piece_used[1 - j], g + j)
                    p, h = piece[j][:, 0:hi_b - lo_b, :], piece_hi[:, 0:hi_b - lo_b, :]
                    nc.vector.tensor_copy(h, p.bitcast(fp32)).then_inc(piece_split[j], 1)
                    dve.wait_ge(piece_split[j], 2 * g + 1)
                    tt(p, p.bitcast(fp32), h.bitcast(fp32), ALU.subtract).then_inc(piece_split[j], 1)

                def finish(g, par, t):
                    step.loop(first_step + 2 * g)
                    dve.wait_ge(piece_used[1], g + 1)
                    dve.wait_ge(old_in[par], 16 * t + 16)
                    if not isinstance(g, int) or g >= 2:
                        dve.wait_ge(stored[par], 16 * t)
                    for a in range(2):
                        for j in range(width(g)):
                            last = nc.vector.scalar_tensor_tensor(
                                mix[:, par, j, :], pA[par][j][:, a, :], rdeg[:, bass.ds(SB * g + j, 1)],
                                mix[:, par, j, :] if a else old[:, par, j, :], ALU.mult, ALU.add)
                        step(last)
                    dve.sem_inc(sum_used, 1)
                    if n == 1:
                        m = mix[:, par, 0:width(g), :]
                        ts(m, m, 0.0, None, ALU.max).then_inc(mixed, 1)
                    else:
                        dve.sem_inc(mixed, 1)
                        for j in range(width(g)):
                            nc.vector.bn_stats(k.stats[:, bass.ds(SB * g + j, 1), :].rearrange("p b s -> p (b s)"),
                                               mix[:, par, j, :])

                def slabs(large):
                    def body(g, par, t):
                        if large:
                            split(g, 0)
                        if not isinstance(g, int) or g:
                            finish(g - 1, 1 - par, t if par else t - 1)
                        if large:
                            split(g, 1)
                    ring(dve, NSLAB, body, peel=2)

                with dve.If(many < 1):
                    slabs(False)
                with dve.If(many > 0):
                    slabs(True)
                finish(NSLAB - 1, (NSLAB - 1) % 2, (NSLAB - 1) // 2)

            @block.tensor
            def _(pe):
                many = pe.value_load(k.many[0:1, 0:1], min_val=0, max_val=1)

                def slabs(large):
                    def total(tile, g, par, half, start, stop):
                        lo_b, hi_b = HALF[half]
                        for b in range(lo_b, hi_b):
                            for j in range(width(g)):
                                last = nc.tensor.matmul(pA[par][j][:, :, :].rearrange("p a d -> p (a d)"),
                                                        tile[:, b - lo_b, j * P:(j + 1) * P],
                                                        u_parts[:, b, :, :].rearrange("p a d -> p (a d)"),
                                                        start=(start and b == 0), stop=(stop and b == NB - 1))
                        return last

                    def body(g, par, t):
                        if not isinstance(g, int) or g >= 2:
                            pe.wait_ge(sum_used, g - 1)
                        for half in range(2):
                            if large:
                                pe.wait_ge(piece_split[half], 2 * g + 2)
                                total(piece_hi, g, par, half, True, False)
                            pe.wait_ge(piece_in[half], 16 * g + 16)
                            total(piece[half], g, par, half, not large, True).then_inc(piece_used[half], 1)

                    pairs(pe, NSLAB, body)

                with pe.If(many < 1):
                    slabs(False)
                with pe.If(many > 0):
                    slabs(True)


def stage_route(k, x3, tok, where, weight):
    nc = k.nc
    with ExitStack() as c:
        mv = k.sb(c, "g_mv", [P, 2, NB], fp32)
        sd = k.sb(c, "g_sd", [P, NB], fp32)
        rstd = k.sb(c, "g_rstd", [P, NB], fp32)
        tn = k.sb(c, "g_tn", [P, 2, D], fp32)
        tT = k.sb(c, "g_tT", [P, 2, KD, P], fp32)
        gw = k.sb(c, "g_gw", [P, KD, EX], fp32)
        gb = k.sb(c, "g_gb", [P, EX], fp32)
        lg = k.sb(c, "g_lg", [P, NB, EX], fp32)
        hot = k.sb(c, "g_hot", [P, NB, EX], fp32)
        cum = k.sb(c, "g_cum", [P, NB, EX], fp32)
        total = k.sb(c, "g_total", [P, NB, EX], fp32)
        a, b, e, pos, kept = (k.sb(c, f"g_{n}", [P, NB], fp32) for n in ("a", "b", "e", "pos", "kept"))
        rank = k.sb(c, "g_rank", [P, EX], fp32)
        token = k.sb(c, "g_token", [P, NB], fp32)
        upto = k.sb(c, "g_upto", [P, P], fp32)
        ones = k.sb(c, "g_ones", [P, P], fp32)
        pT = [k.ps(c, f"gT{i}", [P, KD, P]) for i in range(2)]
        pG = k.ps(c, "gG", [P, NB, EX])
        pC = [k.ps(c, f"gC{i}", [P, NB * EX]) for i in range(2)]
        (x_in, w_in, var_ready, sd_ready, own, consts, tn_ready, stored, t_done, tT_ready, g_done,
         shifted, e_ready, hot_ready, cum_done, pown) = map(k.sem, (
             "g_x_in", "g_w_in", "g_var", "g_sd_ready", "g_own", "g_consts", "g_tn_ready", "g_stored", "g_t_done",
             "g_tT_ready", "g_g_done", "g_shifted", "g_e_ready", "g_hot_ready", "g_cum_done", "g_pown"))
        with nc.Block() as block:

            @block.sync
            def _(sp):
                sp.dma_start(x3[:, :, :], k.x3.rearrange("(b p) d -> p b d", p=P)).then_inc(x_in, 16)
                sp.dma_start(gw[:, :, :], k.ins["L1_ffn_gate_w"].rearrange("(t p) n -> p t n", p=P)).then_inc(w_in, 16)
                sp.dma_start(gb[:, :], row(k.ins["L1_ffn_gate_b"])).then_inc(w_in, 16)

            @block.gpsimd
            def _(pool):
                step = Own(pool, pown)
                pool.iota(rank[:, :], [[-1, EX]], base=EX, channel_multiplier=0, allow_small_or_imprecise_dtypes=True)
                pool.iota(token[:, :], [[P, NB]], base=0, channel_multiplier=1, allow_small_or_imprecise_dtypes=True)
                pool.memset(ones[:, :], 1.0)
                step(pool.memset(upto[:, :], 1.0))
                step(pool.affine_select(out=upto[:, :], in_=upto[:, :], compare_op=ALU.is_ge, fill=0.0, base=0,
                                        pattern=[[1, P]], channel_multiplier=-1))
                pool.sem_inc(consts, 1)

                def body(i, par, _):
                    pool.wait_ge(tn_ready, i + 1)
                    pool.tensor_copy(tok[:, i, :], tn[:, par, :]).then_inc(stored, 1)

                pairs(pool, NB, body)

            @block.vector
            def _(dve):
                step = Own(dve, own)
                tt, ts = nc.vector.tensor_tensor, nc.vector.tensor_scalar
                moments(nc, step, k.stats, mv, sd)
                dve.sem_inc(var_ready, 1)
                dve.wait_ge(sd_ready, 1)
                step(nc.vector.reciprocal(rstd[:, :], sd[:, :]))
                dve.wait_ge(w_in, 32)
                dve.wait_ge(x_in, 16)

                def norm(i, par, _):
                    if not isinstance(i, int) or i >= 2:
                        dve.wait_ge(t_done, i - 1)
                        dve.wait_ge(stored, i - 1)
                    ts(tn[:, par, :], x3[:, i, :], mv[:, 0, bass.ts(i, 1)], rstd[:, bass.ts(i, 1)],
                       ALU.subtract, ALU.mult).then_inc(tn_ready, 1)

                pairs(dve, NB, norm)
                dve.wait_ge(g_done, NB)
                step(tt(lg[:, :, :], pG[:, :, :], gb[:, :].unsqueeze(1).to_broadcast([P, NB, EX]), ALU.add))
                dve.wait_ge(consts, 1)
                wide = lambda v: v.unsqueeze(2).to_broadcast([P, NB, EX])
                step(nc.vector.tensor_reduce(a[:, :], lg[:, :, :], axis=AX.X, op=ALU.max))
                step(tt(lg[:, :, :], lg[:, :, :], wide(a[:, :]), ALU.subtract))
                dve.sem_inc(shifted, 1)
                dve.wait_ge(e_ready, 1)
                step(nc.vector.tensor_reduce(a[:, :], lg[:, :, :], axis=AX.X, op=ALU.add))
                step(nc.vector.reciprocal(weight[:, :], a[:, :]))
                step(ts(hot[:, :, :], lg[:, :, :], 1.0, None, ALU.is_ge))
                rk = rank[:, :].unsqueeze(1).to_broadcast([P, NB, EX])
                step(tt(hot[:, :, :], hot[:, :, :], rk, ALU.mult))
                step(nc.vector.tensor_reduce(e[:, :], hot[:, :, :], axis=AX.X, op=ALU.max))
                step(tt(hot[:, :, :], rk, wide(e[:, :]), ALU.is_equal))
                step(ts(e[:, :], e[:, :], -1.0, float(EX), ALU.mult, ALU.add))
                step(tt(hot[:, :, :], hot[:, :, :], wide(k.valid[:, :]), ALU.mult))
                dve.sem_inc(hot_ready, 1)
                dve.wait_ge(cum_done, 1)
                flat = lambda v: v[:, :, :].rearrange("p b e -> p (b e)")
                nc.vector.tensor_copy(flat(cum), pC[0][:, :])
                step(nc.vector.tensor_copy(flat(total), pC[1][:, :]))
                step(tt(flat(cum), flat(cum), flat(total), ALU.subtract))
                src, other = total, lg
                reach = 1
                while reach < NB:
                    nc.vector.tensor_copy(other[:, 0:reach, :], src[:, 0:reach, :])
                    step(tt(other[:, reach:NB, :], src[:, reach:NB, :], src[:, 0:NB - reach, :], ALU.add))
                    src, other = other, src
                    reach *= 2
                step(tt(flat(cum), flat(cum), flat(src), ALU.add))
                step(tt(cum[:, :, :], cum[:, :, :], hot[:, :, :], ALU.mult))
                step(nc.vector.tensor_reduce(pos[:, :], cum[:, :, :], axis=AX.X, op=ALU.add))
                step(ts(pos[:, :], pos[:, :], -1.0, None, ALU.add))
                step(ts(kept[:, :], pos[:, :], float(CAP), None, ALU.is_lt))
                tt(weight[:, :], weight[:, :], kept[:, :], ALU.mult)
                step(ts(pos[:, :], pos[:, :], float(CAP - 1), 0.0, ALU.min, ALU.max))
                step(ts(e[:, :], e[:, :], float(ROWS), None, ALU.mult))
                step(tt(pos[:, :], pos[:, :], e[:, :], ALU.add))
                nc.vector.tensor_copy(where[:, 1, :], pos[:, :])
                step(ts(a[:, :], token[:, :], float(EX * ROWS), None, ALU.add))
                step(tt(pos[:, :], pos[:, :], a[:, :], ALU.subtract))
                step(tt(pos[:, :], pos[:, :], kept[:, :], ALU.mult))
                step(tt(pos[:, :], pos[:, :], a[:, :], ALU.add))
                nc.vector.tensor_copy(where[:, 0, :], pos[:, :])

            @block.scalar
            def _(act):
                act.wait_ge(var_ready, 1)
                nc.scalar.activation(sd[:, :], sd[:, :], ACT.Sqrt, bias=k.eps[:, 0:1]).then_inc(sd_ready, 1)

                def body(i, par, _):
                    act.wait_ge(t_done, i + 1)
                    if not isinstance(i, int) or i >= 2:
                        act.wait_ge(g_done, i - 1)
                    nc.scalar.copy(tT[:, par, :, :], pT[par][:, :, :]).then_inc(tT_ready, 1)

                pairs(act, NB, body)
                act.wait_ge(shifted, 1)
                nc.scalar.activation(lg[:, :, :], lg[:, :, :], ACT.Exp).then_inc(e_ready, 1)

            @block.tensor
            def _(pe):
                pe.wait_ge(w_in, 32)

                def turn(i, par):
                    pe.wait_ge(tn_ready, i + 1)
                    if not isinstance(i, int) or i >= 2:
                        pe.wait_ge(tT_ready, i - 1)
                    for t in range(KD):
                        last = nc.tensor.transpose(pT[par][:, t, :], tn[:, par, t * P:(t + 1) * P], k.ident[:, :])
                    last.then_inc(t_done, 1)

                turn(0, 0)

                def body(i, par, _):
                    if not (isinstance(i, int) and i == NB - 1):
                        turn(i + 1, 1 - par)
                    pe.wait_ge(tT_ready, i + 1)
                    for t in range(KD):
                        last = nc.tensor.matmul(pG[:, i, :], tT[:, par, t, :], gw[:, t, :], start=(t == 0),
                                                stop=(t == KD - 1))
                    last.then_inc(g_done, 1)

                pairs(pe, NB, body)
                pe.wait_ge(hot_ready, 1)
                h = hot[:, :, :].rearrange("p b e -> p (b e)")
                nc.tensor.matmul(pC[0][:, :], upto[:, :], h, start=True, stop=True)
                nc.tensor.matmul(pC[1][:, :], ones[:, :], h, start=True, stop=True).then_inc(cum_done, 1)


def stage_send(k, tok, where):
    nc = k.nc
    sent = k.sem("h_sent")
    with nc.Block() as block:

        @block.gpsimd
        def _(pool):
            for b in range(NB):
                n = P if b < NB - 1 else LAST
                pool.indirect_dma_start(out=k.inbox[:, :], out_offset=bass.IndirectOffsetOnAxis(ap=where[0:n, 0, b:b + 1], axis=0),
                                        in_=tok[0:n, b, :], in_offset=None).then_inc(sent, 16)
            pool.wait_ge(sent, 16 * NB)


def stage_experts(k, weight):
    nc = k.nc
    FT = FF // P
    TT = ROWS // P
    TOK = CAP + CAP % 2
    LT = TOK - (TT - 1) * P
    HALF = 2 * -(-TOK // 4)
    SPLIT = [(0, HALF), (HALF, TOK)]
    NH = FT * 2
    SLOTS = 4
    TERMS = ((0, 0), (0, 1), (1, 0))
    with ExitStack() as c:
        raw1 = k.sb(c, "h_raw1", [P, KD, FF], fp32)
        raw2 = k.sb(c, "h_raw2", [P, FT, D], fp32)
        w1 = [k.sb(c, f"h_w1{i}", [P, 2, KD, FF], fp32r) for i in range(2)]
        w2 = [k.sb(c, f"h_w2{i}", [P, 2, FT, D], fp32r) for i in range(2)]
        b1 = [k.sb(c, f"h_b1{i}", [P, FT], fp32) for i in range(2)]
        b2 = k.sb(c, "h_b2", [P, EX, D], fp32)
        rows = k.sb(c, "h_rows", [P, TT, D], fp32)
        rT = k.sb(c, "h_rT", [P, 2, KD, TT, P], fp32r)
        mid = k.sb(c, "h_mid", [P, SLOTS, HALF], fp32)
        hT = k.sb(c, "h_hT", [P, 2, FT, TOK], fp32r)
        y = k.sb(c, "h_y", [P, TT, D], fp32)
        nil = k.sb(c, "h_nil", [P, TT, D], fp32)
        nils = k.sb(c, "h_nils", [P, 3], fp32)
        wnil = k.sb(c, "h_wnil", [P, NB], fp32)
        allnils = k.sb(c, "h_allnils", [P, 1], fp32)
        pT = [k.ps(c, f"hT{i}", [P, KD, P]) for i in range(2)]
        pH = [k.ps(c, f"hH{i}", [P, 512]) for i in range(SLOTS)]
        pY = [k.ps(c, f"hY{i}", [P, D]) for i in range(2)]
        b1_in = [k.sem(f"h_b1_in{i}") for i in range(2)]
        (w_in, b_in, rows_in, whi_ready, w_ready, t_done, rhi_ready, rT_ready, h_done, mid_ready, hi_ready, h_ready,
         y_done, y_ready, y_out, padded, nil_made, nil_ready, nil_reduced, own) = map(k.sem, (
             "h_w_in", "h_b_in", "h_rows_in", "h_whi", "h_w_ready", "h_t_done", "h_rhi", "h_rT_ready", "h_h_done",
             "h_mid_ready", "h_hi_ready", "h_h_ready", "h_y_done", "h_y_ready", "h_y_out", "h_padded",
             "h_nil_made", "h_nil_ready", "h_nil_reduced", "h_own"))

        def after(eng, sem, value):
            if not isinstance(value, int) or value > 0:
                eng.wait_ge(sem, value)

        with nc.Block() as block:

            @block.sync
            def _(sp):
                def body(e, par, _):
                    after(sp, t_done, TT * e)
                    sp.dma_start(rows[:, :, :], k.inbox[0:EX * ROWS, :].rearrange("(e t p) d -> p e t d", e=EX, p=P)[
                        :, e, :, :]).then_inc(rows_in, 16)
                    sp.dma_start(b1[par][:, :], k.ins["L1_ffn_b1t"][:, e, :]).then_inc(b1_in[par], 16)
                    after(sp, w_ready, 2 * e)
                    sp.dma_start(raw1[:, :, :], k.ins["L1_ffn_w1"].rearrange("e (t p) f -> p e t f", p=P)[
                        :, e, :, :]).then_inc(w_in, 16)
                    sp.dma_start(raw2[:, :, :], k.ins["L1_ffn_w2"].rearrange("e (t p) d -> p e t d", p=P)[
                        :, e, :, :]).then_inc(w_in, 16)
                    if isinstance(e, int) and e == 0:
                        sp.dma_start(b2[:, :, :].rearrange("p e d -> p (e d)"),
                                     row(k.ins["L1_ffn_b2"].rearrange("e d -> (e d)"))).then_inc(b_in, 16)

                pairs(sp, EX, body)

            @block.gpsimd
            def _(pool):
                def split(e, par):
                    for j, (raw, w) in enumerate(((raw1, w1), (raw2, w2))):
                        pool.wait_ge(whi_ready, 2 * e + j + 1)
                        pool.tensor_tensor(w[par][:, 1, :, :], raw[:, :, :], w[par][:, 0, :, :].bitcast(fp32),
                                           ALU.subtract).then_inc(w_ready, 1)

                split(0, 0)

                def body(e, par, _):
                    if not (isinstance(e, int) and e == EX - 1):
                        split(e + 1, 1 - par)
                    pool.wait_ge(y_ready, TT * e + TT)
                    pool.dma_start(k.outbox.rearrange("(e t p) d -> p e t d", e=EX, p=P)[:, e, :, :], y[:, :, :]
                                   ).then_inc(y_out, 16)

                pairs(pool, EX, body)
                pool.wait_ge(nil_ready, 1)
                pool.partition_all_reduce(allnils[:, :], nils[:, 2:3], P, bass.bass_isa.ReduceOp.max
                                          ).then_inc(nil_reduced, 1)
                pool.wait_ge(y_out, 16 * EX)

            @block.vector
            def _(dve):
                step = Own(dve, own)
                tt = nc.vector.tensor_tensor
                nc.vector.memset(nil[:, :, :], 0.0).then_inc(nil_made, 1)
                nc.vector.memset(y[:, TT - 1, :], 0.0).then_inc(padded, 1)

                def split_rows(e, first=0):
                    for q in range(TT):
                        dve.wait_ge(t_done, TT * e + q + 1)
                        after(dve, h_done, NH * e)
                        nc.vector.tensor_copy(rT[:, 0, :, q, :], pT[q % 2][:, :, :]).then_inc(rhi_ready, 1)
                        dve.wait_ge(rhi_ready, TT * e + q + 1)
                        tt(rT[:, 1, :, q, :], pT[q % 2][:, :, :], rT[:, 0, :, q, :].bitcast(fp32), ALU.subtract
                           ).then_inc(rT_ready, 1)

                split_rows(0)
                dve.wait_ge(b_in, 16)
                dve.wait_ge(padded, 1)

                def body(e, par, _):
                    for f in range(FT):
                        for j, (lo, hi) in enumerate(SPLIT):
                            n = 2 * f + j
                            dve.wait_ge(hi_ready, NH * e + n + 1)
                            tt(hT[:, 1, f, lo:hi], mid[:, n % SLOTS, 0:hi - lo], hT[:, 0, f, lo:hi].bitcast(fp32),
                               ALU.subtract).then_inc(h_ready, 1)
                    if not (isinstance(e, int) and e == EX - 1):
                        split_rows(e + 1)
                    after(dve, y_out, 16 * e)
                    for q in range(TT):
                        dve.wait_ge(y_done, TT * e + q + 1)
                        m = P if q < TT - 1 else LT
                        tt(y[0:m, q, :], pY[q % 2][0:m, :], b2[0:m, e, :], ALU.add).then_inc(y_ready, 1)
                    dve.wait_ge(y_ready, TT * e + TT)
                    dve.wait_ge(nil_made, e + 1)
                    nc.vector.scalar_tensor_tensor(nil[:, :, :], y[:, :, :], 0.0, nil[:, :, :], ALU.mult, ALU.add
                                                   ).then_inc(nil_made, 1)

                pairs(dve, EX, body)
                dve.wait_ge(nil_made, EX + 1)
                nc.vector.tensor_scalar(wnil[:, :], weight[:, :], 0.0, None, ALU.mult)
                step(nc.vector.tensor_reduce(nils[:, 0:1], nil[:, :, :].rearrange("p t d -> p (t d)"), axis=AX.X, op=ALU.add))
                step(nc.vector.tensor_reduce(nils[:, 1:2], wnil[:, :], axis=AX.X, op=ALU.add))
                step(tt(nils[:, 0:1], nils[:, 0:1], nils[:, 1:2], ALU.add))
                nc.vector.tensor_scalar(nils[:, 2:3], nils[:, 0:1], 0.0, None, ALU.not_equal).then_inc(nil_ready, 1)
                dve.wait_ge(nil_reduced, 1)
                nc.vector.tensor_copy(k.odd[:, :], allnils[0:1, :])

            @block.scalar
            def _(act):
                act.preload_act_table(ACT.Relu)

                def first_parts(e, par):
                    act.wait_ge(w_in, 32 * e + 32)
                    for raw, w in ((raw1, w1), (raw2, w2)):
                        nc.scalar.copy(w[par][:, 0, :, :], raw[:, :, :]).then_inc(whi_ready, 1)

                first_parts(0, 0)

                def body(e, par, t):
                    act.wait_ge(b1_in[par], 16 * t + 16)
                    after(act, y_done, TT * e)

                    def hidden(n):
                        f, (lo, hi) = n // 2, SPLIT[n % 2]
                        act.wait_ge(h_done, NH * e + n + 1)
                        after(act, h_ready, NH * e + n + 1 - SLOTS)
                        nc.scalar.activation(mid[:, n % SLOTS, 0:hi - lo], pH[n % SLOTS][:, 0:hi - lo], ACT.Relu,
                                             bias=b1[par][:, f:f + 1]).then_inc(mid_ready, 1)

                    hidden(0)
                    for n in range(NH):
                        if n < NH - 1:
                            hidden(n + 1)
                        f, (lo, hi) = n // 2, SPLIT[n % 2]
                        act.wait_ge(mid_ready, NH * e + n + 1)
                        nc.scalar.copy(hT[:, 0, f, lo:hi], mid[:, n % SLOTS, 0:hi - lo]).then_inc(hi_ready, 1)
                    if not (isinstance(e, int) and e == EX - 1):
                        first_parts(e + 1, 1 - par)

                pairs(act, EX, body)

            @block.tensor
            def _(pe):
                def turn(e):
                    pe.wait_ge(rows_in, 16 * e + 16)
                    for q in range(TT):
                        after(pe, rT_ready, TT * e + q - 1)
                        for t in range(KD):
                            last = nc.tensor.transpose(pT[q % 2][:, t, :], rows[:, q, t * P:(t + 1) * P], k.ident[:, :])
                        last.then_inc(t_done, 1)

                turn(0)

                def body(e, par, t_):
                    pe.wait_ge(w_ready, 2 * e + 2)
                    pe.wait_ge(rT_ready, TT * e + TT)
                    rv = rT[:, :, :, :, :].rearrange("p a t q n -> p a t (q n)")
                    for f in range(FT):
                        for j, (lo, hi) in enumerate(SPLIT):
                            n = 2 * f + j
                            after(pe, mid_ready, NH * e + n + 1 - SLOTS)
                            for i, (a, b) in enumerate(TERMS):
                                for t in range(KD):
                                    last = nc.tensor.matmul(pH[n % SLOTS][:, 0:hi - lo],
                                                            w1[par][:, a, t, f * P:(f + 1) * P], rv[:, b, t, lo:hi],
                                                            start=(i == 0 and t == 0),
                                                            stop=(i == len(TERMS) - 1 and t == KD - 1))
                            last.then_inc(h_done, 1)
                    if not (isinstance(e, int) and e == EX - 1):
                        turn(e + 1)
                    pe.wait_ge(h_ready, NH * e + NH)
                    for q in range(TT):
                        m = P if q < TT - 1 else LT
                        after(pe, y_ready, TT * e + q - 1)
                        for i, (a, b) in enumerate(TERMS):
                            for f in range(FT):
                                last = nc.tensor.matmul(pY[q % 2][0:m, :], hT[:, a, f, q * P:q * P + m],
                                                        w2[par][:, b, f, :], start=(i == 0 and f == 0),
                                                        stop=(i == len(TERMS) - 1 and f == FT - 1))
                        last.then_inc(y_done, 1)

                pairs(pe, EX, body)


def stage_return(k, where, weight):
    nc = k.nc
    with ExitStack() as c:
        PB = 7
        x3, tok = (k.sb(c, f"i_{m}", [P, NB, D], fp32) for m in ("x3", "tok"))
        rest = k.sb(c, "i_rest", [P, 2, PB, D], fp32)
        odd = k.sb(c, "i_odd", [P, 2, PB, D], i32)
        zero = k.sb(c, "i_zero", [P, PB, D], fp32)
        fetched = [k.sem(f"i_fetched{i}") for i in range(NB // PB)]
        padded, x_in, weighted, own, ready, stored = map(k.sem, ("i_padded", "i_x_in", "i_weighted", "i_own", "i_ready", "i_stored"))
        assert NB % PB == 0
        with nc.Block() as block:

            @block.gpsimd
            def _(pool):
                pool.memset(tok[:, NB - 1, :], 0.0).then_inc(padded, 1)
                for b in range(NB):
                    n = P if b < NB - 1 else LAST
                    if b == NB - 1:
                        pool.wait_ge(padded, 1)
                    pool.indirect_dma_start(out=tok[0:n, b, :], out_offset=None, in_=k.outbox[:, :],
                                            in_offset=bass.IndirectOffsetOnAxis(ap=where[0:n, 1, b:b + 1], axis=0)
                                            ).then_inc(fetched[b // PB], 16)

            @block.vector
            def _(dve):
                step = Own(dve, own)
                tt, ts = nc.vector.tensor_tensor, nc.vector.tensor_scalar
                step(nc.vector.memset(zero[:, :, :], 0.0))
                dve.wait_ge(x_in, 16)
                odd_found = dve.value_load(k.odd[0:1, 0:1], min_val=0, max_val=1)
                with dve.If(odd_found < 1):
                    for q in range(NB // PB):
                        dve.wait_ge(weighted, PB * (q + 1))
                        bs = slice(q * PB, (q + 1) * PB)
                        tt(x3[:, bs, :], x3[:, bs, :], tok[:, bs, :], ALU.add).then_inc(ready, 1)
                with dve.If(odd_found > 0):
                    for q in range(NB // PB):
                        dve.wait_ge(weighted, PB * (q + 1))
                        bs = slice(q * PB, (q + 1) * PB)
                        y = tok[:, bs, :]
                        r, o = rest[:, q % 2, :, :], odd[:, q % 2, :, :]
                        step(ts(o, y, 0.0, 0.0, ALU.mult, ALU.not_equal))
                        step(ts(r, y, 10000.0, -10000.0, ALU.min, ALU.max))
                        step(nc.vector.copy_predicated(y, o, r))
                        step(tt(o, y, y, ALU.not_equal))
                        step(nc.vector.copy_predicated(y, o, zero[:, :, :]))
                        tt(x3[:, bs, :], x3[:, bs, :], y, ALU.add).then_inc(ready, 1)

            @block.scalar
            def _(act):
                for q in range(NB // PB):
                    act.wait_ge(fetched[q], 16 * PB)
                    for b in range(q * PB, (q + 1) * PB):
                        nc.scalar.mul(tok[:, b, :], tok[:, b, :], weight[:, b:b + 1]).then_inc(weighted, 1)

            @block.sync
            def _(sp):
                sp.dma_start(x3[:, :, :], k.x3.rearrange("(b p) d -> p b d", p=P)).then_inc(x_in, 16)
                whole = k.out[0:(NB - 1) * P, :].rearrange("(b p) d -> p b d", p=P)
                for q in range(NB // PB):
                    sp.wait_ge(ready, q + 1)
                    hi = min((q + 1) * PB, NB - 1)
                    sp.dma_start(whole[:, q * PB:hi, :], x3[:, q * PB:hi, :]).then_inc(stored, 16)
                sp.dma_start(k.out[(NB - 1) * P:N, :], x3[0:LAST, NB - 1, :]).then_inc(stored, 16)
                sp.wait_ge(stored, 16 * (NB // PB + 1))


def program(nc, ins, out, limit=EXACT):
    with ExitStack() as ctx:
        k = Core(nc, ctx, ins, out)
        with ExitStack() as c:
            assert 2 * NSLAB >= NB and SW == D
            h = k.sb(c, "rows", [P, 2 * NSLAB, D], fp32)
            rows = [h[:, i * NSLAB:(i + 1) * NSLAB, :] for i in range(2)]
            stage_linear(k, h)
            stage_count(k, limit)
            m_parts = k.sb(c, "m_parts", [P, NB, 2, D], fp32r)
            stage_scale(k, h, m_parts)
            stage_sum_out(k, m_parts, rows)
        k.done()
        stage_slice(k)
        with ExitStack() as c:
            u_parts = k.sb(c, "u_parts", [P, NB, 2, D], fp32r)
            stage_project(k, 1, k.x2, u_parts, k.rest)
            stage_mean_in(k, 1, u_parts, k.rest, k.h1)
            stage_project(k, 2, k.h1, u_parts, k.rest)
            stage_mean_in(k, 2, u_parts, k.rest, k.x3)
        k.done()
        with ExitStack() as c:
            where = k.sb(c, "where", [P, 2, NB], i32)
            weight = k.sb(c, "weight", [P, NB], fp32)
            with ExitStack() as c1:
                x3, tok = (k.sb(c1, n, [P, NB, D], fp32) for n in ("x3_rows", "tok"))
                stage_route(k, x3, tok, where, weight)
                stage_send(k, tok, where)
            stage_experts(k, weight)
            stage_return(k, where, weight)


def kernel(**inputs):
    import numpy as _np
    import concourse.bacc as _bacc
    from concourse import mybir as _mybir
    from concourse.bass_utils import run_bass_kernel_spmd as _run

    arrays = {n: _np.asarray(v) for n, v in inputs.items()}
    arrays["L0_gnn_Wt"] = arrays.pop("L0_gnn_W").T
    arrays["L0_ffn_W_xt"] = arrays.pop("L0_ffn_W_x").T
    arrays["L0_ffn_b_xt"] = arrays.pop("L0_ffn_b_x").reshape(H, C).T
    arrays["L1_ffn_b1t"] = arrays.pop("L1_ffn_b1").reshape(EX, FF // P, P).transpose(2, 0, 1)
    arrays = {n: _np.ascontiguousarray(v) for n, v in arrays.items()}
    nc = _bacc.Bacc("TRN2", target_bir_lowering=False, num_devices=1)
    ins = {n: nc.dram_tensor("in_" + n, a.shape, _mybir.dt.from_np(a.dtype), kind="ExternalInput").ap()
           for n, a in arrays.items()}
    out = nc.dram_tensor("out_x", (N, D), fp32, kind="ExternalOutput").ap()
    program(nc, ins, out)
    r = _run(nc, [{"in_" + n: a for n, a in arrays.items()}], core_ids=[0])
    return r.results[0]["out_x"]
```
